# Optimizing a Trainium2 kernel written in Bass

```python
import numpy as np
import jax
import jax.numpy as jnp

def _softmax(x, axis=-1):
    return jax.nn.softmax(x, axis=axis)

def _gelu(x):
    return jax.nn.gelu(x, approximate=True)

def _silu(x):
    return jax.nn.silu(x)

def _sigmoid(x):
    return jax.nn.sigmoid(x)

def _layernorm(x, axis=-1, eps=1e-05):
    m = jnp.mean(x, axis=axis, keepdims=True)
    v = jnp.var(x, axis=axis, keepdims=True)
    return (x - m) / jnp.sqrt(v + eps)

def _scatter_add(tgt, idx, src, axis=0):
    return tgt.at[idx].add(src)

def _segment_sum(src, seg, n):
    return jax.ops.segment_sum(src, seg, n)
kernel_name = 'mk_prb_d1_jaxref_r2_17cfbd'

def setup_inputs(seed: int=0):
    np.random.seed(seed)
    _w = jnp.asarray

    def _L0_attn_setup():
        import jax, jax.numpy as jnp
        import numpy as np
        B, S, D, H = (4, 2048, 512, 16)
        HD = D // H
        EPS = 1e-06

        def _feature_map(t):
            return jax.nn.elu(t) + 1.0
        key = jax.random.key(seed)
        ks = jax.random.split(key, 5)
        scale = 0.02
        return {'x': jax.random.normal(ks[0], (B, S, D), dtype=jnp.float32), 'wq': jax.random.normal(ks[1], (D, D), dtype=jnp.float32) * scale, 'wk': jax.random.normal(ks[2], (D, D), dtype=jnp.float32) * scale, 'wv': jax.random.normal(ks[3], (D, D), dtype=jnp.float32) * scale, 'wo': jax.random.normal(ks[4], (D, D), dtype=jnp.float32) * scale}
    _L0_attn_in = _L0_attn_setup()

    def _L0_ffn_setup():
        import jax, jax.numpy as jnp
        import numpy as np
        import math
        DIM = 512
        NUM_HEADS = 16
        SHARED_HEADS = 1
        ROUTED_HEADS = 3
        HEAD_DIM = DIM // NUM_HEADS
        B, N = (2, 1024)
        key = jax.random.key(seed)
        ks = jax.random.split(key, 16)
        s = 1.0 / math.sqrt(DIM)
        inp = {'x': jax.random.normal(ks[0], (B, N, DIM), dtype=jnp.float32), 'Wq': jax.random.uniform(ks[1], (DIM, DIM), minval=-s, maxval=s), 'bq': jax.random.uniform(ks[2], (DIM,), minval=-s, maxval=s), 'Wk': jax.random.uniform(ks[3], (DIM, DIM), minval=-s, maxval=s), 'bk': jax.random.uniform(ks[4], (DIM,), minval=-s, maxval=s), 'Wv': jax.random.uniform(ks[5], (DIM, DIM), minval=-s, maxval=s), 'bv': jax.random.uniform(ks[6], (DIM,), minval=-s, maxval=s), 'Wp': jax.random.uniform(ks[7], (DIM, DIM), minval=-s, maxval=s), 'bp': jax.random.uniform(ks[8], (DIM,), minval=-s, maxval=s), 'Wr': jax.random.uniform(ks[9], (NUM_HEADS - SHARED_HEADS, DIM), minval=-s, maxval=s), 'br': jax.random.uniform(ks[10], (NUM_HEADS - SHARED_HEADS,), minval=-s, maxval=s), 'Ws': jax.random.uniform(ks[11], (2, DIM), minval=-s, maxval=s), 'bs': jax.random.uniform(ks[12], (2,), minval=-s, maxval=s), 'temperature': jnp.full((NUM_HEADS, 1, 1), float(np.log(np.expm1(1.0 / 0.24))), dtype=jnp.float32), 'query_embedding': 0.02 * jax.random.normal(ks[13], (NUM_HEADS, 1, HEAD_DIM), dtype=jnp.float32)}
        return inp
    _L0_ffn_in = _L0_ffn_setup()
    _d = {'L0_attn_x': _L0_attn_in['x'], 'L0_attn_wq': _L0_attn_in['wq'], 'L0_attn_wk': _L0_attn_in['wk'], 'L0_attn_wv': _L0_attn_in['wv'], 'L0_attn_wo': _L0_attn_in['wo'], 'L0_ffn_Wq': _L0_ffn_in['Wq'], 'L0_ffn_bq': _L0_ffn_in['bq'], 'L0_ffn_Wk': _L0_ffn_in['Wk'], 'L0_ffn_bk': _L0_ffn_in['bk'], 'L0_ffn_Wv': _L0_ffn_in['Wv'], 'L0_ffn_bv': _L0_ffn_in['bv'], 'L0_ffn_Wp': _L0_ffn_in['Wp'], 'L0_ffn_bp': _L0_ffn_in['bp'], 'L0_ffn_Wr': _L0_ffn_in['Wr'], 'L0_ffn_br': _L0_ffn_in['br'], 'L0_ffn_Ws': _L0_ffn_in['Ws'], 'L0_ffn_bs': _L0_ffn_in['bs'], 'L0_ffn_temperature': _L0_ffn_in['temperature'], 'L0_ffn_query_embedding': _L0_ffn_in['query_embedding']}
    _x0 = _d['L0_attn_x']
    _d['L0_attn_x'] = jax.random.normal(jax.random.fold_in(jax.random.key(seed), 1), (4, 2048, 512), dtype=_x0.dtype)
    del _x0
    return _d

def reference(L0_attn_x, L0_attn_wq, L0_attn_wk, L0_attn_wv, L0_attn_wo, L0_ffn_Wq, L0_ffn_bq, L0_ffn_Wk, L0_ffn_bk, L0_ffn_Wv, L0_ffn_bv, L0_ffn_Wp, L0_ffn_bp, L0_ffn_Wr, L0_ffn_br, L0_ffn_Ws, L0_ffn_bs, L0_ffn_temperature, L0_ffn_query_embedding):

    def _L0_attn_ref(x, wq, wk, wv, wo):
        import jax, jax.numpy as jnp
        import numpy as np
        B, S, D, H = (4, 2048, 512, 16)
        HD = D // H
        EPS = 1e-06

        def _feature_map(t):
            return jax.nn.elu(t) + 1.0
        b, s, d = x.shape
        q = _feature_map((x @ wq).reshape(b, s, H, HD))
        k = _feature_map((x @ wk).reshape(b, s, H, HD))
        v = (x @ wv).reshape(b, s, H, HD)
        qs = jnp.moveaxis(q, 1, 0)
        ks = jnp.moveaxis(k, 1, 0)
        vs = jnp.moveaxis(v, 1, 0)

        def step(carry, qkv):
            S_kv, z = carry
            qt, kt, vt = qkv
            S_kv = S_kv + jnp.einsum('bhd,bhe->bhde', kt, vt)
            z = z + kt
            num = jnp.einsum('bhd,bhde->bhe', qt, S_kv)
            den = jnp.einsum('bhd,bhd->bh', qt, z)[..., None] + EPS
            return ((S_kv, z), num / den)
        init = (jnp.zeros((b, H, HD, HD), x.dtype), jnp.zeros((b, H, HD), x.dtype))
        _, outs = jax.lax.scan(step, init, (qs, ks, vs))
        out = jnp.moveaxis(outs, 0, 1).reshape(b, s, d) @ wo
        return out

    def _L0_ffn_ref(x, Wq, bq, Wk, bk, Wv, bv, Wp, bp, Wr, br, Ws, bs, temperature, query_embedding):
        import jax, jax.numpy as jnp
        import numpy as np
        import math
        DIM = 512
        NUM_HEADS = 16
        SHARED_HEADS = 1
        ROUTED_HEADS = 3
        HEAD_DIM = DIM // NUM_HEADS
        B, N = (2, 1024)
        Bsz, Nn, C = x.shape
        H, hd = (NUM_HEADS, HEAD_DIM)

        def heads(W, b):
            y = x @ W.T + b
            return y.reshape(Bsz, Nn, H, hd).transpose(0, 2, 1, 3)
        q = heads(Wq, bq)
        k = heads(Wk, bk)
        v = heads(Wv, bv)
        q_norm = q / jnp.linalg.norm(q, axis=-1, keepdims=True)
        q_scaled = (q_norm + query_embedding[None]) * jax.nn.softplus(temperature)[None]
        attn = jnp.einsum('bhqd,bhkd->bhqk', q_scaled, k) / math.sqrt(hd)
        attn = jax.nn.softmax(attn, axis=-1)
        h = jnp.einsum('bhqk,bhkd->bhqd', attn, v)
        h = h.transpose(0, 2, 1, 3).reshape(Bsz, Nn, C)
        gates = jax.nn.softmax(h @ Wr.T + br, axis=-1)
        _, idx = jax.lax.top_k(gates, ROUTED_HEADS)
        mask = jax.nn.one_hot(idx, H - SHARED_HEADS, dtype=gates.dtype).sum(axis=-2)
        routed_gates = gates * mask * ROUTED_HEADS
        sw = jax.nn.softmax(h @ Ws.T + bs, axis=-1)
        shared_gates = sw * SHARED_HEADS
        weight_0 = sw * 2.0
        shared_gates = weight_0[..., 0:1] * shared_gates
        routed_gates = weight_0[..., 1:2] * routed_gates
        masked_gates = jnp.concatenate([shared_gates, routed_gates], axis=-1)
        out = h * masked_gates.sum(axis=-1, keepdims=True)
        return out @ Wp.T + bp
    x = L0_attn_x
    xn = _layernorm(x, axis=-1)
    x = x + _L0_attn_ref(xn, L0_attn_wq, L0_attn_wk, L0_attn_wv, L0_attn_wo) + _L0_ffn_ref(xn, L0_ffn_Wq, L0_ffn_bq, L0_ffn_Wk, L0_ffn_bk, L0_ffn_Wv, L0_ffn_bv, L0_ffn_Wp, L0_ffn_bp, L0_ffn_Wr, L0_ffn_br, L0_ffn_Ws, L0_ffn_bs, L0_ffn_temperature, L0_ffn_query_embedding)
    return x

_drawn_inputs = setup_inputs


def setup_inputs(seed=0):
    import zlib

    import numpy as np

    out = dict(_drawn_inputs(seed))
    spreads = {'L0_ffn_temperature': (4.151041507720947, 0.6)}
    factors = {'L0_attn_wq': 8.0,
     'L0_attn_wk': 8.0,
     'L0_attn_wv': 4.403,
     'L0_attn_wo': 4.321,
     'L0_ffn_Wq': 4.839,
     'L0_ffn_bq': 8.0,
     'L0_ffn_Wk': 4.842,
     'L0_ffn_bk': 64.0,
     'L0_ffn_Wv': 3.42,
     'L0_ffn_Wr': 8.0,
     'L0_ffn_br': 42.08,
     'L0_ffn_Ws': 8.0,
     'L0_ffn_bs': 28.156,
     'L0_ffn_query_embedding': 8.0,
     'L0_ffn_bp': 3.586}
    for name, (base, spread) in spreads.items():
        noise = np.random.default_rng([zlib.crc32(name.encode()), seed]).standard_normal(out[name].shape)
        drawn = base * np.exp(spread * noise) if base else spread * noise
        out[name] = jnp.asarray(drawn.astype(out[name].dtype))
    for name, factor in factors.items():
        out[name] = (out[name] * factor).astype(out[name].dtype)
    return out
```

```python
from contextlib import ExitStack

import concourse.bass as bass
from concourse import mybir

F32 = mybir.dt.float32
F32R = mybir.dt.float32r
I32 = mybir.dt.int32
ALU = mybir.AluOpType
ACT = mybir.ActivationFunctionType
AX = mybir.AxisListType

P = 128
B, S, D, H, HD = 4, 2048, 512, 16, 32
HG = P // HD
NG = H // HG
KC = D // P
TT = S // P
CH = 2
NCH = TT // CH
CT = CH * P
LC = 4
NLC = TT // LC
QN = 512
NQ = S // QN
FT = 4
NF = TT // FT
W6 = 6 * P
NR, NS = 15, 2
NGATE = NR + NS + 1
TOP = 3
DVE_SUMS = TT - 1 + TT // 2
POOL_SUMS = TT // 2
DEN_PARTS = 4
VW = HD + 1
LN_EPS, ATT_EPS = 1e-5, 1e-6
SHIFT = 65.0
BOUND2 = (2 * SHIFT) ** 2


def f32(ap):
    return ap.bitcast(F32)


def build(nc, x_d, w6_d, wop_d, wg_d, bqkv_d, bp_d, bg_d, temp_d, qe_d, out_d):
    o1_d = nc.dram_tensor("o1_scratch", [B, S, D], F32, kind="Internal").ap()
    hT_d = nc.dram_tensor("hT_scratch", [B, D, S], F32, kind="Internal").ap()

    with ExitStack() as ctx:
        def sem(name):
            return ctx.enter_context(nc.semaphore(name))

        counted = []

        def counter(name, ahead=0):
            counted.append((sem(name), 1 + ahead))
            return counted[-1][0]

        KB = 1024
        cursor = [17 * KB]

        def at(name, shape, dt, off):
            return nc.alloc_sbuf_tensor_at(name, shape, dt, offset=off)

        def sb(name, shape, dt):
            n = 4
            for d in shape[1:]:
                n *= d
            off = cursor[0]
            cursor[0] += (n + 31) // 32 * 32
            return at(name, shape, dt, off)

        xT = sb("xT", [P, KC, S], F32)
        kaug = sb("kaug", [P, HG, S], F32R)
        qaug = sb("qaug", [P, HG, S], F32R)
        w_hi = sb("w_hi", [P, KC, W6], F32R)
        w_lo = sb("w_lo", [P, KC, W6], F32R)
        v = sb("v", [P, TT, P], F32)
        state = sb("state", [P, LC + 1, HG, VW], F32)
        ident = sb("ident", [P, P], F32)
        causal = sb("causal", [P, P], F32)
        headmask = sb("headmask", [P, HG], F32)
        ones32 = sb("ones32", [P, HD], F32)
        minus_half = sb("minus_half", [P, CH, HG], F32)
        neg_shift = sb("neg_shift", [P, 1], F32)
        bias_g = sb("bias_g", [P, 3 * P], F32)
        kmean_b = sb("kmean_b", [P, P], F32)
        bp = sb("bp", [P, D], F32)
        bg = sb("bg", [P, NR + NS], F32)
        et = sb("et", [P, H, HD], F32)
        et_g = sb("et_g", [P, P], F32)
        temp = sb("temp", [P, H], F32)
        tnt = sb("tnt", [P, H], F32)
        tsc = sb("tsc", [P, H], F32)
        tsc_g = sb("tsc_g", [P, HG], F32)
        tb = sb("tb", [P, H], F32)
        tb_g = sb("tb_g", [P, HG], F32)
        xpart = sb("xpart", [P, KC, TT // LC], F32)
        xmean = sb("xmean", [P, KC], F32)
        xbar = sb("xbar", [P, KC, P], F32R)
        stats = sb("stats", [P, LC, 6], F32)
        mv = sb("mv", [P, LC, 2], F32)
        rstd = sb("rstd", [P, LC], F32)
        ss = sb("ss", [P, CH, HG], F32)
        rn = sb("rn", [P, CH, HG], F32)
        rnt = sb("rnt", [P, CH, HG], F32)
        kss = sb("kss", [P, CH, HG], F32)
        kmax = sb("kmax", [P, CH, HG], F32)
        kmax2 = sb("kmax2", [P, HG], F32)
        bound = sb("bound", [P, 1], F32)
        bound1 = sb("bound1", [1, 1], F32)
        flag = sb("flag", [1, 1], I32)
        rowmax = sb("rowmax", [P, 1], F32)
        dn = sb("dn", [P, 2, HG], F32)
        rdn = sb("rdn", [P, 2, HG], F32)
        wg_raw = sb("wg_raw", [P, KC, NGATE], F32)
        wg_hi = sb("wg_hi", [P, KC, NGATE], F32R)
        wg_lo = sb("wg_lo", [P, KC, NGATE], F32R)
        NZ = NR + NS + TOP
        rden = sb("rden", [P, QN], F32)
        lgT = rden[0:NGATE, :]
        lg = sb("lg", [P, FT, NR + NS], F32)
        top8 = sb("top8", [P, FT, 8], F32)
        smax = sb("smax", [P, FT, 1], F32)
        z = sb("z", [P, FT, NZ], F32)
        zsum = sb("zsum", [P, FT, 3], F32)
        zrec = sb("zrec", [P, FT, 2], F32)
        share = sb("share", [P, FT, 4], F32)
        gain = sb("gain", [P, FT], F32)
        r1 = cursor[0]
        xs_hi = [at(f"xs_hi{s}", [P, KC, CT], F32R, r1 + s * 4 * KB) for s in range(2)]
        xs_lo = [at(f"xs_lo{s}", [P, KC, CT], F32R, r1 + (8 + s * 4) * KB) for s in range(2)]
        q_cat = at("q_cat", [P, CH, HG, P], F32R, r1 + 16 * KB)
        k_cat = at("k_cat", [P, CH, HG, P], F32R, r1 + 20 * KB)
        qk = at("qk", [P, 2, CH, P], F32, r1 + 24 * KB)
        sq = at("sq", [P, CH, P], F32, r1 + 26 * KB)
        ksq = at("ksq", [P, CH, P], F32, r1 + 27 * KB)
        qh = at("qh", [P, CH, P], F32, r1 + 28 * KB)
        ex = at("ex", [P, LC, 2 * P], F32, r1)
        phi = at("phi", [P, LC, 2 * P], F32, r1 + 4 * KB)
        qkT = at("qkT", [P, LC, 2, P], F32, r1 + 8 * KB)
        v1 = at("v1", [P, LC, HG, VW], F32, r1 + 12 * KB)
        o1 = at("o1", [P, LC, P], F32, r1 + 12 * KB + 2112)
        kvm = at("kvm", [P, LC, HG, VW], F32, r1)
        c2 = r1 + 12 * KB + 2112 + 2048
        qbd = at("qbd", [P, LC, HG, P], F32, c2)
        am = at("am", [P, LC, HG, P], F32, c2 + 8 * KB)
        hT_out = [at(f"hT_out{s}", [P, QN], F32, c2 + (16 + 2 * s) * KB) for s in range(2)]
        r1_end = c2 + 20 * KB
        w_raw = at("w_raw", [P, KC, W6], F32, r1)
        hT_in = at("hT_in", [P, KC, FT * P], F32, r1)
        x_in = [at(f"x_in{s}", [P, LC, D], F32, r1 + (12 + s * 8) * KB) for s in range(2)]
        o1_in = at("o1_in", [P, FT, D], F32, r1 + 28 * KB)
        scan_q = at("scan_q", [P, P], F32R, r1)
        scan_m = at("scan_m", [P, P], F32, r1 + KB)
        r2 = (r1_end + 31) // 32 * 32
        lin = at("lin", [P, TT, 3 * P], F32, r2)
        prob = [[at(f"prob{t}{p}", [P, 2, QN], F32, r2 + (t * 2 + p) * 4 * KB) for p in range(2)] for t in range(2)]
        acc = [[at(f"acc{s}{p}", [P, 2, QN], F32, (r2 + 16 * KB, r1 + 12 * KB)[s] + p * 4 * KB) for p in range(2)]
               for s in range(2)]
        acc_pool = [at(f"acc_pool{s}", [P, 2, QN], F32, r1 + (28 - 8 * s) * KB) for s in range(2)]
        hT_hi1 = at("hT_hi1", [P, KC, FT * P], F32R, r2)
        hT_lo1 = at("hT_lo1", [P, KC, FT * P], F32R, r2 + 8 * KB)
        y = [at("y0", [P, FT, D], F32, r2 + 16 * KB), v[:].rearrange("p t (a n) -> p t a n", a=1).rearrange(
            "p (j r) a n -> p j (r a n)", j=FT)]
        assert r2 + 24 * KB <= nc.sbuf_usable_end, (r2 + 24 * KB, nc.sbuf_usable_end)
        wop_raw = xT[:, 0:2, :].rearrange("p a (k n) -> p a k n", k=KC)
        wop_hi = kaug[:, 0:2, :].rearrange("p a (k n) -> p a k n", k=KC)
        wop_lo = kaug[:, 2:4, :].rearrange("p a (k n) -> p a k n", k=KC)
        hT_hi = [qaug[:, 0, :].rearrange("p (k n) -> p k n", k=KC), hT_hi1[:]]
        hT_lo = [qaug[:, 1, :].rearrange("p (k n) -> p k n", k=KC), hT_lo1[:]]
        oT_hi = qaug[:, 2, :].rearrange("p (k n) -> p k n", k=KC)
        oT_lo = qaug[:, 3, :].rearrange("p (k n) -> p k n", k=KC)

        low = ctx.enter_context(nc.psum_tensor("low", [P, 4, 512], F32))
        high = ctx.enter_context(nc.psum_tensor("high", [P, 4, 512], F32))
        flat = [t[:, i, :] for t in (low, high) for i in range(4)]
        places = [low[:, 0:2, :], low[:, 2:4, :], high[:, 0:2, :]]
        out_bank, den_bank = flat[6], flat[7]

        const_in = sem("const_in")
        settled = sem("settled")
        pool_const = sem("pool_const")
        dve_const = counter("dve_const")
        act_const = sem("act_const")
        x_loaded = [counter(f"x_loaded{s}") for s in range(2)]
        ln_stats, ln_rstd, ln_dve, ln_done = counter("ln_stats"), counter("ln_rstd"), counter("ln_dve"), counter("ln_done")
        ln_pool = counter("ln_pool")
        xT_turned, xT_kept = counter("xT_turned", LC), counter("xT_kept")
        xpart_done, xbar_ready = counter("xpart_done"), counter("xbar_ready")
        w_loaded, w_split, w_hi_done = counter("w_loaded"), counter("w_split"), counter("w_hi_done")
        xs_hi_done, xs_done = counter("xs_hi_done"), counter("xs_done")
        proj_done, projA_kept, projB_kept = counter("proj_done"), counter("projA_kept"), counter("projB_kept")
        qk_kept = counter("qk_kept")
        ss_ready, rn_ready, qh_ready = counter("ss_ready"), counter("rn_ready"), counter("qh_ready")
        cat_hi, k_cat_done, q_cat_done = counter("cat_hi"), counter("k_cat_done"), counter("q_cat_done")
        k_turned, q_turned, k_kept, q_kept = counter("k_turned"), counter("q_turned"), counter("k_kept"), counter("q_kept")
        g_dve, g_set = counter("g_dve"), counter("g_set")
        kmean_done, bias_ready = counter("kmean_done"), counter("bias_ready")
        bound_ready, bound_turned, flag_ready = counter("bound_ready"), counter("bound_turned"), counter("flag_ready")
        scan_staged, scan_scored, scan_max, scan_turned, scan_row = (
            counter("scan_staged"), counter("scan_scored"), counter("scan_max"), counter("scan_turned"), counter("scan_row"))
        bound_dve, scan_reduced = counter("bound_dve"), counter("scan_reduced")
        neg_part, exp_part, phi_ready, v1_ready = counter("neg_part"), counter("exp_part"), counter("phi_ready"), counter("v1_ready")
        phi_turned, qkT_kept, kv_done, qbd_ready = counter("phi_turned"), counter("qkT_kept"), counter("kv_done"), counter("qbd_ready")
        at_done, am_ready, state_ready, num_done = counter("at_done"), counter("am_ready"), counter("state_ready"), counter("num_done")
        c_dve, c_set, o1_ready, o1_stored = counter("c_dve"), counter("c_set"), counter("o1_ready"), counter("o1_stored")
        scored, exped, weighted = counter("scored"), counter("exped"), counter("weighted")
        summed, pool_summed = counter("summed"), counter("pool_summed")
        out_kept, den_done, rden_done, h_done = counter("out_kept"), counter("den_done"), counter("rden_done"), counter("h_done")
        hT_stored = [counter(f"hT_stored{s}") for s in range(2)]
        wop_loaded, wop_hi_done, wop_done = counter("wop_loaded"), counter("wop_hi_done"), counter("wop_done")
        hT_loaded, o1_loaded, xr_loaded = counter("hT_loaded"), counter("o1_loaded"), counter("xr_loaded")
        hT_hi_done, hT_done = counter("hT_hi_done"), counter("hT_done")
        o1_turned, oT_hi_done, oT_done = counter("o1_turned"), counter("oT_hi_done"), counter("oT_done")
        gateT_done, gateT_kept = counter("gateT_done"), counter("gateT_kept")
        gate_done, gate_z, gate_exp, gain_ready = counter("gate_done"), counter("gate_z"), counter("gate_exp"), counter("gain_ready")
        f_dve, yz_done, y_done = counter("f_dve"), counter("yz_done", FT), counter("y_done")
        y_biased = counter("y_biased")
        y_stored = [counter(f"y_stored{s}") for s in range(2)]

        NCONST = 5
        POOL_CONST = 8
        DVE_CONST = 16
        L_STEPS, SET_STEPS, G_STEPS, BOUND_STEPS, C_STEPS, F_STEPS = 2, 5, 6, 3, 10, 13

        dve_order = [(kt, p) for kt in range(1, TT) for p in range(2) if p == 0 or kt % 2]
        DVE_AT = {kp: i + 1 for i, kp in enumerate(dve_order)} | {(0, 0): 1}
        assert len(dve_order) == DVE_SUMS and POOL_SUMS == 2 * KC

        UNITS = 2 * TT

        def place(u, s):
            return (u + s * (UNITS % 3)) % 3

        def unit_before(n, u, s):
            if u >= 3:
                return n * UNITS + (u - 3) + 1
            return n * UNITS - UNITS + max(w for w in range(UNITS) if place(w, 1 - s) == place(u, s)) + 1

        def settle(eng):
            eng.sem_inc(settled, 1)

        block = ctx.enter_context(nc.Block())

        @block.sync
        def _(sp):
            sp.dma_start(w_raw[:], w6_d[0]).then_inc(w_loaded, 16)
            sp.dma_start(bias_g[:], bqkv_d[0].partition_broadcast(P)).then_inc(w_loaded, 16)
            for dst, src in (
                (bp[:], bp_d.partition_broadcast(P)),
                (bg[:], bg_d.partition_broadcast(P)),
                (temp[:], temp_d.partition_broadcast(P)),
                (et[:].rearrange("p h e -> p (h e)"), qe_d.partition_broadcast(P)),
                (wg_raw[:, :, 0:NR + NS], wg_d),
            ):
                sp.dma_start(dst, src).then_inc(const_in, 16)

            for started, n in counted:
                sp.sem_inc(started, n)

            def load_x(lb, batch, t, s):
                sp.wait_ge(xT_turned, (lb * NF + t - 1) * LC + LC + 1)
                sp.dma_start(x_in[s][:], x_d[batch, bass.ds(t * (LC * P), LC * P), :].rearrange(
                    "o (t p) d -> p (o t) d", p=P)).then_inc(x_loaded[s], 16)

            with sp.Fori(0, NF // 2) as i:
                for s in range(2):
                    load_x(0, slice(0, 1), i * 2 + s, s)

            with sp.Fori(0, B) as b:
                with sp.Fori(0, NG) as g:
                    ig = b * NG + g
                    with sp.Fori(0, NLC) as c:
                        m = ig * NLC + c
                        sp.wait_ge(o1_ready, m * 2 + 2 + 1)
                        sp.dma_start(
                            o1_d[bass.ds(b, 1), bass.ds(c * (LC * P), LC * P), bass.ds(g * P, P)].rearrange(
                                "o (t p) d -> p (o t) d", p=P), o1[:]).then_inc(o1_stored, 16)
                    sp.wait_ge(num_done, ig * TT + TT + 1)
                    sp.wait_ge(o1_stored, (ig + 1) * (16 * NLC) + 1)
                    sp.wait_ge(scored, ig * (NQ * UNITS) + 1 + 1)
                    sp.dma_start(w_raw[:], w6_d[bass.ds((g + 1) % NG, 1)].rearrange("o p k n -> p (o k) n")).then_inc(
                        w_loaded, 16)
                    sp.dma_start(bias_g[:], bqkv_d[bass.ds((g + 1) % NG, 1), :].rearrange(
                        "o n -> (o n)").partition_broadcast(P)).then_inc(w_loaded, 16)
                    def store_h(i, s):
                        sp.wait_ge(h_done, ig * NQ + i * 2 + (s + 1) + 1)
                        sp.dma_start(hT_d[bass.ds(b, 1), bass.ds(g * P, P), bass.ds(i * (2 * QN) + s * QN, QN)].rearrange(
                            "o p n -> (o p) n"), hT_out[s][:]).then_inc(hT_stored[s], 16)

                    with sp.Fori(0, NQ // 2 - 1) as i:
                        store_h(i, 0)
                        store_h(i, 1)
                    store_h(NQ // 2 - 1, 0)

                sp.dma_start(wop_raw, wop_d).then_inc(wop_loaded, 16)
                def load(f, s, half):
                    n = b * NF + f
                    sp.wait_ge(hT_done, n + 1)
                    settle(sp)
                    sp.dma_start(hT_in[:], hT_d[bass.ds(b, 1), :, bass.ds(f * (FT * P), FT * P)].rearrange(
                        "o (k p) n -> p (o k) n", p=P)).then_inc(hT_loaded, 16)
                    sp.wait_ge(o1_turned, n * FT + 1)
                    sp.wait_ge(hT_stored[1], (b + 1) * (16 * NG * NQ // 2) + 1)
                    sp.dma_start(o1_in[:], o1_d[bass.ds(b, 1), bass.ds(f * (FT * P), FT * P), :].rearrange(
                        "o (t p) d -> p (o t) d", p=P)).then_inc(o1_loaded, 16)
                    load_x(b + 1, bass.ds((b + 1) % B, 1), f, s)
                    sp.wait_ge(y_stored[s], (b * (NF // 2) + half) * 16 + 1)
                    sp.dma_start(y[s][:], x_d[bass.ds(b, 1), bass.ds(f * (FT * P), FT * P), :].rearrange(
                        "o (t p) d -> p (o t) d", p=P)).then_inc(xr_loaded, 16)

                def store(f, s):
                    sp.wait_ge(y_done, (b * NF + f) * FT + FT + 1)
                    sp.dma_start(out_d[bass.ds(b, 1), bass.ds(f * (FT * P), FT * P), :].rearrange(
                        "o (t p) d -> p (o t) d", p=P), y[s][:]).then_inc(y_stored[s], 16)

                sp.wait_ge(w_split, (b + 1) * NG + 1 + 1)
                sp.wait_ge(hT_stored[0], (b + 1) * (16 * NG * NQ // 2) + 1)
                settle(sp)
                load(0, 0, 0)
                with sp.Fori(0, NF // 2 - 1) as i:
                    load(i * 2 + 1, 1, i)
                    store(i * 2, 0)
                    load(i * 2 + 2, 0, i + 1)
                    store(i * 2 + 1, 1)
                load(NF - 1, 1, NF // 2 - 1)
                store(NF - 2, 0)
                store(NF - 1, 1)
            for s in range(2):
                sp.wait_ge(y_stored[s], 16 * B * NF // 2 + 1)
                sp.wait_ge(x_loaded[s], 16 * (B + 1) * NF // 2 + 1)
                sp.wait_ge(hT_stored[s], 16 * B * NG * NQ // 2 + 1)
            sp.wait_ge(o1_stored, 16 * B * NG * NLC + 1)
            sp.wait_ge(w_loaded, 32 * (B * NG + 1) + 1)

        @block.gpsimd
        def _(pool):
            g = nc.gpsimd
            g.memset(ident[:], 0.0).then_inc(pool_const, 1)
            g.memset(causal[:], 1.0).then_inc(pool_const, 1)
            g.memset(headmask[:], 1.0).then_inc(pool_const, 1)
            g.memset(minus_half[:], -0.5).then_inc(pool_const, 1)
            pool.wait_ge(pool_const, 4)
            g.affine_select(out=ident[:], in_=ident[:], compare_op=ALU.not_equal, fill=1.0, base=0,
                            pattern=[[-1, P]], channel_multiplier=1).then_inc(pool_const, 1)
            g.affine_select(out=causal[:], in_=causal[:], compare_op=ALU.is_ge, fill=0.0, base=0,
                            pattern=[[1, P]], channel_multiplier=-1).then_inc(pool_const, 1)
            g.affine_select(out=headmask[:], in_=headmask[:], compare_op=ALU.is_ge, fill=0.0, base=0,
                            pattern=[[-HD, HG]], channel_multiplier=1).then_inc(pool_const, 1)
            pool.wait_ge(pool_const, 7)
            g.affine_select(out=headmask[:], in_=headmask[:], compare_op=ALU.is_ge, fill=0.0, base=HD - 1,
                            pattern=[[HD, HG]], channel_multiplier=-1).then_inc(pool_const, 1)

            HW6 = W6 // 2

            def round_weights(n, i):
                if i == 0:
                    pool.wait_ge(w_loaded, n * 32 + 32 + 1)
                    settle(pool)
                r = slice(i % 2 * HW6, (i % 2 + 1) * HW6)
                g.tensor_copy(w_hi[:, i // 2, r], w_raw[:, i // 2, r]).then_inc(w_hi_done, 1)

            def rest_of_weights(n, i):
                r = slice(i % 2 * HW6, (i % 2 + 1) * HW6)
                pool.wait_ge(w_hi_done, (n + 1) * (2 * KC) + 1)
                ins = g.tensor_tensor(w_lo[:, i // 2, r], w_raw[:, i // 2, r], f32(w_hi[:, i // 2, r]), ALU.subtract)
                if i == 2 * KC - 1:
                    ins.then_inc(w_split, 1)

            def rstd_of(lb, t):
                pool.wait_ge(ln_stats, lb * NF + t + 1 + 1)
                g.tensor_tensor(rstd[:], rstd[:], minus_half[:].rearrange("p a b -> p (a b)")[:, 0:LC],
                                ALU.pow).then_inc(ln_rstd, 1)

            for i in range(2 * KC):
                round_weights(0, i)
            for i in range(2 * KC):
                rest_of_weights(0, i)
            with pool.Fori(0, NF) as t:
                rstd_of(0, t)
            with pool.Fori(0, B) as b:
                with pool.Fori(0, NG) as gr:
                    ig = b * NG + gr
                    with pool.Fori(0, NCH) as c:
                        n = ig * NCH + c
                        pool.wait_ge(ss_ready, n + 1 + 1)
                        g.tensor_tensor(rn[:], ss[:], minus_half[:], ALU.pow).then_inc(rn_ready, 1)

                    def scale(q, s):
                        pool.wait_ge(rden_done, (ig * NQ + q) * DEN_PARTS + DEN_PARTS + 1)
                        g.tensor_tensor(hT_out[s][:], hT_out[s][:], rden[:], ALU.mult).then_inc(h_done, 1)

                    def sums(q, s, first=False, split=None):
                        n = ig * NQ + q
                        if not first:
                            pool.wait_ge(den_done, n)
                        for m in range(POOL_SUMS):
                            pool.wait_ge(exped, n * UNITS + (4 * m + 2) + 1)
                            if m == 0:
                                settle(pool)
                                g.tensor_copy(acc_pool[s][:], prob[0][1][:]).then_inc(pool_summed, 1)
                            else:
                                pool.wait_ge(pool_summed, n * POOL_SUMS + m + 1)
                                g.tensor_tensor(acc_pool[s][:], acc_pool[s][:], prob[0][1][:], ALU.add
                                                ).then_inc(pool_summed, 1)
                            if split and m >= 3:
                                for piece in range((m - 3) * 8 // 5, (m - 2) * 8 // 5):
                                    split(ig + 1, piece)
                            if m == 4 and not first:
                                scale(q - 1, 1 - s)

                    sums(0, 0, first=True, split=round_weights)
                    with pool.Fori(0, NQ // 2 - 1) as i:
                        sums(i * 2 + 1, 1)
                        sums(i * 2 + 2, 0)
                    sums(NQ - 1, 1, split=rest_of_weights)
                    scale(NQ - 1, 1)

                pool.wait_ge(h_done, (b + 1) * (NG * NQ) + 1)
                settle(pool)
                with pool.Fori(0, NF // 2) as i:
                    for s in range(2):
                        f = i * 2 + s
                        n = b * NF + f
                        pool.wait_ge(hT_loaded, n * 16 + 16 + 1)
                        pool.wait_ge(yz_done, (n - 1) * FT + FT + 1)
                        settle(pool)
                        g.tensor_copy(hT_hi[s], hT_in[:]).then_inc(hT_hi_done, 1)
                        pool.wait_ge(hT_hi_done, n + 1 + 1)
                        g.tensor_tensor(hT_lo[s], hT_in[:], f32(hT_hi[s]), ALU.subtract).then_inc(hT_done, 1)
                        pool.wait_ge(xr_loaded, n * 16 + 16 + 1)
                        g.tensor_tensor(y[s][:], y[s][:], bp[:].unsqueeze(1).broadcast_to([P, FT, D]), ALU.add
                                        ).then_inc(y_biased, 1)
                        rstd_of(b + 1, f)

        @block.scalar
        def _(act):
            s_ = nc.scalar
            act.wait_ge(dve_const, 2 + 1)
            s_.activation(tnt[:], tnt[:], ACT.Exp).then_inc(act_const, 1)
            act.wait_ge(dve_const, 3 + 1)
            s_.activation(tnt[:], tnt[:], ACT.Ln).then_inc(act_const, 1)
            act.wait_ge(dve_const, DVE_CONST + 1)

            def keep_x(lb, t, j):
                n = (lb * NF + t) * LC + j
                act.wait_ge(xT_turned, n + 1 + LC + 1)
                settle(act)
                s_.activation(xT[:, :, bass.ds(t * (LC * P) + j * P, P)], flat[3].rearrange("p (k n) -> p k n", k=KC),
                              ACT.Copy).then_inc(xT_kept, 1)

            with act.Fori(0, NF) as t:
                for j in range(LC):
                    keep_x(0, t, j)

            with act.Fori(0, B) as b:
                with act.Fori(0, NG) as g:
                    ig = b * NG + g

                    def part_x(c, s):
                        s_.activation(xs_hi[s][:], xT[:, :, bass.ds(c * CT, CT)], ACT.Copy).then_inc(xs_hi_done, 1)

                    def keep_q(c):
                        n = ig * NCH + c
                        for j in range(CH):
                            act.wait_ge(q_turned, n * CH + (j + 1) + 1)
                            settle(act)
                            s_.activation(qaug[:, :, bass.ds(c * CT + j * P, P)],
                                          flat[4 + j].rearrange("p (h n) -> p h n", h=HG),
                                          ACT.Copy).then_inc(q_kept, 1)

                    def chunk(c, s, first, last):
                        n = ig * NCH + c
                        if not last:
                            act.wait_ge(proj_done, n * CH + 1)
                            settle(act)
                            part_x(c + 1, 1 - s)
                        for j in range(CH):
                            act.wait_ge(proj_done, n * CH + (j + 1) + 1)
                            settle(act)
                            s_.activation(lin[:, bass.ds(c * CH + j, 1), :].rearrange("p o n -> p (o n)"),
                                          flat[2 * j + 1][:, 0:3 * P], ACT.Copy).then_inc(projB_kept, 1)
                        if not first:
                            keep_q(c - 1)
                        act.wait_ge(qk_kept, n + 1 + 1)
                        act.wait_ge(k_turned, n * CH + 1)
                        s_.activation(k_cat[:, :, :, 0:2 * HD].rearrange("p c h (r e) -> p (c h) r e", r=2),
                                      qk[:, 1].rearrange("p c (h e) -> p (c h) e", h=HG).unsqueeze(2)
                                      .broadcast_to([P, CH * HG, 2, HD]), ACT.Copy).then_inc(cat_hi, 1)
                        act.wait_ge(qh_ready, n + 1 + 1)
                        act.wait_ge(q_turned, n * CH + 1)
                        s_.activation(q_cat[:, :, :, 0:4 * HD].rearrange("p c h (r e) -> p (c h) r e", r=4)[:, :, 0:3:2],
                                      qh[:].rearrange("p c (h e) -> p (c h) e", h=HG).unsqueeze(2)
                                      .broadcast_to([P, CH * HG, 2, HD]), ACT.Copy).then_inc(cat_hi, 1)

                    act.wait_ge(h_done, ig * NQ + 1)
                    act.wait_ge(w_split, ig + 1 + 1)
                    act.wait_ge(xbar_ready, b + 1 + 1)
                    act.wait_ge(y_stored[0], b * (16 * NF // 2) + 1)
                    part_x(0, 0)
                    chunk(0, 0, True, False)
                    chunk(1, 1, False, False)
                    with act.Fori(1, NCH // 2 - 1) as i:
                        chunk(i * 2, 0, False, False)
                        chunk(i * 2 + 1, 1, False, False)
                    chunk(NCH - 2, 0, False, False)
                    chunk(NCH - 1, 1, False, True)
                    keep_q(NCH - 1)

                    with act.Fori(0, NLC) as c:
                        m = ig * NLC + c
                        act.wait_ge(neg_part, m + 1 + 1)
                        s_.activation(ex[:], ex[:], ACT.Exp).then_inc(exp_part, 1)
                        act.wait_ge(num_done, m * LC + 1)
                        settle(act)
                        s_.activation(v1[:, :, :, 0:HD], lin[:, bass.ds(c * LC, LC), 2 * P:3 * P].rearrange(
                            "p t (h e) -> p t h e", h=HG), ACT.Copy).then_inc(v1_ready, 1)
                        for u in range(2):
                            act.wait_ge(phi_turned, m * 2 + (u + 1) + 1)
                            s_.activation(qkT[:, 2 * u:2 * u + 2].rearrange("p t a n -> p (t a n)"), flat[u],
                                          ACT.Copy).then_inc(qkT_kept, 1)

                    act.wait_ge(flag_ready, ig + 1 + 1)
                    settle(act)
                    wide = act.value_load(flag[0:1, 0:1], min_val=0, max_val=1)
                    with act.If(wide):
                        act.wait_ge(o1_stored, (ig + 1) * (16 * NLC) + 1)
                        with act.Fori(0, HG * TT) as r:
                            act.wait_ge(scan_scored, ig * (HG * TT) + r + 1)
                            settle(act)
                            s_.activation(scan_q[:], f32(qaug[:].rearrange("p h n -> p (h n)")[:, bass.ds(r * P, P)]),
                                          ACT.Copy).then_inc(scan_staged, 1)
                    with act.Else():
                        act.sem_inc(scan_staged, HG * TT)

                    act.wait_ge(o1_ready, (ig + 1) * (2 * NLC) + 1)
                    def exps(q, s, first=False):
                        n = ig * NQ + q
                        for kt in range(TT):
                            for p in range(2):
                                act.wait_ge(scored, n * UNITS + (2 * kt + p + 1) + 1)
                                back, n0 = (kt - 2, n) if kt >= 2 else (kt - 2 + TT, n - 1)
                                if kt >= 2 or not first:
                                    if p == 0:
                                        act.wait_ge(weighted, n0 * TT + (back + 1) + 1)
                                    if p == 1 and kt % 2 == 0:
                                        act.wait_ge(pool_summed, n0 * POOL_SUMS + (back // 2 + 1) + 1)
                                    else:
                                        act.wait_ge(summed, n0 * DVE_SUMS + DVE_AT[back, p] + 1)
                                s_.activation(prob[kt % 2][p][:], places[place(2 * kt + p, s)], ACT.Exp,
                                              bias=neg_shift[:, 0:1]).then_inc(exped, 1)

                    exps(0, 0, first=True)
                    with act.Fori(0, NQ // 2 - 1) as i:
                        exps(i * 2 + 1, 1)
                        exps(i * 2 + 2, 0)
                    exps(NQ - 1, 1)
                    act.wait_ge(h_done, (ig + 1) * NQ + 1)
                    act.dma_start(hT_d[bass.ds(b, 1), bass.ds(g * P, P), S - QN:S].rearrange("o p n -> (o p) n"),
                                  hT_out[(NQ - 1) % 2][:]).then_inc(hT_stored[(NQ - 1) % 2], 16)

                act.wait_ge(wop_loaded, b * 16 + 16 + 1)
                for a in range(2):
                    s_.activation(wop_hi[:, a], wop_raw[:, a], ACT.Copy).then_inc(wop_hi_done, 1)
                with act.Fori(0, NF) as f:
                    n = b * NF + f

                    def keep_o(j):
                        act.wait_ge(o1_turned, n * FT + (j + 1) + 1)
                        act.wait_ge(yz_done, (n - 1) * FT + (j + 1) + FT + 1)
                        s_.activation(oT_hi[:, :, j * P:(j + 1) * P], flat[j % 2].rearrange("p (k n) -> p k n", k=KC),
                                      ACT.Copy).then_inc(oT_hi_done, 1)

                    keep_o(0)
                    keep_o(1)
                    act.wait_ge(gateT_done, n + 1 + 1)
                    s_.activation(lgT, flat[2][0:NGATE, :], ACT.Copy).then_inc(gateT_kept, 1)
                    keep_x(b + 1, f, 0)
                    keep_o(2)
                    act.wait_ge(gate_z, n + 1 + 1)
                    s_.activation(z[:], z[:], ACT.Exp).then_inc(gate_exp, 1)
                    keep_x(b + 1, f, 1)
                    keep_o(3)
                    keep_x(b + 1, f, 2)
                    keep_x(b + 1, f, 3)

        @block.tensor
        def _(pe):
            t_ = nc.tensor
            pe.wait_ge(pool_const, POOL_CONST)
            pe.wait_ge(dve_const, DVE_CONST + 1)

            def parts(out, hi, lo, whi, wlo, open_group=True):
                for k in range(KC):
                    t_.matmul(out, hi(k), whi(k), start=(k == 0 and open_group), stop=False)
                    t_.matmul(out, hi(k), wlo(k), start=False, stop=False)
                    last = t_.matmul(out, lo(k), whi(k), start=False, stop=(k == KC - 1))
                return last

            def turn_x(lb, t, s, j):
                n = (lb * NF + t) * LC + j
                if j == 0:
                    pe.wait_ge(ln_done, lb * NF + t + 1 + 1)
                pe.wait_ge(xT_kept, n + 1)
                for k in range(KC):
                    last = t_.transpose(flat[3][:, k * P:(k + 1) * P], x_in[s][:, j, k * P:(k + 1) * P], ident[:])
                last.then_inc(xT_turned, 1)

            with pe.Fori(0, NF // 2) as i:
                for s in range(2):
                    for j in range(LC):
                        turn_x(0, i * 2 + s, s, j)

            with pe.Fori(0, B) as b:
                with pe.Fori(0, NG) as g:
                    ig = b * NG + g

                    pe.wait_ge(w_split, ig + 1 + 1)
                    pe.wait_ge(xbar_ready, b + 1 + 1)
                    pe.wait_ge(h_done, ig * NQ + 1)
                    pe.wait_ge(xT_kept, (b + 1) * TT + 1)
                    pe.wait_ge(y_done, b * TT + 1)
                    for k in range(KC):
                        last = t_.matmul(flat[6][:, 0:P], xbar[:, k, :], w_hi[:, k, P:2 * P],
                                         start=(k == 0), stop=(k == KC - 1))
                    last.then_inc(kmean_done, 1)

                    def project(c, s):
                        n = ig * NCH + c
                        pe.wait_ge(xs_done, n + 1 + 1)
                        for j in range(CH):
                            pe.wait_ge(projA_kept, n * CH + 1)
                            pe.wait_ge(projB_kept, n * CH + 1)
                            for k in range(KC):
                                hi, lo = (x[:, k, j * P:(j + 1) * P] for x in (xs_hi[s], xs_lo[s]))
                                for x, w in ((hi, w_hi), (hi, w_lo), (lo, w_hi)):
                                    for a in range(2):
                                        last = t_.matmul(flat[2 * j + a][:, 0:3 * P], x,
                                                         w[:, k, a * 3 * P:(a + 1) * 3 * P],
                                                         start=(k == 0 and x is hi and w is w_hi),
                                                         stop=(k == KC - 1 and x is lo))
                            last.then_inc(proj_done, 1)

                    def turn(c, first):
                        n = ig * NCH + c
                        for what, cat, done, kept, turned, b0 in (
                            ("k", k_cat, k_cat_done, k_kept, k_turned, 6), ("q", q_cat, q_cat_done, q_kept, q_turned, 4)):
                            pe.wait_ge(done, n + 1 + 1)
                            if first and what == "k":
                                pe.wait_ge(bias_ready, ig + 1 + 1)
                            pe.wait_ge(kept, n * CH + 1)
                            for j in range(CH):
                                for h in range(HG):
                                    last = t_.transpose(flat[b0 + j][:, h * P:(h + 1) * P], f32(cat[:, j, h, :]), ident[:])
                                last.then_inc(turned, 1)

                    project(0, 0)
                    project(1, 1)
                    turn(0, True)
                    with pe.Fori(1, NCH // 2) as i:
                        project(i * 2, 0)
                        turn(i * 2 - 1, False)
                        project(i * 2 + 1, 1)
                        turn(i * 2, False)
                    turn(NCH - 1, False)

                    pe.wait_ge(bound_ready, ig + 1 + 1)
                    pe.wait_ge(projA_kept, (ig + 1) * TT + 1)
                    t_.transpose(flat[2][0:1, 0:P], bound[:], ident[:]).then_inc(bound_turned, 1)

                    pe.wait_ge(projB_kept, (ig + 1) * TT + 1)
                    pe.wait_ge(q_kept, (ig + 1) * TT + 1)
                    pe.wait_ge(k_kept, (ig + 1) * TT + 1)
                    pe.wait_ge(flag_ready, ig + 1 + 1)
                    settle(pe)
                    with pe.Fori(0, NLC) as c:
                        m = ig * NLC + c
                        pe.wait_ge(phi_ready, m + 1 + 1)
                        pe.wait_ge(qkT_kept, m * 2 + 1)
                        for t in range(LC):
                            for a in range(2):
                                last = t_.transpose(flat[t // 2][:, (t % 2) * 2 * P + a * P:(t % 2) * 2 * P + (a + 1) * P],
                                                    phi[:, t, a * P:(a + 1) * P], ident[:])
                            if t % 2:
                                last.then_inc(phi_turned, 1)
                        pe.wait_ge(v1_ready, m + 1 + 1)
                        pe.wait_ge(o1_ready, m * 2 + 1)
                        for t in range(LC):
                            t_.matmul(flat[6 + t // 3][:, (t % 3) * HG * VW:(t % 3 + 1) * HG * VW], phi[:, t, P:2 * P],
                                      v1[:, t].rearrange("p h e -> p (h e)"), start=True, stop=True).then_inc(kv_done, 1)
                        for t in range(LC):
                            pe.wait_ge(qbd_ready, m * LC + (t + 1) + 1)
                            pe.wait_ge(am_ready, m * LC + 1)
                            t_.matmul(flat[2 + t], qkT[:, t, 1, :], qbd[:, t].rearrange("p h n -> p (h n)"),
                                      start=True, stop=True).then_inc(at_done, 1)
                        pe.wait_ge(state_ready, m + 1 + 1)
                        for t in range(LC):
                            o = (t % 2) * HG * VW
                            t_.matmul(flat[6 + t // 2][:, o:o + HG * VW], qkT[:, t, 0, :],
                                      state[:, t].rearrange("p h e -> p (h e)"), start=True, stop=True)
                            pe.wait_ge(am_ready, m * LC + (t + 1) + 1)
                            for h in range(HG):
                                last = t_.matmul(flat[6 + t // 2][:, o + h * VW:o + (h + 1) * VW], am[:, t, h, :],
                                                 v1[:, t, h, :], start=False, stop=True, skip_group_check=True)
                            last.then_inc(num_done, 1)

                    wide = pe.value_load(flag[0:1, 0:1], min_val=0, max_val=1)
                    pe.wait_ge(o1_ready, (ig + 1) * (2 * NLC) + 1)
                    pe.wait_ge(am_ready, (ig + 1) * TT + 1)
                    with pe.If(wide):
                        with pe.Fori(0, HG) as h:
                            with pe.Fori(0, TT) as r:
                                n = ig * (HG * TT) + h * TT + r
                                pe.wait_ge(scan_staged, n + 1 + 1)
                                pe.wait_ge(scan_row, n + 1)
                                for k in range(4):
                                    last = t_.matmul(flat[k], scan_q[:], kaug[:].rearrange("p h n -> p (h n)")[
                                        :, bass.ds(h * S + k * 512, 512)], start=True, stop=True)
                                last.then_inc(scan_scored, 1)
                                pe.wait_ge(scan_max, n + 1 + 1)
                                t_.transpose(flat[4][:, 0:P], scan_m[:], ident[:]).then_inc(scan_turned, 1)
                    with pe.Else():
                        pe.sem_inc(scan_scored, HG * TT)
                        pe.sem_inc(scan_turned, HG * TT)

                    pe.wait_ge(scan_row, (ig + 1) * (HG * TT) + 1)
                    settle(pe)
                    def score(q, s, u, first=False):
                        kt, p = u // 2, u % 2
                        if u >= 3 or not first:
                            pe.wait_ge(exped, unit_before(ig * NQ + q, u, s) + 1)
                        for a in range(2):
                            h = 2 * p + a
                            last = t_.matmul(places[place(u, s)][:, a, :], kaug[:, h, kt * P:(kt + 1) * P],
                                             qaug[:, h, bass.ds(q * QN, QN)], start=True, stop=True)
                        last.then_inc(scored, 1)

                    def weigh(q, kt):
                        pe.wait_ge(exped, (ig * NQ + q) * UNITS + (2 * kt + 2) + 1)
                        for h in range(HG):
                            last = t_.matmul(out_bank[h * HD:(h + 1) * HD, :], v[:, kt, h * HD:(h + 1) * HD],
                                             prob[kt % 2][h // 2][:, h % 2, :], start=(kt == 0), stop=(kt == TT - 1))
                        last.then_inc(weighted, 1)

                    def total(q, s):
                        n = ig * NQ + q
                        pe.wait_ge(summed, (n + 1) * DVE_SUMS + 1)
                        pe.wait_ge(pool_summed, (n + 1) * POOL_SUMS + 1)
                        pe.wait_ge(rden_done, n * DEN_PARTS + 1)
                        for i in range(2):
                            for h in range(i * 2, HG):
                                last = t_.matmul(den_bank[h * HD:(h + 1) * HD, :], ones32[:],
                                                 (acc_pool[s] if i else acc[s][h // 2])[:, h % 2, :],
                                                 start=(i == 0), stop=(i == 1 or h < 2))
                        last.then_inc(den_done, 1)

                    def attend(q, s, first=False, last=False):
                        for kt in range(TT):
                            for u in (2 * kt + 2, 2 * kt + 3):
                                if u < UNITS:
                                    score(q, s, u, first)
                                elif not last:
                                    score(q + 1, 1 - s, u - UNITS)
                            if kt == 0 and not first:
                                total(q - 1, 1 - s)
                                pe.wait_ge(out_kept, ig * NQ + q + 1)
                            weigh(q, kt)

                    for u in range(2):
                        score(0, 0, u, first=True)
                    attend(0, 0, first=True)
                    with pe.Fori(0, NQ // 2 - 1) as i:
                        attend(i * 2 + 1, 1)
                        attend(i * 2 + 2, 0)
                    attend(NQ - 1, 1, last=True)
                    total(NQ - 1, 1)

                pe.wait_ge(h_done, (b + 1) * (NG * NQ) + 1)
                settle(pe)
                with pe.Fori(0, NF // 2) as i:
                    for s in range(2):
                        f = i * 2 + s
                        n = b * NF + f

                        def turn_o(j):
                            if j == 0:
                                pe.wait_ge(o1_loaded, n * 16 + 16 + 1)
                            pe.wait_ge(oT_done, n * FT + max(j - 1, 0) + 1)
                            for k in range(KC):
                                last = t_.transpose(flat[j % 2][:, k * P:(k + 1) * P], o1_in[:, j, k * P:(k + 1) * P], ident[:])
                            last.then_inc(o1_turned, 1)

                        def out_o(j):
                            r = slice(j * P, (j + 1) * P)
                            pe.wait_ge(oT_done, n * FT + (j + 1) + 1)
                            pe.wait_ge(y_done, n * FT + max(j - 1, 0) + 1)
                            parts(flat[4 + j % 2], lambda k: oT_hi[:, k, r], lambda k: oT_lo[:, k, r],
                                  lambda k: wop_hi[:, 0, k, :], lambda k: wop_lo[:, 0, k, :])

                        def out_h(j):
                            r = slice(j * P, (j + 1) * P)
                            parts(flat[6 + j % 2], lambda k: hT_hi[s][:, k, r], lambda k: hT_lo[s][:, k, r],
                                  lambda k: wop_hi[:, 1, k, :], lambda k: wop_lo[:, 1, k, :]).then_inc(yz_done, 1)

                        turn_o(0)
                        turn_o(1)
                        pe.wait_ge(hT_done, n + 1 + 1)
                        pe.wait_ge(gain_ready, n + 1)
                        parts(flat[2][0:NGATE, :], lambda k: wg_hi[:, k, :], lambda k: wg_lo[:, k, :],
                              lambda k: hT_hi[s][:, k, :], lambda k: hT_lo[s][:, k, :]).then_inc(gateT_done, 1)
                        pe.wait_ge(wop_done, (b + 1) * 2 + 1)
                        out_o(0)
                        out_h(0)
                        pe.wait_ge(gateT_kept, n + 1 + 1)
                        settle(pe)
                        for j in range(FT):
                            last = t_.transpose(flat[2][:, j * NGATE:(j + 1) * NGATE], lgT[:, j * P:(j + 1) * P],
                                                ident[0:NGATE, 0:NGATE])
                        last.then_inc(gate_done, 1)
                        turn_x(b + 1, f, s, 0)
                        turn_o(2)
                        out_o(1)
                        out_h(1)
                        turn_x(b + 1, f, s, 1)
                        turn_o(3)
                        out_o(2)
                        turn_x(b + 1, f, s, 2)
                        out_h(2)
                        turn_x(b + 1, f, s, 3)
                        out_o(3)
                        out_h(3)

        @block.vector
        def _(dve):
            v_ = nc.vector

            def linker(sem_, base):
                count = [0]

                def link(ins):
                    count[0] += 1
                    ins.then_inc(sem_, 1)
                    dve.wait_ge(sem_, base + count[0] + 1)
                    return count[0]
                return link

            dve.wait_ge(const_in, 16 * NCONST)
            link = linker(dve_const, 0)
            link(v_.tensor_scalar(tnt[:], temp[:], -1.0, None, ALU.mult))
            link(v_.tensor_tensor(tnt[:], tnt[:], temp[:], ALU.min))
            dve.wait_ge(act_const, 1)
            link(v_.tensor_scalar(tnt[:], tnt[:], 1.0, None, ALU.add))
            dve.wait_ge(act_const, 2)
            link(v_.scalar_tensor_tensor(tsc[:], temp[:], 0.0, tnt[:], ALU.max, ALU.add))
            link(v_.tensor_scalar(tsc[:], tsc[:], HD ** -0.5, None, ALU.mult))
            link(v_.tensor_tensor(et[:], et[:], tsc[:].unsqueeze(2).broadcast_to([P, H, HD]), ALU.mult))
            link(v_.tensor_tensor(xT[:, 0, 0:D], et[:].rearrange("p h e -> p (h e)"), et[:].rearrange("p h e -> p (h e)"),
                                  ALU.mult))
            link(v_.tensor_reduce(tb[:], xT[:, 0, 0:D].rearrange("p (h e) -> p h e", h=H), AX.X, ALU.add))
            link(v_.tensor_tensor(tnt[:], tsc[:], tsc[:], ALU.mult))
            link(v_.tensor_tensor(tb[:], tb[:], tnt[:], ALU.add))
            link(v_.tensor_scalar(tb[:], tb[:], 2.0, None, ALU.mult))
            link(v_.memset(wg_raw[:, :, NR + NS:NGATE], 0.0))
            link(v_.tensor_copy(wg_hi[:], wg_raw[:]))
            link(v_.tensor_tensor(wg_lo[:], wg_raw[:], f32(wg_hi[:]), ALU.subtract))
            link(v_.memset(ones32[:], 1.0))
            link(v_.memset(neg_shift[:], -SHIFT))
            dve.wait_ge(pool_const, POOL_CONST)

            def normalise(lb, t, s, half):
                n = lb * NF + t
                xt = x_in[s]
                link = linker(ln_dve, n * L_STEPS)
                dve.wait_ge(x_loaded[s], (lb * (NF // 2) + half) * 16 + 16 + 1)
                settle(dve)
                for j in range(LC):
                    ins = v_.bn_stats(stats[:, j, :], xt[:, j, :])
                link(ins)
                settle(dve)
                for j in range(LC):
                    ins = v_.bn_aggr(mv[:, j, :], stats[:, j, :])
                assert link(ins) == L_STEPS
                v_.tensor_scalar(rstd[:], mv[:, :, 1], LN_EPS, None, ALU.add).then_inc(ln_stats, 1)
                dve.wait_ge(ln_rstd, n + 1 + 1)
                for j in range(LC):
                    ins = v_.tensor_scalar(xt[:, j, :], xt[:, j, :], mv[:, j, 0:1], rstd[:, j:j + 1],
                                           ALU.subtract, ALU.mult)
                ins.then_inc(ln_done, 1)

            def sum_x(lb, t):
                dve.wait_ge(xT_kept, (lb * NF + t) * LC + LC + 1)
                settle(dve)
                v_.tensor_reduce(xpart[:, :, bass.ds(t, 1)].rearrange("p k o -> p (k o)"),
                                 xT[:, :, bass.ds(t * (LC * P), LC * P)], AX.X, ALU.add).then_inc(xpart_done, 1)

            with dve.Fori(0, NF // 2) as i:
                for s in range(2):
                    normalise(0, i * 2 + s, s, i)
                    sum_x(0, i * 2 + s)

            with dve.Fori(0, B) as b:
                dve.wait_ge(xpart_done, (b + 1) * NF + 1)
                settle(dve)
                link = linker(g_set, b * (2 + SET_STEPS * NG))
                link(v_.tensor_reduce(xmean[:], xpart[:], AX.X, ALU.add))
                link(v_.tensor_scalar(xmean[:], xmean[:], 1.0 / S, None, ALU.mult))
                v_.tensor_copy(xbar[:], xmean[:].unsqueeze(2).broadcast_to([P, KC, P])).then_inc(xbar_ready, 1)

                with dve.Fori(0, NG) as g:
                    ig = b * NG + g

                    link = linker(g_set, b * (2 + SET_STEPS * NG) + g * SET_STEPS + 2)
                    dve.wait_ge(w_split, ig + 1 + 1)
                    dve.wait_ge(y_stored[1], b * (16 * NF // 2) + 1)
                    link(v_.tensor_copy(et_g[:], et[:, bass.ds(g * HG, HG), :].rearrange("p h e -> p (h e)")))
                    link(v_.tensor_copy(tsc_g[:], tsc[:, bass.ds(g * HG, HG)]))
                    link(v_.tensor_copy(tb_g[:], tb[:, bass.ds(g * HG, HG)]))
                    v_.memset(kmax[:], 0.0)
                    v_.memset(f32(q_cat[:, :, :, 3 * HD:P]), 0.0)
                    v_.memset(f32(k_cat[:, :, :, 3 * HD + 1:P]), 0.0)
                    link(v_.memset(f32(k_cat[:, :, :, 3 * HD:3 * HD + 1]), 1.0))
                    dve.wait_ge(kmean_done, ig + 1 + 1)
                    v_.tensor_tensor(kmean_b[:], flat[6][:, 0:P], bias_g[:, P:2 * P], ALU.add).then_inc(bias_ready, 1)
                    dve.wait_ge(bias_ready, ig + 1 + 1)
                    assert link(v_.tensor_tensor(bias_g[:, P:2 * P], bias_g[:, P:2 * P], kmean_b[:], ALU.subtract)
                                ) == SET_STEPS

                    def part_x(c, s):
                        dve.wait_ge(xs_hi_done, ig * NCH + c + 1 + 1)
                        v_.tensor_tensor(xs_lo[s][:], xT[:, :, bass.ds(c * CT, CT)], f32(xs_hi[s][:]),
                                         ALU.subtract).then_inc(xs_done, 1)

                    def keep_k(c):
                        n = ig * NCH + c
                        for j in range(CH):
                            dve.wait_ge(k_turned, n * CH + (j + 1) + 1)
                            settle(dve)
                            v_.tensor_copy(kaug[:, :, bass.ds(c * CT + j * P, P)],
                                           flat[6 + j].rearrange("p (h n) -> p h n", h=HG)).then_inc(k_kept, 1)

                    def chunk(c, s, first, last):
                        n = ig * NCH + c
                        link = linker(g_dve, n * G_STEPS)
                        if not last:
                            part_x(c + 1, 1 - s)
                        dve.wait_ge(cat_hi, n * 2 + 1)
                        for j in range(CH):
                            dve.wait_ge(proj_done, n * CH + (j + 1) + 1)
                            ins = v_.tensor_tensor(qk[:, :, j, :], flat[2 * j][:, 0:2 * P].rearrange("p (a n) -> p a n", a=2),
                                                   bias_g[:, 0:2 * P].rearrange("p (a n) -> p a n", a=2), ALU.add)
                            if j == CH - 1:
                                ins.then_inc(qk_kept, 1)
                            v_.tensor_tensor(v[:, bass.ds(c * CH + j, 1), :].rearrange("p o n -> p (o n)"),
                                             flat[2 * j][:, 2 * P:3 * P], bias_g[:, 2 * P:3 * P],
                                             ALU.add).then_inc(projA_kept, 1)
                        if not first:
                            keep_k(c - 1)
                        dve.wait_ge(qk_kept, n + 1 + 1)
                        link(v_.tensor_tensor(sq[:], qk[:, 0], qk[:, 0], ALU.mult))
                        v_.tensor_reduce(ss[:], sq[:].rearrange("p c (h e) -> p c h e", h=HG), AX.X, ALU.add
                                         ).then_inc(ss_ready, 1)
                        link(v_.tensor_tensor(ksq[:], qk[:, 1], qk[:, 1], ALU.mult))
                        link(v_.tensor_reduce(kss[:], ksq[:].rearrange("p c (h e) -> p c h e", h=HG), AX.X, ALU.add))
                        link(v_.tensor_tensor(kmax[:], kmax[:], kss[:], ALU.max))
                        dve.wait_ge(cat_hi, n * 2 + 1 + 1)
                        v_.tensor_tensor(k_cat[:, :, :, 2 * HD:3 * HD], qk[:, 1].rearrange("p c (h e) -> p c h e", h=HG),
                                         f32(k_cat[:, :, :, 0:HD]), ALU.subtract).then_inc(k_cat_done, 1)
                        dve.wait_ge(rn_ready, n + 1 + 1)
                        link(v_.tensor_tensor(rnt[:], rn[:], tsc_g[:].unsqueeze(1).broadcast_to([P, CH, HG]), ALU.mult))
                        assert link(v_.tensor_tensor(qh[:].rearrange("p c (h e) -> p c h e", h=HG),
                                              qk[:, 0].rearrange("p c (h e) -> p c h e", h=HG),
                                              rnt[:].unsqueeze(3).broadcast_to([P, CH, HG, HD]), ALU.mult)) == G_STEPS
                        v_.tensor_tensor(qh[:], qh[:], et_g[:].unsqueeze(1).broadcast_to([P, CH, P]),
                                         ALU.add).then_inc(qh_ready, 1)
                        dve.wait_ge(cat_hi, n * 2 + 2 + 1)
                        v_.tensor_tensor(q_cat[:, :, :, HD:2 * HD], qh[:].rearrange("p c (h e) -> p c h e", h=HG),
                                         f32(q_cat[:, :, :, 0:HD]), ALU.subtract).then_inc(q_cat_done, 1)

                    part_x(0, 0)
                    chunk(0, 0, True, False)
                    chunk(1, 1, False, False)
                    with dve.Fori(1, NCH // 2 - 1) as i:
                        chunk(i * 2, 0, False, False)
                        chunk(i * 2 + 1, 1, False, False)
                    chunk(NCH - 2, 0, False, False)
                    chunk(NCH - 1, 1, False, True)
                    keep_k(NCH - 1)

                    link = linker(bound_dve, ig * BOUND_STEPS)
                    link(v_.tensor_tensor(kmax2[:], kmax[:, 0, :], kmax[:, 1, :], ALU.max))
                    link(v_.tensor_tensor(kmax2[:], kmax2[:], tb_g[:], ALU.mult))
                    v_.tensor_reduce(bound[:], kmax2[:], AX.X, ALU.max).then_inc(bound_ready, 1)
                    dve.wait_ge(bound_turned, ig + 1 + 1)
                    assert link(v_.tensor_reduce(bound1[:], flat[2][0:1, 0:P], AX.X, ALU.max)) == BOUND_STEPS
                    v_.tensor_scalar(flag[:], bound1[:], BOUND2, None, ALU.is_gt).then_inc(flag_ready, 1)

                    dve.wait_ge(projB_kept, (ig + 1) * TT + 1)
                    dve.wait_ge(q_kept, (ig + 1) * TT + 1)
                    dve.wait_ge(q_cat_done, (ig + 1) * NCH + 1)
                    v_.memset(v1[:, :, :, HD:VW], 1.0)
                    v_.memset(state[:, LC], 0.0).then_inc(c_set, 1)
                    dve.wait_ge(c_set, ig + 1 + 1)
                    settle(dve)
                    with dve.Fori(0, NLC) as c:
                        m = ig * NLC + c
                        link = linker(c_dve, m * C_STEPS)
                        raw = lin[:, bass.ds(c * LC, LC), 0:2 * P]
                        v_.tensor_scalar(ex[:], raw, 0.0, None, ALU.min).then_inc(neg_part, 1)
                        dve.wait_ge(kv_done, m * LC + 1)
                        dve.wait_ge(exp_part, m + 1 + 1)
                        v_.scalar_tensor_tensor(phi[:], raw, 0.0, ex[:], ALU.max, ALU.add).then_inc(phi_ready, 1)
                        dve.wait_ge(num_done, m * LC + 1)
                        link(v_.tensor_copy(state[:, 0], state[:, LC]))
                        for t in range(LC):
                            dve.wait_ge(qkT_kept, m * 2 + (t // 2 + 1) + 1)
                            v_.tensor_tensor(qbd[:, t], qkT[:, t, 0, :].unsqueeze(1).broadcast_to([P, HG, P]),
                                             headmask[:].unsqueeze(2).broadcast_to([P, HG, P]), ALU.mult
                                             ).then_inc(qbd_ready, 1)
                        for t0, t1 in ((0, 3), (3, LC)):
                            dve.wait_ge(kv_done, m * LC + t1 + 1)
                            link(v_.tensor_tensor(
                                kvm[:, t0:t1], flat[6 + t0 // 3][:, 0:(t1 - t0) * HG * VW].rearrange(
                                    "p (t h e) -> p t h e", t=t1 - t0, h=HG),
                                headmask[:].unsqueeze(1).unsqueeze(3).broadcast_to([P, t1 - t0, HG, VW]), ALU.mult))
                        for t in range(LC):
                            ins = v_.tensor_tensor(state[:, t + 1], state[:, t], kvm[:, t], ALU.add)
                            if t == LC - 1:
                                ins.then_inc(state_ready, 1)
                            else:
                                link(ins)
                        for t in range(LC):
                            dve.wait_ge(at_done, m * LC + (t + 1) + 1)
                            v_.tensor_tensor(am[:, t], flat[2 + t].rearrange("p (h n) -> p h n", h=HG),
                                             causal[:].unsqueeze(1).broadcast_to([P, HG, P]), ALU.mult
                                             ).then_inc(am_ready, 1)
                        dve.wait_ge(o1_stored, m * 16 + 1)
                        for u in range(2):
                            dve.wait_ge(num_done, m * LC + (2 * u + 2) + 1)
                            num = flat[6 + u][:, 0:2 * HG * VW].rearrange("p (t h e) -> p t h e", t=2, h=HG)
                            link(v_.tensor_scalar(dn[:], num[:, :, :, HD], ATT_EPS, None, ALU.add))
                            steps = link(v_.reciprocal(rdn[:], dn[:]))
                            v_.tensor_tensor(o1[:, 2 * u:2 * u + 2].rearrange("p t (h e) -> p t h e", h=HG),
                                             num[:, :, :, 0:HD], rdn[:].unsqueeze(3).broadcast_to([P, 2, HG, HD]),
                                             ALU.mult).then_inc(o1_ready, 1)
                            if u == 0:
                                dve.wait_ge(o1_ready, m * 2 + 1 + 1)
                        assert steps == C_STEPS

                    dve.wait_ge(flag_ready, ig + 1 + 1)
                    settle(dve)
                    wide = dve.value_load(flag[0:1, 0:1], min_val=0, max_val=1)
                    with dve.If(wide):
                        dve.wait_ge(o1_stored, (ig + 1) * (16 * NLC) + 1)
                        v_.memset(scan_m[:], 0.0)
                        with dve.Fori(0, HG * TT) as r:
                            n = ig * (HG * TT) + r
                            dve.wait_ge(scan_scored, n + 1 + 1)
                            v_.tensor_reduce(rowmax[:], low[:], AX.XY, ALU.max).then_inc(scan_reduced, 1)
                            dve.wait_ge(scan_reduced, n + 1 + 1)
                            v_.tensor_scalar(scan_m[:, 3 * HD:3 * HD + 1], rowmax[:], -1.0, SHIFT, ALU.mult, ALU.add
                                             ).then_inc(scan_max, 1)
                            dve.wait_ge(scan_turned, n + 1 + 1)
                            settle(dve)
                            v_.tensor_copy(qaug[3 * HD:3 * HD + 1, :, :].rearrange("p h n -> p (h n)")[:, bass.ds(r * P, P)],
                                           flat[4][3 * HD:3 * HD + 1, 0:P]).then_inc(scan_row, 1)
                    with dve.Else():
                        dve.sem_inc(scan_reduced, HG * TT)
                        dve.sem_inc(scan_max, HG * TT)
                        dve.sem_inc(scan_row, HG * TT)

                    def sums(kt, n, s):
                        for p in range(2):
                            if (kt, p) in dve_order:
                                dve.wait_ge(exped, n * UNITS + (2 * kt + p + 1) + 1)
                                if kt > 1 + p:
                                    dve.wait_ge(summed, n * DVE_SUMS + DVE_AT[kt - 1 - p, p] + 1)
                                if kt == 1 and p == 1:
                                    settle(dve)
                                    v_.tensor_copy(acc[s][p][:], prob[1][p][:]).then_inc(summed, 1)
                                else:
                                    v_.tensor_tensor(acc[s][p][:], prob[0][p][:] if kt == 1 else acc[s][p][:], prob[kt % 2][p][:],
                                                     ALU.add).then_inc(summed, 1)

                    def keep_out(q, s, half):
                        dve.wait_ge(hT_stored[s], (ig * (NQ // 2) + half) * 16 + 1)
                        dve.wait_ge(weighted, (ig * NQ + q) * TT + TT + 1)
                        settle(dve)
                        v_.tensor_copy(hT_out[s][:], out_bank).then_inc(out_kept, 1)

                    def invert(q, part):
                        n = ig * NQ + q
                        cols = slice(part * QN // DEN_PARTS, (part + 1) * QN // DEN_PARTS)
                        dve.wait_ge(den_done, n + 1 + 1)
                        dve.wait_ge(h_done, n + 1)
                        v_.reciprocal(rden[:, cols], den_bank[:, cols]).then_inc(rden_done, 1)

                    def attend(q, s, half, first=False):
                        n = ig * NQ + q
                        if not first:
                            dve.wait_ge(den_done, n)
                        for kt in range(1, TT):
                            sums(kt, n, s)
                            if kt % 2 == 0 and kt // 2 <= DEN_PARTS and not first:
                                invert(q - 1, kt // 2 - 1)
                        keep_out(q, s, half)

                    attend(0, 0, 0, first=True)
                    with dve.Fori(0, NQ // 2 - 1) as i:
                        attend(i * 2 + 1, 1, i)
                        attend(i * 2 + 2, 0, i + 1)
                    attend(NQ - 1, 1, NQ // 2 - 1)
                    for part in range(DEN_PARTS):
                        invert(NQ - 1, part)

                for a in range(2):
                    dve.wait_ge(wop_hi_done, b * 2 + a + 1 + 1)
                    v_.tensor_tensor(wop_lo[:, a], wop_raw[:, a], f32(wop_hi[:, a]), ALU.subtract).then_inc(wop_done, 1)
                with dve.Fori(0, NF // 2) as i:
                    for s in range(2):
                        f = i * 2 + s
                        n = b * NF + f
                        link = linker(f_dve, n * F_STEPS)

                        def split_o(j):
                            dve.wait_ge(oT_hi_done, n * FT + (j + 1) + 1)
                            v_.tensor_tensor(oT_lo[:, :, j * P:(j + 1) * P], flat[j % 2].rearrange("p (k n) -> p k n", k=KC),
                                             f32(oT_hi[:, :, j * P:(j + 1) * P]), ALU.subtract).then_inc(oT_done, 1)

                        def add_y(j):
                            dve.wait_ge(yz_done, n * FT + (j + 1) + FT + 1)
                            steps = link(v_.tensor_tensor(y[s][:, j, :], flat[4 + j % 2], y[s][:, j, :], ALU.add))
                            v_.scalar_tensor_tensor(y[s][:, j, :], flat[6 + j % 2], gain[:, j:j + 1], y[s][:, j, :],
                                                    ALU.mult, ALU.add).then_inc(y_done, 1)
                            return steps

                        split_o(0)
                        split_o(1)
                        normalise(b + 1, f, s, i)
                        split_o(2)
                        dve.wait_ge(gate_done, n + 1 + 1)
                        link(v_.tensor_tensor(lg[:], flat[2][:, 0:FT * NGATE].rearrange("p (t n) -> p t n", t=FT)[:, :, 0:NR + NS],
                                              bg[:].unsqueeze(1).broadcast_to([P, FT, NR + NS]), ALU.add))
                        settle(dve)
                        for j in range(FT):
                            ins = v_.max(top8[:, j, :], lg[:, j, 0:NR])
                        link(ins)
                        link(v_.tensor_reduce(smax[:], lg[:, :, NR:NR + NS], AX.X, ALU.max))
                        v_.tensor_tensor(z[:, :, 0:NR], lg[:, :, 0:NR], top8[:, :, 0:1].broadcast_to([P, FT, NR]), ALU.subtract)
                        v_.tensor_tensor(z[:, :, NR:NR + NS], lg[:, :, NR:NR + NS], smax[:].broadcast_to([P, FT, NS]), ALU.subtract)
                        v_.tensor_tensor(z[:, :, NR + NS:NZ], top8[:, :, 0:TOP], top8[:, :, 0:1].broadcast_to([P, FT, TOP]),
                                         ALU.subtract).then_inc(gate_z, 1)
                        dve.wait_ge(gate_exp, n + 1 + 1)
                        v_.tensor_reduce(zsum[:, :, 0], z[:, :, 0:NR], AX.X, ALU.add)
                        v_.tensor_reduce(zsum[:, :, 1], z[:, :, NR:NR + NS], AX.X, ALU.add)
                        link(v_.tensor_reduce(zsum[:, :, 2], z[:, :, NR + NS:NZ], AX.X, ALU.add))
                        link(v_.reciprocal(zrec[:], zsum[:, :, 0:2]))
                        link(v_.tensor_tensor(share[:, :, 0:NS], z[:, :, NR:NR + NS], zrec[:, :, 1:2].broadcast_to([P, FT, NS]),
                                              ALU.mult))
                        v_.tensor_tensor(share[:, :, 2], share[:, :, 0], share[:, :, 1], ALU.add)
                        link(v_.tensor_tensor(share[:, :, 3], zsum[:, :, 2], zrec[:, :, 0], ALU.mult))
                        link(v_.tensor_tensor(share[:, :, 2], share[:, :, 2], share[:, :, 0], ALU.mult))
                        link(v_.scalar_tensor_tensor(share[:, :, 3], share[:, :, 3], 2.0 * TOP, share[:, :, 1], ALU.mult, ALU.mult))
                        v_.scalar_tensor_tensor(gain[:], share[:, :, 2], 2.0, share[:, :, 3], ALU.mult, ALU.add
                                                ).then_inc(gain_ready, 1)
                        dve.wait_ge(gain_ready, n + 1 + 1)
                        dve.wait_ge(y_biased, n + 1 + 1)
                        add_y(0)
                        split_o(3)
                        for j in range(1, FT):
                            steps = add_y(j)
                        assert steps == F_STEPS
                        sum_x(b + 1, f)


def kernel(**inputs):
    import numpy as np
    import concourse.bacc as bacc
    from concourse import mybir as mb
    from concourse.bass_utils import run_bass_kernel_spmd

    a = {k: np.asarray(v) for k, v in inputs.items()}
    six = [a["L0_ffn_Wq"].T, a["L0_ffn_Wk"].T, a["L0_ffn_Wv"].T, a["L0_attn_wq"], a["L0_attn_wk"], a["L0_attn_wv"]]

    def rows(w):
        return w.reshape(KC, P, -1).transpose(1, 0, 2)

    arrays = {
        "x": a["L0_attn_x"],
        "w6": np.stack([rows(np.concatenate([w[:, g * P:(g + 1) * P] for w in six], axis=1)) for g in range(NG)]),
        "wop": np.stack([rows(a["L0_attn_wo"]), rows(a["L0_ffn_Wp"].T)], axis=1),
        "wg": rows(np.concatenate([a["L0_ffn_Wr"], a["L0_ffn_Ws"]], axis=0).T),
        "bqkv": np.stack([np.concatenate([a[n][g * P:(g + 1) * P] for n in ("L0_ffn_bq", "L0_ffn_bk", "L0_ffn_bv")])
                          for g in range(NG)]),
        "bp": a["L0_ffn_bp"],
        "bg": np.concatenate([a["L0_ffn_br"], a["L0_ffn_bs"]]),
        "temp": a["L0_ffn_temperature"].reshape(-1),
        "qe": a["L0_ffn_query_embedding"].reshape(-1),
    }
    arrays = {f"in_{k}": np.ascontiguousarray(v) for k, v in arrays.items()}
    nc = bacc.Bacc("TRN2", target_bir_lowering=False, num_devices=1)
    args = [nc.dram_tensor(k, v.shape, mb.dt.from_np(v.dtype), kind="ExternalInput").ap() for k, v in arrays.items()]
    args.append(nc.dram_tensor("out", (B, S, D), mb.dt.float32, kind="ExternalOutput").ap())
    build(nc, *args)
    r = run_bass_kernel_spmd(nc, [arrays], core_ids=[0])
    return r.results[0]["out"]
```

```python
from contextlib import ExitStack

import concourse.bass as bass
from concourse import mybir

F32 = mybir.dt.float32
F32R = mybir.dt.float32r
I32 = mybir.dt.int32
ALU = mybir.AluOpType
ACT = mybir.ActivationFunctionType
AX = mybir.AxisListType

P = 128
B, S, D, H, HD = 4, 2048, 512, 16, 32
HG = P // HD
NG = H // HG
KC = D // P
TT = S // P
CH = 2
NCH = TT // CH
CT = CH * P
LC = 4
NLC = TT // LC
QN = 512
NQ = S // QN
FT = 4
NF = TT // FT
W6 = 6 * P
NR, NS = 15, 2
NGATE = NR + NS + 1
TOP = 3
DVE_SUMS = TT + TT // 2
POOL_SUMS = TT // 2 - 1
DEN_PARTS = 4
VW = HD + 1
LN_EPS, ATT_EPS = 1e-5, 1e-6
SHIFT = 65.0
BOUND2 = (2 * SHIFT) ** 2


def f32(ap):
    return ap.bitcast(F32)


def build(nc, x_d, w6_d, wop_d, wg_d, bqkv_d, bp_d, bg_d, temp_d, qe_d, out_d):
    o1_d = nc.dram_tensor("o1_scratch", [B, S, D], F32, kind="Internal").ap()
    hT_d = nc.dram_tensor("hT_scratch", [B, D, S], F32, kind="Internal").ap()

    with ExitStack() as ctx:
        def sem(name):
            return ctx.enter_context(nc.semaphore(name))

        counted = []

        def counter(name, ahead=0):
            counted.append((sem(name), 1 + ahead))
            return counted[-1][0]

        KB = 1024
        cursor = [17 * KB]

        def at(name, shape, dt, off):
            return nc.alloc_sbuf_tensor_at(name, shape, dt, offset=off)

        def sb(name, shape, dt):
            n = 4
            for d in shape[1:]:
                n *= d
            off = cursor[0]
            cursor[0] += (n + 31) // 32 * 32
            return at(name, shape, dt, off)

        xT = sb("xT", [P, KC, S], F32)
        kaug = sb("kaug", [P, HG, S], F32R)
        qaug = sb("qaug", [P, HG, S], F32R)
        w_hi = sb("w_hi", [P, KC, W6], F32R)
        w_lo = sb("w_lo", [P, KC, W6], F32R)
        v = sb("v", [P, TT, P], F32)
        sq = sb("sq", [P, CH, P], F32)
        state = sb("state", [P, 2 * CH, HG, VW], F32)
        ident = sb("ident", [P, P], F32)
        ident_r = sb("ident_r", [P, P], F32R)
        causal = sb("causal", [P, P], F32)
        headmask = sb("headmask", [P, HG], F32)
        ones32 = sb("ones32", [P, HD], F32)
        minus_half = sb("minus_half", [P, CH, HG], F32)
        neg_shift = sb("neg_shift", [P, 1], F32)
        bias_g = sb("bias_g", [P, 3 * P], F32)
        kmean_b = sb("kmean_b", [P, P], F32)
        bp = sb("bp", [P, D], F32)
        bg = sb("bg", [P, NR + NS], F32)
        et = sb("et", [P, H, HD], F32)
        et_g = sb("et_g", [P, P], F32)
        temp = sb("temp", [P, H], F32)
        tnt = sb("tnt", [P, H], F32)
        tsc = sb("tsc", [P, H], F32)
        tsc_g = sb("tsc_g", [P, HG], F32)
        tb = sb("tb", [P, H], F32)
        tb_g = sb("tb_g", [P, HG], F32)
        xpart = sb("xpart", [P, KC, TT // LC], F32)
        xmean = sb("xmean", [P, KC], F32)
        xbar = sb("xbar", [P, KC, P], F32R)
        stats = sb("stats", [P, LC, 6], F32)
        mv = sb("mv", [P, LC, 2], F32)
        rstd = sb("rstd", [P, LC], F32)
        ss = sb("ss", [P, CH, HG], F32)
        rn = sb("rn", [P, CH, HG], F32)
        rnt = sb("rnt", [P, CH, HG], F32)
        kss = sb("kss", [P, CH, HG], F32)
        kmax = sb("kmax", [P, CH, HG], F32)
        kmax2 = sb("kmax2", [P, HG], F32)
        bound = sb("bound", [P, 1], F32)
        bound1 = sb("bound1", [1, 1], F32)
        flag = sb("flag", [1, 1], I32)
        rowmax = sb("rowmax", [P, 1], F32)
        dn = sb("dn", [P, 2, HG], F32)
        rdn = sb("rdn", [P, 2, HG], F32)
        wg_raw = sb("wg_raw", [P, KC, NGATE], F32)
        wg_hi = sb("wg_hi", [P, KC, NGATE], F32R)
        wg_lo = sb("wg_lo", [P, KC, NGATE], F32R)
        NZ = NR + NS + TOP
        rden = sb("rden", [P, QN], F32)
        lgT = rden[0:NGATE, :]
        lg = sb("lg", [P, FT, NR + NS], F32)
        top8 = sb("top8", [P, FT, 8], F32)
        smax = sb("smax", [P, FT, 1], F32)
        z = sb("z", [P, FT, NZ], F32)
        zsum = sb("zsum", [P, FT, 3], F32)
        zrec = sb("zrec", [P, FT, 2], F32)
        share = sb("share", [P, FT, 4], F32)
        gain = sb("gain", [P, FT], F32)
        r1 = cursor[0]
        xs_hi = [at(f"xs_hi{s}", [P, KC, CT], F32R, r1 + s * 4 * KB) for s in range(2)]
        xs_lo = [at(f"xs_lo{s}", [P, KC, CT], F32R, r1 + (8 + s * 4) * KB) for s in range(2)]
        q_cat = at("q_cat", [P, CH, HG, P], F32R, r1 + 16 * KB)
        k_cat = at("k_cat", [P, CH, HG, P], F32R, r1 + 20 * KB)
        xs0_hi = at("xs0_hi", [P, KC, P], F32R, r1 + 24 * KB)
        xs0_lo = at("xs0_lo", [P, KC, P], F32R, r1 + 26 * KB)
        qh = at("qh", [P, CH, P], F32, r1 + 28 * KB)
        ksq = at("ksq", [P, CH, P], F32, r1 + 31 * KB)
        o1 = at("o1", [P, LC, P], F32, r1 + 29 * KB)
        hT_out = [at(f"hT_out{s}", [P, QN], F32, r1 + (32 + 2 * s) * KB) for s in range(2)]
        r1_end = r1 + 36 * KB
        w_raw = at("w_raw", [P, KC, W6], F32, r1)
        hT_in = at("hT_in", [P, KC, FT * P], F32, r1)
        x_in = [at(f"x_in{s}", [P, LC, D], F32, r1 + (12 + s * 8) * KB) for s in range(2)]
        o1_in = at("o1_in", [P, FT, D], F32, r1 + 28 * KB)
        scan_q = at("scan_q", [P, P], F32R, r1)
        scan_m = at("scan_m", [P, P], F32, r1 + KB)
        r2 = (r1_end + 31) // 32 * 32
        lin = [at(f"lin{s}", [P, CH, 3 * P], F32, r2 + s * 3 * KB) for s in range(2)]
        ex = at("ex", [P, CH, 2 * P], F32, r2 + 6 * KB)
        phi = [at(f"phi{s}", [P, CH, 2 * P], F32, r2 + (8 + s * 2) * KB) for s in range(2)]
        qkT = [at(f"qkT{a}", [P, CH, 2, P], F32, (r2 + 12 * KB, r1)[a]) for a in range(2)]
        qbd = [at(f"qbd{a}", [P, CH, HG, P], F32, (r2 + 14 * KB, r1 + 2 * KB)[a]) for a in range(2)]
        am = [at(f"am{a}", [P, CH, HG, P], F32, (r1 + 32 * KB, r1 + 6 * KB)[a]) for a in range(2)]
        VB = CH * HG * VW * 4
        v1 = [at(f"v1{s}", [P, CH, HG, VW], F32, r2 + 18 * KB + s * VB) for s in range(2)]
        kvm = at("kvm", [P, CH, HG, VW], F32, r2 + 18 * KB + 2 * VB)
        qk = at("qk", [P, 2, CH, P], F32, r2 + 22 * KB)
        assert 18 * KB + 3 * VB <= 22 * KB
        prob = [[at(f"prob{t}{p}", [P, 2, QN], F32, r2 + (t * 2 + p) * 4 * KB) for p in range(2)] for t in range(2)]
        acc = [[at(f"acc{s}{p}", [P, 2, QN], F32, (r2 + 16 * KB, r1 + 12 * KB)[s] + p * 4 * KB) for p in range(2)]
               for s in range(2)]
        acc_pool = [at(f"acc_pool{s}", [P, 2, QN], F32, r1 + (28 - 8 * s) * KB) for s in range(2)]
        hT_hi1 = at("hT_hi1", [P, KC, FT * P], F32R, r2)
        hT_lo1 = at("hT_lo1", [P, KC, FT * P], F32R, r2 + 8 * KB)
        y = [at("y0", [P, FT, D], F32, r2 + 16 * KB), v[:].rearrange("p t (a n) -> p t a n", a=1).rearrange(
            "p (j r) a n -> p j (r a n)", j=FT)]
        assert r2 + 24 * KB <= nc.sbuf_usable_end, (r2 + 24 * KB, nc.sbuf_usable_end)
        wop_raw = xT[:, 0:2, :].rearrange("p a (k n) -> p a k n", k=KC)
        wop_hi = kaug[:, 0:2, :].rearrange("p a (k n) -> p a k n", k=KC)
        wop_lo = kaug[:, 2:4, :].rearrange("p a (k n) -> p a k n", k=KC)
        hT_hi = [qaug[:, 0, :].rearrange("p (k n) -> p k n", k=KC), hT_hi1[:]]
        hT_lo = [qaug[:, 1, :].rearrange("p (k n) -> p k n", k=KC), hT_lo1[:]]
        oT_hi = qaug[:, 2, :].rearrange("p (k n) -> p k n", k=KC)
        oT_lo = qaug[:, 3, :].rearrange("p (k n) -> p k n", k=KC)

        low = ctx.enter_context(nc.psum_tensor("low", [P, 4, 512], F32))
        high = ctx.enter_context(nc.psum_tensor("high", [P, 4, 512], F32))
        flat = [t[:, i, :] for t in (low, high) for i in range(4)]
        places = [low[:, 0:2, :], low[:, 2:4, :], high[:, 0:2, :]]
        out_bank, den_bank = flat[6], flat[7]

        const_in = sem("const_in")
        settled = sem("settled")
        pool_const = sem("pool_const")
        dve_const = counter("dve_const")
        act_const = sem("act_const")
        x_loaded = [counter(f"x_loaded{s}") for s in range(2)]
        ln_stats, ln_rstd, ln_dve, ln_done = counter("ln_stats"), counter("ln_rstd"), counter("ln_dve"), counter("ln_done")
        ln_pool = counter("ln_pool")
        xT_turned, xT_kept = counter("xT_turned", LC), counter("xT_kept")
        xpart_done, xbar_ready = counter("xpart_done"), counter("xbar_ready")
        w_loaded, w_split, w_hi_done = counter("w_loaded"), counter("w_split"), counter("w_hi_done")
        xs_hi_done, xs_done = counter("xs_hi_done"), counter("xs_done")
        xs0_hi_done, xs0_done = counter("xs0_hi_done"), counter("xs0_done")
        proj_done, projA_kept, projB_kept = counter("proj_done"), counter("projA_kept"), counter("projB_kept")
        qk_kept = counter("qk_kept")
        ss_ready, rn_ready, qh_ready = counter("ss_ready"), counter("rn_ready"), counter("qh_ready")
        cat_hi, k_cat_done, q_cat_done = counter("cat_hi"), counter("k_cat_done"), counter("q_cat_done")
        k_turned, q_turned, k_kept, q_kept = counter("k_turned"), counter("q_turned"), counter("k_kept"), counter("q_kept")
        g_dve, g_set = counter("g_dve"), counter("g_set")
        kmean_done, bias_ready = counter("kmean_done"), counter("bias_ready")
        bound_ready, bound_turned, flag_ready = counter("bound_ready"), counter("bound_turned"), counter("flag_ready")
        scan_staged, scan_scored, scan_max, scan_turned, scan_row = (
            counter("scan_staged"), counter("scan_scored"), counter("scan_max"), counter("scan_turned"), counter("scan_row"))
        bound_dve, scan_reduced = counter("bound_dve"), counter("scan_reduced")
        neg_part, exp_part, phi_ready, v1_ready = counter("neg_part"), counter("exp_part"), counter("phi_ready"), counter("v1_ready")
        phi_turned, qkT_kept, kv_done, qbd_ready = counter("phi_turned"), counter("qkT_kept"), counter("kv_done"), counter("qbd_ready")
        at_done, am_ready, state_ready, num_done = counter("at_done"), counter("am_ready"), counter("state_ready"), counter("num_done")
        states_dve, outputs_dve, o1_ready, o1_stored = counter("states_dve"), counter("outputs_dve"), counter("o1_ready"), counter("o1_stored")
        scored, exped, weighted = counter("scored"), counter("exped"), counter("weighted")
        summed, pool_summed = counter("summed"), counter("pool_summed")
        out_kept, den_done, rden_done, h_done = counter("out_kept"), counter("den_done"), counter("rden_done"), counter("h_done")
        hT_stored = [counter(f"hT_stored{s}") for s in range(2)]
        wop_loaded, wop_hi_done, wop_done = counter("wop_loaded"), counter("wop_hi_done"), counter("wop_done")
        hT_loaded, o1_loaded, xr_loaded = counter("hT_loaded"), counter("o1_loaded"), counter("xr_loaded")
        hT_hi_done, hT_done = counter("hT_hi_done"), counter("hT_done")
        o1_turned, oT_hi_done, oT_done = counter("o1_turned"), counter("oT_hi_done"), counter("oT_done")
        gateT_done, gateT_kept = counter("gateT_done"), counter("gateT_kept")
        gate_done, gate_z, gate_exp, gain_ready = counter("gate_done"), counter("gate_z"), counter("gate_exp"), counter("gain_ready")
        f_dve, yz_done, y_done = counter("f_dve"), counter("yz_done", FT), counter("y_done")
        y_biased = counter("y_biased")
        y_stored = [counter(f"y_stored{s}") for s in range(2)]

        NCONST = 5
        POOL_CONST = 8
        DVE_CONST = 16
        L_STEPS, SET_STEPS, G_STEPS, BOUND_STEPS, C_STEPS, F_STEPS = 2, 5, 6, 3, 2, 13

        dve_order = [(0, 1)] + [(kt, p) for kt in range(1, TT) for p in range(2) if p == 0 or kt % 2]
        DVE_AT = {kp: i + 1 for i, kp in enumerate(dve_order)} | {(0, 0): 2}
        assert len(dve_order) == DVE_SUMS

        UNITS = 2 * TT

        def place(u, s):
            return (u + s * (UNITS % 3)) % 3

        def unit_before(n, u, s):
            if u >= 3:
                return n * UNITS + (u - 3) + 1
            return n * UNITS - UNITS + max(w for w in range(UNITS) if place(w, 1 - s) == place(u, s)) + 1

        def settle(eng):
            eng.sem_inc(settled, 1)

        block = ctx.enter_context(nc.Block())

        @block.sync
        def _(sp):
            for dst, src in (
                (bp[:], bp_d.partition_broadcast(P)),
                (bg[:], bg_d.partition_broadcast(P)),
                (temp[:], temp_d.partition_broadcast(P)),
                (et[:].rearrange("p h e -> p (h e)"), qe_d.partition_broadcast(P)),
                (wg_raw[:, :, 0:NR + NS], wg_d),
            ):
                sp.dma_start(dst, src).then_inc(const_in, 16)

            for started, n in counted:
                sp.sem_inc(started, n)

            def load_x(lb, batch, t, s):
                sp.wait_ge(xT_turned, (lb * NF + t - 1) * LC + LC + 1)
                sp.dma_start(x_in[s][:], x_d[batch, bass.ds(t * (LC * P), LC * P), :].rearrange(
                    "o (t p) d -> p (o t) d", p=P)).then_inc(x_loaded[s], 16)

            for s in range(2):
                load_x(0, slice(0, 1), s, s)
            sp.dma_start(w_raw[:], w6_d[0]).then_inc(w_loaded, 16)
            sp.dma_start(bias_g[:], bqkv_d[0].partition_broadcast(P)).then_inc(w_loaded, 16)
            with sp.Fori(1, NF // 2) as i:
                for s in range(2):
                    load_x(0, slice(0, 1), i * 2 + s, s)

            with sp.Fori(0, B) as b:
                def load_h(f):
                    sp.dma_start(hT_in[:], hT_d[bass.ds(b, 1), :, bass.ds(f * (FT * P), FT * P)].rearrange(
                        "o (k p) n -> p (o k) n", p=P)).then_inc(hT_loaded, 16)

                with sp.Fori(0, NG) as g:
                    ig = b * NG + g
                    with sp.Fori(0, NLC) as c:
                        m = ig * NLC + c
                        sp.wait_ge(o1_ready, (m + 1) * (LC // CH) + 1)
                        sp.dma_start(
                            o1_d[bass.ds(b, 1), bass.ds(c * (LC * P), LC * P), bass.ds(g * P, P)].rearrange(
                                "o (t p) d -> p (o t) d", p=P), o1[:]).then_inc(o1_stored, 16)
                    sp.wait_ge(num_done, ig * TT + TT + 1)
                    sp.wait_ge(o1_stored, (ig + 1) * (16 * NLC) + 1)
                    sp.wait_ge(scored, ig * (NQ * UNITS) + 1 + 1)
                    sp.dma_start(w_raw[:], w6_d[bass.ds((g + 1) % NG, 1)].rearrange("o p k n -> p (o k) n")).then_inc(
                        w_loaded, 16)
                    sp.dma_start(bias_g[:], bqkv_d[bass.ds((g + 1) % NG, 1), :].rearrange(
                        "o n -> (o n)").partition_broadcast(P)).then_inc(w_loaded, 16)
                    def store_h(i, s):
                        sp.wait_ge(h_done, ig * NQ + i * 2 + (s + 1) + 1)
                        sp.dma_start(hT_d[bass.ds(b, 1), bass.ds(g * P, P), bass.ds(i * (2 * QN) + s * QN, QN)].rearrange(
                            "o p n -> (o p) n"), hT_out[s][:]).then_inc(hT_stored[s], 16)

                    with sp.If((g + 1) % NG):
                        settle(sp)
                    with sp.Else():
                        sp.dma_start(wop_raw, wop_d).then_inc(wop_loaded, 16)
                    with sp.Fori(0, NQ // 2 - 1) as i:
                        store_h(i, 0)
                        store_h(i, 1)
                    store_h(NQ // 2 - 1, 0)
                    with sp.If((g + 1) % NG):
                        settle(sp)
                    with sp.Else():
                        sp.wait_ge(w_split, (b + 1) * NG + 1 + 1)
                        sp.wait_ge(hT_stored[0], (b + 1) * (16 * NG * NQ // 2) + 1)
                        settle(sp)
                        load_h(0)
                    store_h(NQ // 2 - 1, 1)

                def load(f, s, half, first=False):
                    n = b * NF + f
                    if not first:
                        sp.wait_ge(hT_done, n + 1)
                        settle(sp)
                        load_h(f)
                    sp.wait_ge(o1_turned, n * FT + 1)
                    sp.wait_ge(hT_stored[1], (b + 1) * (16 * NG * NQ // 2) + 1)
                    sp.dma_start(o1_in[:], o1_d[bass.ds(b, 1), bass.ds(f * (FT * P), FT * P), :].rearrange(
                        "o (t p) d -> p (o t) d", p=P)).then_inc(o1_loaded, 16)
                    load_x(b + 1, bass.ds((b + 1) % B, 1), f, s)
                    sp.wait_ge(y_stored[s], (b * (NF // 2) + half) * 16 + 1)
                    sp.dma_start(y[s][:], x_d[bass.ds(b, 1), bass.ds(f * (FT * P), FT * P), :].rearrange(
                        "o (t p) d -> p (o t) d", p=P)).then_inc(xr_loaded, 16)

                def store(f, s):
                    sp.wait_ge(y_done, (b * NF + f) * FT + FT + 1)
                    sp.dma_start(out_d[bass.ds(b, 1), bass.ds(f * (FT * P), FT * P), :].rearrange(
                        "o (t p) d -> p (o t) d", p=P), y[s][:]).then_inc(y_stored[s], 16)

                load(0, 0, 0, first=True)
                with sp.Fori(0, NF // 2 - 1) as i:
                    load(i * 2 + 1, 1, i)
                    store(i * 2, 0)
                    load(i * 2 + 2, 0, i + 1)
                    store(i * 2 + 1, 1)
                load(NF - 1, 1, NF // 2 - 1)
                store(NF - 2, 0)
                store(NF - 1, 1)
            for s in range(2):
                sp.wait_ge(y_stored[s], 16 * B * NF // 2 + 1)
                sp.wait_ge(x_loaded[s], 16 * (B + 1) * NF // 2 + 1)
                sp.wait_ge(hT_stored[s], 16 * B * NG * NQ // 2 + 1)
            sp.wait_ge(o1_stored, 16 * B * NG * NLC + 1)
            sp.wait_ge(w_loaded, 32 * (B * NG + 1) + 1)

        @block.gpsimd
        def _(pool):
            g = nc.gpsimd
            g.memset(ident[:], 0.0).then_inc(pool_const, 1)
            g.memset(causal[:], 1.0).then_inc(pool_const, 1)
            g.memset(headmask[:], 1.0).then_inc(pool_const, 1)
            g.memset(minus_half[:], -0.5).then_inc(pool_const, 1)
            pool.wait_ge(pool_const, 4)
            g.affine_select(out=ident[:], in_=ident[:], compare_op=ALU.not_equal, fill=1.0, base=0,
                            pattern=[[-1, P]], channel_multiplier=1).then_inc(pool_const, 1)
            g.affine_select(out=causal[:], in_=causal[:], compare_op=ALU.is_ge, fill=0.0, base=0,
                            pattern=[[1, P]], channel_multiplier=-1).then_inc(pool_const, 1)
            g.affine_select(out=headmask[:], in_=headmask[:], compare_op=ALU.is_ge, fill=0.0, base=0,
                            pattern=[[-HD, HG]], channel_multiplier=1).then_inc(pool_const, 1)
            pool.wait_ge(pool_const, 7)
            g.affine_select(out=headmask[:], in_=headmask[:], compare_op=ALU.is_ge, fill=0.0, base=HD - 1,
                            pattern=[[HD, HG]], channel_multiplier=-1).then_inc(pool_const, 1)

            HW6 = W6 // 2

            def round_weights(n, i):
                if i == 0:
                    pool.wait_ge(w_loaded, n * 32 + 32 + 1)
                    settle(pool)
                r = slice(i % 2 * HW6, (i % 2 + 1) * HW6)
                g.tensor_copy(w_hi[:, i // 2, r], w_raw[:, i // 2, r]).then_inc(w_hi_done, 1)

            def rest_of_weights(n, i):
                r = slice(i % 2 * HW6, (i % 2 + 1) * HW6)
                pool.wait_ge(w_hi_done, (n + 1) * (2 * KC) + 1)
                ins = g.tensor_tensor(w_lo[:, i // 2, r], w_raw[:, i // 2, r], f32(w_hi[:, i // 2, r]), ALU.subtract)
                if i == 2 * KC - 1:
                    ins.then_inc(w_split, 1)

            def rstd_of(lb, t):
                pool.wait_ge(ln_stats, lb * NF + t + 1 + 1)
                g.tensor_tensor(rstd[:], rstd[:], minus_half[:].rearrange("p a b -> p (a b)")[:, 0:LC],
                                ALU.pow).then_inc(ln_rstd, 1)

            for t in range(NF):
                rstd_of(0, t)
                if t == 1:
                    for i in range(2 * KC):
                        rest_of_weights(0, i)
            with pool.Fori(0, B) as b:
                with pool.Fori(0, NG) as gr:
                    ig = b * NG + gr
                    with pool.Fori(0, NCH) as c:
                        n = ig * NCH + c
                        pool.wait_ge(ss_ready, n + 1 + 1)
                        g.tensor_tensor(rn[:], ss[:], minus_half[:], ALU.pow).then_inc(rn_ready, 1)

                    def scale(q, s):
                        pool.wait_ge(rden_done, (ig * NQ + q) * DEN_PARTS + DEN_PARTS + 1)
                        g.tensor_tensor(hT_out[s][:], hT_out[s][:], rden[:], ALU.mult).then_inc(h_done, 1)

                    def sums(q, s, first=False, split=None, m0=0):
                        n = ig * NQ + q
                        pool.wait_ge(summed, n * DVE_SUMS + DVE_AT[0, 1] + 1)
                        for m in range(1, POOL_SUMS + 1):
                            pool.wait_ge(exped, n * UNITS + (4 * m + 2) + 1)
                            if m > 1:
                                pool.wait_ge(pool_summed, n * POOL_SUMS + (m - 1) + 1)
                            g.tensor_tensor(acc_pool[s][:], acc_pool[s][:], prob[0][1][:], ALU.add
                                            ).then_inc(pool_summed, 1)
                            if split and m0 <= m < m0 + 5:
                                for piece in range((m - m0) * 8 // 5, (m - m0 + 1) * 8 // 5):
                                    split(ig + 1, piece)
                            if m == 4 and not first:
                                scale(q - 1, 1 - s)

                    sums(0, 0, first=True, split=round_weights, m0=3)
                    with pool.Fori(0, NQ // 2 - 1) as i:
                        sums(i * 2 + 1, 1)
                        sums(i * 2 + 2, 0)
                    sums(NQ - 1, 1, split=rest_of_weights, m0=1)
                    scale(NQ - 1, 1)

                pool.wait_ge(h_done, (b + 1) * (NG * NQ) + 1)
                settle(pool)
                with pool.Fori(0, NF // 2) as i:
                    for s in range(2):
                        f = i * 2 + s
                        n = b * NF + f
                        pool.wait_ge(hT_loaded, n * 16 + 16 + 1)
                        pool.wait_ge(yz_done, (n - 1) * FT + FT + 1)
                        settle(pool)
                        g.tensor_copy(hT_hi[s], hT_in[:]).then_inc(hT_hi_done, 1)
                        pool.wait_ge(hT_hi_done, n + 1 + 1)
                        g.tensor_tensor(hT_lo[s], hT_in[:], f32(hT_hi[s]), ALU.subtract).then_inc(hT_done, 1)
                        pool.wait_ge(xr_loaded, n * 16 + 16 + 1)
                        g.tensor_tensor(y[s][:], y[s][:], bp[:].unsqueeze(1).broadcast_to([P, FT, D]), ALU.add
                                        ).then_inc(y_biased, 1)
                        rstd_of(b + 1, f)

        @block.scalar
        def _(act):
            s_ = nc.scalar
            act.wait_ge(dve_const, 2 + 1)
            s_.activation(tnt[:], tnt[:], ACT.Exp).then_inc(act_const, 1)
            act.wait_ge(dve_const, 3 + 1)
            s_.activation(tnt[:], tnt[:], ACT.Ln).then_inc(act_const, 1)
            act.wait_ge(dve_const, DVE_CONST + 1)

            def keep_x(lb, t, j, bank=3):
                n = (lb * NF + t) * LC + j
                act.wait_ge(xT_turned, n + 1 + LC + 1)
                settle(act)
                s_.activation(xT[:, :, bass.ds(t * (LC * P) + j * P, P)], flat[bank].rearrange("p (k n) -> p k n", k=KC),
                              ACT.Copy).then_inc(xT_kept, 1)

            act.wait_ge(w_loaded, 32 + 1)
            s_.activation(w_hi[:], w_raw[:], ACT.Copy).then_inc(w_hi_done, 2 * KC)
            with act.Fori(0, NF) as t:
                for j in range(LC):
                    keep_x(0, t, j, 3 - j % 2)

            with act.Fori(0, B) as b:
                act.wait_ge(xbar_ready, b + 1 + 1)
                s_.activation(xs0_hi[:], xT[:, :, 0:P], ACT.Copy).then_inc(xs0_hi_done, 1)
                with act.Fori(0, NG) as g:
                    ig = b * NG + g

                    def part_x(c, s, tile0=0):
                        s_.activation(xs_hi[s][:, :, tile0 * P:CT], xT[:, :, bass.ds(c * CT + tile0 * P, CT - tile0 * P)],
                                      ACT.Copy).then_inc(xs_hi_done, 1)

                    def keep_lin(c, s, j):
                        act.wait_ge(proj_done, (ig * NCH + c) * CH + (j + 1) + 1)
                        s_.activation(lin[s][:, j, :], flat[2 * j + 1][:, 0:3 * P], ACT.Copy).then_inc(projB_kept, 1)

                    def stack_k(c):
                        n = ig * NCH + c
                        act.wait_ge(qk_kept, n + 1 + 1)
                        act.wait_ge(k_turned, n * CH + 1)
                        s_.activation(k_cat[:, :, :, 0:2 * HD].rearrange("p c h (r e) -> p (c h) r e", r=2),
                                      qk[:, 1].rearrange("p c (h e) -> p (c h) e", h=HG).unsqueeze(2)
                                      .broadcast_to([P, CH * HG, 2, HD]), ACT.Copy).then_inc(cat_hi, 1)

                    def stack_q(c):
                        n = ig * NCH + c
                        act.wait_ge(qh_ready, n + 1 + 1)
                        act.wait_ge(q_turned, n * CH + 1)
                        s_.activation(q_cat[:, :, :, 0:4 * HD].rearrange("p c h (r e) -> p (c h) r e", r=4)[:, :, 0:3:2],
                                      qh[:].rearrange("p c (h e) -> p (c h) e", h=HG).unsqueeze(2)
                                      .broadcast_to([P, CH * HG, 2, HD]), ACT.Copy).then_inc(cat_hi, 1)

                    def keep_q(c, j):
                        act.wait_ge(q_turned, (ig * NCH + c) * CH + (j + 1) + 1)
                        settle(act)
                        s_.activation(qaug[:, :, bass.ds(c * CT + j * P, P)], flat[5].rearrange("p (h n) -> p h n", h=HG),
                                      ACT.Copy).then_inc(q_kept, 1)

                    def exp_part_of(c):
                        act.wait_ge(neg_part, ig * NCH + c + 1 + 1)
                        s_.activation(ex[:], ex[:], ACT.Exp).then_inc(exp_part, 1)

                    def keep_v(c, s):
                        s_.activation(v1[s][:, :, :, 0:HD], lin[s][:, :, 2 * P:3 * P].rearrange("p t (h e) -> p t h e", h=HG),
                                      ACT.Copy).then_inc(v1_ready, 1)

                    def keep_qkT(c, a=0, bank=6):
                        act.wait_ge(phi_turned, ig * NCH + c + 1 + 1)
                        s_.activation(qkT[a][:].rearrange("p t a n -> p (t a n)"), flat[bank], ACT.Copy).then_inc(qkT_kept, 1)

                    def step(c, s, project=True, turn=True, linear=True, ahead=True):
                        if turn:
                            stack_k(c - 1)
                        if linear:
                            keep_qkT(c - 2)
                        if turn:
                            stack_q(c - 1)
                            exp_part_of(c - 1)
                        if ahead:
                            act.wait_ge(proj_done, (ig * NCH + c) * CH + 1)
                            settle(act)
                            part_x(c + 1, 1 - s)
                        if project:
                            keep_lin(c, s, 0)
                        if turn:
                            keep_v(c - 1, 1 - s)
                            keep_q(c - 1, 0)
                        if project:
                            keep_lin(c, s, 1)
                        if turn:
                            keep_q(c - 1, 1)

                    act.wait_ge(den_done, ig * NQ + 1)
                    act.wait_ge(w_split, ig + 1 + 1)
                    act.wait_ge(xbar_ready, b + 1 + 1)
                    act.wait_ge(y_stored[0], b * (16 * NF // 2) + 1)
                    part_x(0, 0, tile0=1)
                    step(0, 0, turn=False, linear=False)
                    step(1, 1, linear=False)
                    with act.Fori(1, NCH // 2 - 1) as i:
                        step(i * 2, 0)
                        step(i * 2 + 1, 1)
                    step(NCH - 2, 0)
                    step(NCH - 1, 1, ahead=False)
                    c0, c1 = NCH - 2, NCH - 1
                    stack_k(c1)
                    keep_qkT(c0)
                    stack_q(c1)
                    exp_part_of(c1)
                    keep_v(c1, 1)
                    keep_q(c1, 0)
                    keep_qkT(c1, 1, 0)
                    keep_q(c1, 1)

                    act.wait_ge(flag_ready, ig + 1 + 1)
                    settle(act)
                    wide = act.value_load(flag[0:1, 0:1], min_val=0, max_val=1)
                    with act.If(wide):
                        act.wait_ge(o1_stored, (ig + 1) * (16 * NLC) + 1)
                        with act.Fori(0, HG * TT) as r:
                            act.wait_ge(scan_scored, ig * (HG * TT) + r + 1)
                            settle(act)
                            s_.activation(scan_q[:], f32(qaug[:].rearrange("p h n -> p (h n)")[:, bass.ds(r * P, P)]),
                                          ACT.Copy).then_inc(scan_staged, 1)
                    with act.Else():
                        act.sem_inc(scan_staged, HG * TT)

                    act.wait_ge(o1_ready, (ig + 1) * NCH + 1)
                    def exps(q, s, first=False):
                        n = ig * NQ + q
                        for kt in range(TT):
                            for p in range(2):
                                act.wait_ge(scored, n * UNITS + (2 * kt + p + 1) + 1)
                                back, n0 = (kt - 2, n) if kt >= 2 else (kt - 2 + TT, n - 1)
                                if kt >= 2 or not first:
                                    if p == 0:
                                        act.wait_ge(weighted, n0 * TT + (back + 1) + 1)
                                    if p == 1 and back % 2 == 0 and back > 0:
                                        act.wait_ge(pool_summed, n0 * POOL_SUMS + back // 2 + 1)
                                    else:
                                        act.wait_ge(summed, n0 * DVE_SUMS + DVE_AT[back, p] + 1)
                                s_.activation(prob[kt % 2][p][:], places[place(2 * kt + p, s)], ACT.Exp,
                                              bias=neg_shift[:, 0:1]).then_inc(exped, 1)

                    exps(0, 0, first=True)
                    with act.Fori(0, NQ // 2 - 1) as i:
                        exps(i * 2 + 1, 1)
                        exps(i * 2 + 2, 0)
                    exps(NQ - 1, 1)

                act.wait_ge(wop_loaded, b * 16 + 16 + 1)
                for a in range(2):
                    s_.activation(wop_hi[:, a], wop_raw[:, a], ACT.Copy).then_inc(wop_hi_done, 1)
                with act.Fori(0, NF) as f:
                    n = b * NF + f

                    def keep_o(j):
                        act.wait_ge(o1_turned, n * FT + (j + 1) + 1)
                        act.wait_ge(yz_done, (n - 1) * FT + (j + 1) + FT + 1)
                        s_.activation(oT_hi[:, :, j * P:(j + 1) * P], flat[j % 2].rearrange("p (k n) -> p k n", k=KC),
                                      ACT.Copy).then_inc(oT_hi_done, 1)

                    keep_o(0)
                    keep_o(1)
                    act.wait_ge(gateT_done, n + 1 + 1)
                    s_.activation(lgT, flat[2][0:NGATE, :], ACT.Copy).then_inc(gateT_kept, 1)
                    keep_x(b + 1, f, 0)
                    keep_o(2)
                    act.wait_ge(gate_z, n + 1 + 1)
                    s_.activation(z[:], z[:], ACT.Exp).then_inc(gate_exp, 1)
                    keep_x(b + 1, f, 1)
                    keep_o(3)
                    keep_x(b + 1, f, 2)
                    keep_x(b + 1, f, 3)

        @block.tensor
        def _(pe):
            t_ = nc.tensor
            pe.wait_ge(pool_const, POOL_CONST)
            pe.wait_ge(dve_const, DVE_CONST + 1)

            def parts(out, hi, lo, whi, wlo, open_group=True):
                for k in range(KC):
                    t_.matmul(out, hi(k), whi(k), start=(k == 0 and open_group), stop=False)
                    t_.matmul(out, hi(k), wlo(k), start=False, stop=False)
                    last = t_.matmul(out, lo(k), whi(k), start=False, stop=(k == KC - 1))
                return last

            def turn_x(lb, t, s, j, bank=3):
                n = (lb * NF + t) * LC + j
                if j == 0:
                    pe.wait_ge(ln_done, lb * NF + t + 1 + 1)
                pe.wait_ge(xT_kept, n + 1 if j == 0 or bank == 3 else n)
                for k in range(KC):
                    last = t_.transpose(flat[bank][:, k * P:(k + 1) * P], x_in[s][:, j, k * P:(k + 1) * P], ident[:])
                last.then_inc(xT_turned, 1)

            with pe.Fori(0, NF // 2) as i:
                for s in range(2):
                    for j in range(LC):
                        turn_x(0, i * 2 + s, s, j, 3 - j % 2)

            with pe.Fori(0, B) as b:
                with pe.Fori(0, NG) as g:
                    ig = b * NG + g

                    pe.wait_ge(w_split, ig + 1 + 1)
                    pe.wait_ge(xbar_ready, b + 1 + 1)
                    pe.wait_ge(out_kept, ig * NQ + 1)
                    pe.wait_ge(xT_kept, (b + 1) * TT + 1)
                    pe.wait_ge(y_done, b * TT + 1)
                    for k in range(KC):
                        last = t_.matmul(flat[6][:, 0:P], xbar[:, k, :], w_hi[:, k, P:2 * P],
                                         start=(k == 0), stop=(k == KC - 1))
                    last.then_inc(kmean_done, 1)

                    def project(c, s, j, pieces=range(KC), first=False):
                        n = ig * NCH + c
                        if first:
                            pe.wait_ge(xs0_done, b + 1 + 1)
                        else:
                            pe.wait_ge(xs_done, n + 1 + 1)
                        pe.wait_ge(projA_kept, n * CH + 1)
                        pe.wait_ge(projB_kept, n * CH + 1)
                        for k in pieces:
                            hi, lo = (x[:, k, :] for x in (xs0_hi, xs0_lo)) if first else (
                                x[:, k, j * P:(j + 1) * P] for x in (xs_hi[s], xs_lo[s]))
                            for x, w in ((hi, w_hi), (hi, w_lo), (lo, w_hi)):
                                for a in range(2):
                                    last = t_.matmul(flat[2 * j + a][:, 0:3 * P], x, w[:, k, a * 3 * P:(a + 1) * 3 * P],
                                                     start=(k == 0 and x is hi and w is w_hi),
                                                     stop=(k == KC - 1 and x is lo))
                        if k == KC - 1:
                            last.then_inc(proj_done, 1)

                    def turn_cat(c, j, cat, done, kept, turned, bank):
                        n = ig * NCH + c
                        pe.wait_ge(done, n + 1 + 1)
                        pe.wait_ge(kept, n * CH + j + 1)
                        for h in range(HG):
                            last = t_.transpose(bank[:, h * P:(h + 1) * P].bitcast(F32R), cat[:, j, h, :], ident_r[:])
                        last.then_inc(turned, 1)

                    def turn_k(c, j):
                        turn_cat(c, j, k_cat, k_cat_done, k_kept, k_turned, flat[4])

                    def turn_q(c, j):
                        turn_cat(c, j, q_cat, q_cat_done, q_kept, q_turned, flat[5])

                    def turn_phi(c, s, bank=6):
                        n = ig * NCH + c
                        pe.wait_ge(phi_ready, n + 1 + 1)
                        if bank == 6:
                            pe.wait_ge(bias_ready, ig + 1 + 1)
                            pe.wait_ge(o1_ready, n + 1)
                        for t in range(CH):
                            for a in range(2):
                                last = t_.transpose(flat[bank][:, (2 * t + a) * P:(2 * t + a + 1) * P],
                                                    phi[s][:, t, a * P:(a + 1) * P], ident[:])
                        last.then_inc(phi_turned, 1)

                    def key_values(c, s, bank=7):
                        n = ig * NCH + c
                        pe.wait_ge(v1_ready, n + 1 + 1)
                        if bank == 7:
                            pe.wait_ge(rden_done, ig * (NQ * DEN_PARTS) + 1)
                            pe.wait_ge(am_ready, n * CH + 1)
                        for t in range(CH):
                            last = t_.matmul(flat[bank][:, t * HG * VW:(t + 1) * HG * VW], phi[s][:, t, P:2 * P],
                                             v1[s][:, t].rearrange("p h e -> p (h e)"), start=True, stop=True)
                        last.then_inc(kv_done, 1)

                    def key_query(c, t, a=0, bank=6):
                        n = ig * NCH + c
                        pe.wait_ge(qkT_kept, n + 1 + 1)
                        if t:
                            pe.wait_ge(state_ready, n + 1 + 1)
                        pe.wait_ge(qbd_ready, n * CH + (t + 1) + 1)
                        t_.matmul(flat[bank + t], qkT[a][:, t, 1, :], qbd[a][:, t].rearrange("p h n -> p (h n)"),
                                  start=True, stop=True).then_inc(at_done, 1)

                    def outputs(c, s, t, a=0, bank=6):
                        n = ig * NCH + c
                        pe.wait_ge(state_ready, n + 1 + 1)
                        pe.wait_ge(am_ready, n * CH + (t + 1) + 1)
                        o = t * HG * VW
                        t_.matmul(flat[bank][:, o:o + HG * VW], qkT[a][:, t, 0, :],
                                  state[:, 2 * s + t].rearrange("p h e -> p (h e)"), start=True, stop=True)
                        for h in range(HG):
                            last = t_.matmul(flat[bank][:, o + h * VW:o + (h + 1) * VW], am[a][:, t, h, :], v1[s][:, t, h, :],
                                             start=False, stop=True, skip_group_check=True)
                        last.then_inc(num_done, 1)

                    def step(c, s, turn=True, linear=True, first=False):
                        project(c, s, 0, range(KC // 2), first)
                        if linear:
                            turn_phi(c - 2, s)
                        project(c, s, 0, range(KC // 2, KC), first)
                        if linear:
                            key_values(c - 2, s)
                        if turn:
                            turn_k(c - 1, 0)
                            turn_q(c - 1, 0)
                        if linear:
                            key_query(c - 2, 0)
                        project(c, s, 1)
                        if linear:
                            key_query(c - 2, 1)
                            outputs(c - 2, s, 0)
                        if turn:
                            turn_k(c - 1, 1)
                            turn_q(c - 1, 1)
                        if linear:
                            outputs(c - 2, s, 1)

                    step(0, 0, turn=False, linear=False, first=True)
                    step(1, 1, linear=False)
                    with pe.Fori(1, NCH // 2) as i:
                        step(i * 2, 0)
                        step(i * 2 + 1, 1)
                    c0, c1 = NCH - 2, NCH - 1
                    turn_phi(c0, 0)
                    key_values(c0, 0)
                    pe.wait_ge(bound_ready, ig + 1 + 1)
                    pe.wait_ge(projA_kept, (ig + 1) * TT + 1)
                    pe.wait_ge(projB_kept, (ig + 1) * TT + 1)
                    t_.transpose(flat[2][0:1, 0:P], bound[:], ident[:]).then_inc(bound_turned, 1)
                    turn_k(c1, 0)
                    turn_q(c1, 0)
                    key_query(c0, 0)
                    turn_phi(c1, 1, 0)
                    key_values(c1, 1, 1)
                    key_query(c0, 1)
                    outputs(c0, 0, 0)
                    turn_k(c1, 1)
                    turn_q(c1, 1)
                    pe.wait_ge(flag_ready, ig + 1 + 1)
                    key_query(c1, 0, 1, 2)
                    key_query(c1, 1, 1, 2)
                    outputs(c0, 0, 1)
                    outputs(c1, 1, 0, 1, 0)
                    outputs(c1, 1, 1, 1, 0)
                    pe.wait_ge(q_kept, (ig + 1) * TT + 1)
                    pe.wait_ge(k_kept, (ig + 1) * TT + 1)
                    settle(pe)

                    wide = pe.value_load(flag[0:1, 0:1], min_val=0, max_val=1)
                    pe.wait_ge(o1_ready, (ig + 1) * NCH + 1)
                    pe.wait_ge(am_ready, (ig + 1) * TT + 1)
                    with pe.If(wide):
                        with pe.Fori(0, HG) as h:
                            with pe.Fori(0, TT) as r:
                                n = ig * (HG * TT) + h * TT + r
                                pe.wait_ge(scan_staged, n + 1 + 1)
                                pe.wait_ge(scan_row, n + 1)
                                for k in range(4):
                                    last = t_.matmul(flat[k], scan_q[:], kaug[:].rearrange("p h n -> p (h n)")[
                                        :, bass.ds(h * S + k * 512, 512)], start=True, stop=True)
                                last.then_inc(scan_scored, 1)
                                pe.wait_ge(scan_max, n + 1 + 1)
                                t_.transpose(flat[4][:, 0:P], scan_m[:], ident[:]).then_inc(scan_turned, 1)
                    with pe.Else():
                        pe.sem_inc(scan_scored, HG * TT)
                        pe.sem_inc(scan_turned, HG * TT)

                    pe.wait_ge(scan_row, (ig + 1) * (HG * TT) + 1)
                    settle(pe)
                    def score(q, s, u, first=False):
                        kt, p = u // 2, u % 2
                        if u >= 3 or not first:
                            pe.wait_ge(exped, unit_before(ig * NQ + q, u, s) + 1)
                        for a in range(2):
                            h = 2 * p + a
                            last = t_.matmul(places[place(u, s)][:, a, :], kaug[:, h, kt * P:(kt + 1) * P],
                                             qaug[:, h, bass.ds(q * QN, QN)], start=True, stop=True)
                        last.then_inc(scored, 1)

                    def weigh(q, kt):
                        pe.wait_ge(exped, (ig * NQ + q) * UNITS + (2 * kt + 2) + 1)
                        for h in range(HG):
                            last = t_.matmul(out_bank[h * HD:(h + 1) * HD, :], v[:, kt, h * HD:(h + 1) * HD],
                                             prob[kt % 2][h // 2][:, h % 2, :], start=(kt == 0), stop=(kt == TT - 1))
                        last.then_inc(weighted, 1)

                    def total(q, s):
                        n = ig * NQ + q
                        pe.wait_ge(summed, (n + 1) * DVE_SUMS + 1)
                        pe.wait_ge(pool_summed, (n + 1) * POOL_SUMS + 1)
                        pe.wait_ge(rden_done, n * DEN_PARTS + 1)
                        for i in range(2):
                            for h in range(i * 2, HG):
                                last = t_.matmul(den_bank[h * HD:(h + 1) * HD, :], ones32[:],
                                                 (acc_pool[s] if i else acc[s][h // 2])[:, h % 2, :],
                                                 start=(i == 0), stop=(i == 1 or h < 2))
                        last.then_inc(den_done, 1)

                    def attend(q, s, first=False, last=False):
                        for kt in range(TT):
                            for u in (2 * kt + 2, 2 * kt + 3):
                                if u < UNITS:
                                    score(q, s, u, first)
                                elif not last:
                                    score(q + 1, 1 - s, u - UNITS)
                            if kt == 0 and not first:
                                total(q - 1, 1 - s)
                                pe.wait_ge(out_kept, ig * NQ + q + 1)
                            weigh(q, kt)

                    for u in range(2):
                        score(0, 0, u, first=True)
                    attend(0, 0, first=True)
                    with pe.Fori(0, NQ // 2 - 1) as i:
                        attend(i * 2 + 1, 1)
                        attend(i * 2 + 2, 0)
                    attend(NQ - 1, 1, last=True)
                    total(NQ - 1, 1)

                pe.wait_ge(h_done, (b + 1) * (NG * NQ) + 1)
                settle(pe)
                with pe.Fori(0, NF // 2) as i:
                    for s in range(2):
                        f = i * 2 + s
                        n = b * NF + f

                        def turn_o(j):
                            if j == 0:
                                pe.wait_ge(o1_loaded, n * 16 + 16 + 1)
                            pe.wait_ge(oT_done, n * FT + max(j - 1, 0) + 1)
                            for k in range(KC):
                                last = t_.transpose(flat[j % 2][:, k * P:(k + 1) * P], o1_in[:, j, k * P:(k + 1) * P], ident[:])
                            last.then_inc(o1_turned, 1)

                        def out_o(j):
                            r = slice(j * P, (j + 1) * P)
                            pe.wait_ge(oT_done, n * FT + (j + 1) + 1)
                            pe.wait_ge(y_done, n * FT + max(j - 1, 0) + 1)
                            parts(flat[4 + j % 2], lambda k: oT_hi[:, k, r], lambda k: oT_lo[:, k, r],
                                  lambda k: wop_hi[:, 0, k, :], lambda k: wop_lo[:, 0, k, :])

                        def out_h(j):
                            r = slice(j * P, (j + 1) * P)
                            parts(flat[6 + j % 2], lambda k: hT_hi[s][:, k, r], lambda k: hT_lo[s][:, k, r],
                                  lambda k: wop_hi[:, 1, k, :], lambda k: wop_lo[:, 1, k, :]).then_inc(yz_done, 1)

                        turn_o(0)
                        turn_o(1)
                        pe.wait_ge(hT_done, n + 1 + 1)
                        pe.wait_ge(gain_ready, n + 1)
                        parts(flat[2][0:NGATE, :], lambda k: wg_hi[:, k, :], lambda k: wg_lo[:, k, :],
                              lambda k: hT_hi[s][:, k, :], lambda k: hT_lo[s][:, k, :]).then_inc(gateT_done, 1)
                        pe.wait_ge(wop_done, (b + 1) * 2 + 1)
                        out_o(0)
                        out_h(0)
                        pe.wait_ge(gateT_kept, n + 1 + 1)
                        settle(pe)
                        for j in range(FT):
                            last = t_.transpose(flat[2][:, j * NGATE:(j + 1) * NGATE], lgT[:, j * P:(j + 1) * P],
                                                ident[0:NGATE, 0:NGATE])
                        last.then_inc(gate_done, 1)
                        turn_x(b + 1, f, s, 0)
                        turn_o(2)
                        out_o(1)
                        out_h(1)
                        turn_x(b + 1, f, s, 1)
                        turn_o(3)
                        out_o(2)
                        turn_x(b + 1, f, s, 2)
                        out_h(2)
                        turn_x(b + 1, f, s, 3)
                        out_o(3)
                        out_h(3)

        @block.vector
        def _(dve):
            v_ = nc.vector

            def linker(sem_, base):
                count = [0]

                def link(ins):
                    count[0] += 1
                    ins.then_inc(sem_, 1)
                    dve.wait_ge(sem_, base + count[0] + 1)
                    return count[0]
                return link

            dve.wait_ge(const_in, 16 * NCONST)
            link = linker(dve_const, 0)
            link(v_.tensor_scalar(tnt[:], temp[:], -1.0, None, ALU.mult))
            link(v_.tensor_tensor(tnt[:], tnt[:], temp[:], ALU.min))
            dve.wait_ge(act_const, 1)
            link(v_.tensor_scalar(tnt[:], tnt[:], 1.0, None, ALU.add))
            dve.wait_ge(act_const, 2)
            link(v_.scalar_tensor_tensor(tsc[:], temp[:], 0.0, tnt[:], ALU.max, ALU.add))
            link(v_.tensor_scalar(tsc[:], tsc[:], HD ** -0.5, None, ALU.mult))
            link(v_.tensor_tensor(et[:], et[:], tsc[:].unsqueeze(2).broadcast_to([P, H, HD]), ALU.mult))
            link(v_.tensor_tensor(xT[:, 0, 0:D], et[:].rearrange("p h e -> p (h e)"), et[:].rearrange("p h e -> p (h e)"),
                                  ALU.mult))
            link(v_.tensor_reduce(tb[:], xT[:, 0, 0:D].rearrange("p (h e) -> p h e", h=H), AX.X, ALU.add))
            link(v_.tensor_tensor(tnt[:], tsc[:], tsc[:], ALU.mult))
            link(v_.tensor_tensor(tb[:], tb[:], tnt[:], ALU.add))
            link(v_.tensor_scalar(tb[:], tb[:], 2.0, None, ALU.mult))
            link(v_.memset(wg_raw[:, :, NR + NS:NGATE], 0.0))
            link(v_.tensor_copy(wg_hi[:], wg_raw[:]))
            link(v_.tensor_tensor(wg_lo[:], wg_raw[:], f32(wg_hi[:]), ALU.subtract))
            link(v_.memset(ones32[:], 1.0))
            dve.wait_ge(pool_const, POOL_CONST)
            v_.tensor_copy(ident_r[:], ident[:])
            link(v_.memset(neg_shift[:], -SHIFT))

            def normalise(lb, t, s, half):
                n = lb * NF + t
                xt = x_in[s]
                link = linker(ln_dve, n * L_STEPS)
                dve.wait_ge(x_loaded[s], (lb * (NF // 2) + half) * 16 + 16 + 1)
                settle(dve)
                for j in range(LC):
                    ins = v_.bn_stats(stats[:, j, :], xt[:, j, :])
                link(ins)
                settle(dve)
                for j in range(LC):
                    ins = v_.bn_aggr(mv[:, j, :], stats[:, j, :])
                assert link(ins) == L_STEPS
                v_.tensor_scalar(rstd[:], mv[:, :, 1], LN_EPS, None, ALU.add).then_inc(ln_stats, 1)
                dve.wait_ge(ln_rstd, n + 1 + 1)
                for j in range(LC):
                    ins = v_.tensor_scalar(xt[:, j, :], xt[:, j, :], mv[:, j, 0:1], rstd[:, j:j + 1],
                                           ALU.subtract, ALU.mult)
                ins.then_inc(ln_done, 1)

            def sum_x(lb, t):
                dve.wait_ge(xT_kept, (lb * NF + t) * LC + LC + 1)
                settle(dve)
                v_.tensor_reduce(xpart[:, :, bass.ds(t, 1)].rearrange("p k o -> p (k o)"),
                                 xT[:, :, bass.ds(t * (LC * P), LC * P)], AX.X, ALU.add).then_inc(xpart_done, 1)

            with dve.Fori(0, NF // 2) as i:
                for s in range(2):
                    normalise(0, i * 2 + s, s, i)
                for s in range(2):
                    sum_x(0, i * 2 + s)

            with dve.Fori(0, B) as b:
                dve.wait_ge(xpart_done, (b + 1) * NF + 1)
                settle(dve)
                link = linker(g_set, b * (2 + SET_STEPS * NG))
                link(v_.tensor_reduce(xmean[:], xpart[:], AX.X, ALU.add))
                link(v_.tensor_scalar(xmean[:], xmean[:], 1.0 / S, None, ALU.mult))
                v_.tensor_copy(xbar[:], xmean[:].unsqueeze(2).broadcast_to([P, KC, P])).then_inc(xbar_ready, 1)
                dve.wait_ge(xs0_hi_done, b + 1 + 1)
                v_.tensor_tensor(xs0_lo[:], xT[:, :, 0:P], f32(xs0_hi[:]), ALU.subtract).then_inc(xs0_done, 1)

                with dve.Fori(0, NG) as g:
                    ig = b * NG + g

                    def part_x(c, s, tile0=0):
                        r = slice(tile0 * P, CT)
                        dve.wait_ge(xs_hi_done, ig * NCH + c + 1 + 1)
                        v_.tensor_tensor(xs_lo[s][:, :, r], xT[:, :, bass.ds(c * CT + tile0 * P, CT - tile0 * P)],
                                         f32(xs_hi[s][:, :, r]), ALU.subtract).then_inc(xs_done, 1)

                    part_x(0, 0, tile0=1)
                    link = linker(g_set, b * (2 + SET_STEPS * NG) + g * SET_STEPS + 2)
                    dve.wait_ge(w_split, ig + 1 + 1)
                    dve.wait_ge(y_stored[1], b * (16 * NF // 2) + 1)
                    link(v_.tensor_copy(et_g[:], et[:, bass.ds(g * HG, HG), :].rearrange("p h e -> p (h e)")))
                    link(v_.tensor_copy(tsc_g[:], tsc[:, bass.ds(g * HG, HG)]))
                    link(v_.tensor_copy(tb_g[:], tb[:, bass.ds(g * HG, HG)]))
                    v_.memset(kmax[:], 0.0)
                    v_.memset(f32(q_cat[:, :, :, 3 * HD:P]), 0.0)
                    v_.memset(f32(k_cat[:, :, :, 3 * HD + 1:P]), 0.0)
                    link(v_.memset(f32(k_cat[:, :, :, 3 * HD:3 * HD + 1]), 1.0))
                    for s in range(2):
                        v_.memset(v1[s][:, :, :, HD:VW], 1.0)
                    v_.memset(state[:, 0], 0.0)
                    dve.wait_ge(kmean_done, ig + 1 + 1)
                    v_.tensor_tensor(kmean_b[:], flat[6][:, 0:P], bias_g[:, P:2 * P], ALU.add).then_inc(bias_ready, 1)
                    dve.wait_ge(bias_ready, ig + 1 + 1)
                    assert link(v_.tensor_tensor(bias_g[:, P:2 * P], bias_g[:, P:2 * P], kmean_b[:], ALU.subtract)
                                ) == SET_STEPS

                    def keep_qk(c, j):
                        n = ig * NCH + c
                        if j == 0:
                            dve.wait_ge(cat_hi, n * 2 + 1)
                            dve.wait_ge(k_cat_done, n + 1)
                        dve.wait_ge(proj_done, n * CH + (j + 1) + 1)
                        ins = v_.tensor_tensor(qk[:, :, j, :], flat[2 * j][:, 0:2 * P].rearrange("p (a n) -> p a n", a=2),
                                               bias_g[:, 0:2 * P].rearrange("p (a n) -> p a n", a=2), ALU.add)
                        if j == CH - 1:
                            ins.then_inc(qk_kept, 1)
                        v_.tensor_tensor(v[:, bass.ds(c * CH + j, 1), :].rearrange("p o n -> p (o n)"),
                                         flat[2 * j][:, 2 * P:3 * P], bias_g[:, 2 * P:3 * P], ALU.add).then_inc(projA_kept, 1)

                    def squares(c):
                        n = ig * NCH + c
                        link = linker(g_dve, n * G_STEPS)
                        dve.wait_ge(qk_kept, n + 1 + 1)
                        link(v_.tensor_tensor(sq[:], qk[:, 0], qk[:, 0], ALU.mult))
                        v_.tensor_reduce(ss[:], sq[:].rearrange("p c (h e) -> p c h e", h=HG), AX.X, ALU.add
                                         ).then_inc(ss_ready, 1)
                        link(v_.tensor_tensor(ksq[:], qk[:, 1], qk[:, 1], ALU.mult))
                        link(v_.tensor_reduce(kss[:], ksq[:].rearrange("p c (h e) -> p c h e", h=HG), AX.X, ALU.add))
                        link(v_.tensor_tensor(kmax[:], kmax[:], kss[:], ALU.max))

                    def stack_lows(c):
                        n = ig * NCH + c
                        link = linker(g_dve, n * G_STEPS + 4)
                        dve.wait_ge(rn_ready, n + 1 + 1)
                        link(v_.tensor_tensor(rnt[:], rn[:], tsc_g[:].unsqueeze(1).broadcast_to([P, CH, HG]), ALU.mult))
                        steps = link(v_.tensor_tensor(qh[:].rearrange("p c (h e) -> p c h e", h=HG),
                                                      qk[:, 0].rearrange("p c (h e) -> p c h e", h=HG),
                                                      rnt[:].unsqueeze(3).broadcast_to([P, CH, HG, HD]), ALU.mult))
                        assert 4 + steps == G_STEPS
                        v_.tensor_tensor(qh[:], qh[:], et_g[:].unsqueeze(1).broadcast_to([P, CH, P]),
                                         ALU.add).then_inc(qh_ready, 1)
                        dve.wait_ge(cat_hi, n * 2 + 1 + 1)
                        v_.tensor_tensor(k_cat[:, :, :, 2 * HD:3 * HD], qk[:, 1].rearrange("p c (h e) -> p c h e", h=HG),
                                         f32(k_cat[:, :, :, 0:HD]), ALU.subtract).then_inc(k_cat_done, 1)
                        dve.wait_ge(cat_hi, n * 2 + 2 + 1)
                        v_.tensor_tensor(q_cat[:, :, :, HD:2 * HD], qh[:].rearrange("p c (h e) -> p c h e", h=HG),
                                         f32(q_cat[:, :, :, 0:HD]), ALU.subtract).then_inc(q_cat_done, 1)

                    def keep_k(c, j):
                        dve.wait_ge(k_turned, (ig * NCH + c) * CH + (j + 1) + 1)
                        settle(dve)
                        v_.tensor_copy(kaug[:, :, bass.ds(c * CT + j * P, P)], flat[4].rearrange("p (h n) -> p h n", h=HG)
                                       ).then_inc(k_kept, 1)

                    def negatives(c, s):
                        dve.wait_ge(projB_kept, (ig * NCH + c) * CH + CH + 1)
                        v_.tensor_scalar(ex[:], lin[s][:, :, 0:2 * P], 0.0, None, ALU.min).then_inc(neg_part, 1)

                    def features(c, s):
                        dve.wait_ge(exp_part, ig * NCH + c + 1 + 1)
                        v_.scalar_tensor_tensor(phi[s][:], lin[s][:, :, 0:2 * P], 0.0, ex[:], ALU.max, ALU.add
                                                ).then_inc(phi_ready, 1)

                    def spread_q(c, a=0):
                        dve.wait_ge(qkT_kept, ig * NCH + c + 1 + 1)
                        for t in range(CH):
                            v_.tensor_tensor(qbd[a][:, t], qkT[a][:, t, 0, :].unsqueeze(1).broadcast_to([P, HG, P]),
                                             headmask[:].unsqueeze(2).broadcast_to([P, HG, P]), ALU.mult).then_inc(qbd_ready, 1)

                    def states(c, s, bank=7, last=False):
                        n = ig * NCH + c
                        link = linker(states_dve, n * C_STEPS)
                        dve.wait_ge(state_ready, n + 1)
                        dve.wait_ge(kv_done, n + 1 + 1)
                        link(v_.tensor_tensor(kvm[:], flat[bank][:, 0:CH * HG * VW].rearrange("p (t h e) -> p t h e", t=CH, h=HG),
                                              headmask[:].unsqueeze(1).unsqueeze(3).broadcast_to([P, CH, HG, VW]), ALU.mult))
                        assert link(v_.tensor_tensor(state[:, 2 * s + 1], state[:, 2 * s], kvm[:, 0], ALU.add)) == C_STEPS
                        if last:
                            dve.sem_inc(state_ready, 1)
                        else:
                            v_.tensor_tensor(state[:, 2 * (1 - s)], state[:, 2 * s + 1], kvm[:, 1], ALU.add
                                             ).then_inc(state_ready, 1)

                    def mask(c, t, a=0, bank=6):
                        n = ig * NCH + c
                        for s in range(2):
                            dve.wait_ge(hT_stored[s], ig * (16 * NQ // 2) + 1)
                        dve.wait_ge(at_done, n * CH + (t + 1) + 1)
                        v_.tensor_tensor(am[a][:, t], flat[bank + t].rearrange("p (h n) -> p h n", h=HG),
                                         causal[:].unsqueeze(1).broadcast_to([P, HG, P]), ALU.mult).then_inc(am_ready, 1)

                    def outputs(c, s, store, bank=6):
                        n = ig * NCH + c
                        link = linker(outputs_dve, n * C_STEPS)
                        dve.wait_ge(o1_ready, n + 1)
                        if s == 0:
                            dve.wait_ge(o1_stored, (ig * NLC + store) * 16 + 1)
                        dve.wait_ge(num_done, n * CH + CH + 1)
                        num = flat[bank][:, 0:CH * HG * VW].rearrange("p (t h e) -> p t h e", t=CH, h=HG)
                        link(v_.tensor_scalar(dn[:], num[:, :, :, HD], ATT_EPS, None, ALU.add))
                        assert link(v_.reciprocal(rdn[:], dn[:])) == C_STEPS
                        v_.tensor_tensor(o1[:, s * CH:(s + 1) * CH].rearrange("p t (h e) -> p t h e", h=HG),
                                         num[:, :, :, 0:HD], rdn[:].unsqueeze(3).broadcast_to([P, CH, HG, HD]),
                                         ALU.mult).then_inc(o1_ready, 1)

                    def step(i, s, project=True, turn=True, linear=True, ahead=True):
                        c = i * 2 + s
                        if turn:
                            negatives(c - 1, 1 - s)
                            stack_lows(c - 1)
                        if linear:
                            spread_q(c - 2)
                        if turn:
                            features(c - 1, 1 - s)
                        if project:
                            keep_qk(c, 0)
                        if linear:
                            states(c - 2, s)
                        if turn:
                            keep_k(c - 1, 0)
                        if ahead:
                            part_x(c + 1, 1 - s)
                        if linear:
                            mask(c - 2, 0)
                        if project:
                            keep_qk(c, 1)
                        if linear:
                            mask(c - 2, 1)
                        if project:
                            squares(c)
                        if turn:
                            keep_k(c - 1, 1)
                        if linear:
                            outputs(c - 2, s, i - 1)

                    step(0, 0, turn=False, linear=False)
                    step(0, 1, linear=False)
                    with dve.Fori(1, NCH // 2 - 1) as i:
                        step(i, 0)
                        step(i, 1)
                    step(NCH // 2 - 1, 0)
                    step(NCH // 2 - 1, 1, ahead=False)
                    link = linker(bound_dve, ig * BOUND_STEPS)
                    link(v_.tensor_tensor(kmax2[:], kmax[:, 0, :], kmax[:, 1, :], ALU.max))
                    link(v_.tensor_tensor(kmax2[:], kmax2[:], tb_g[:], ALU.mult))
                    v_.tensor_reduce(bound[:], kmax2[:], AX.X, ALU.max).then_inc(bound_ready, 1)
                    c0, c1 = NCH - 2, NCH - 1
                    negatives(c1, 1)
                    stack_lows(c1)
                    spread_q(c0)
                    states(c0, 0)
                    features(c1, 1)
                    dve.wait_ge(bound_turned, ig + 1 + 1)
                    assert link(v_.tensor_reduce(bound1[:], flat[2][0:1, 0:P], AX.X, ALU.max)) == BOUND_STEPS
                    v_.tensor_scalar(flag[:], bound1[:], BOUND2, None, ALU.is_gt).then_inc(flag_ready, 1)
                    keep_k(c1, 0)
                    mask(c0, 0)
                    spread_q(c1, 1)
                    states(c1, 1, 1, last=True)
                    mask(c0, 1)
                    keep_k(c1, 1)
                    for t in range(CH):
                        mask(c1, t, 1, 2)
                    outputs(c0, 0, NLC - 1)
                    outputs(c1, 1, NLC - 1, 0)

                    dve.wait_ge(flag_ready, ig + 1 + 1)
                    settle(dve)
                    wide = dve.value_load(flag[0:1, 0:1], min_val=0, max_val=1)
                    with dve.If(wide):
                        dve.wait_ge(o1_stored, (ig + 1) * (16 * NLC) + 1)
                        v_.memset(scan_m[:], 0.0)
                        with dve.Fori(0, HG * TT) as r:
                            n = ig * (HG * TT) + r
                            dve.wait_ge(scan_scored, n + 1 + 1)
                            v_.tensor_reduce(rowmax[:], low[:], AX.XY, ALU.max).then_inc(scan_reduced, 1)
                            dve.wait_ge(scan_reduced, n + 1 + 1)
                            v_.tensor_scalar(scan_m[:, 3 * HD:3 * HD + 1], rowmax[:], -1.0, SHIFT, ALU.mult, ALU.add
                                             ).then_inc(scan_max, 1)
                            dve.wait_ge(scan_turned, n + 1 + 1)
                            settle(dve)
                            v_.tensor_copy(qaug[3 * HD:3 * HD + 1, :, :].rearrange("p h n -> p (h n)")[:, bass.ds(r * P, P)],
                                           flat[4][3 * HD:3 * HD + 1, 0:P]).then_inc(scan_row, 1)
                    with dve.Else():
                        dve.sem_inc(scan_reduced, HG * TT)
                        dve.sem_inc(scan_max, HG * TT)
                        dve.sem_inc(scan_row, HG * TT)

                    def sums(kt, n, s):
                        for p in range(2):
                            if (kt, p) in dve_order:
                                dve.wait_ge(exped, n * UNITS + (2 * kt + p + 1) + 1)
                                if kt > 1 + p:
                                    dve.wait_ge(summed, n * DVE_SUMS + DVE_AT[kt - 1 - p, p] + 1)
                                if kt < 2 and p == 1:
                                    settle(dve)
                                    v_.tensor_copy((acc[s][p] if kt else acc_pool[s])[:], prob[kt][p][:]).then_inc(summed, 1)
                                else:
                                    v_.tensor_tensor(acc[s][p][:], prob[0][p][:] if kt == 1 else acc[s][p][:], prob[kt % 2][p][:],
                                                     ALU.add).then_inc(summed, 1)

                    def keep_out(q, s, half):
                        dve.wait_ge(hT_stored[s], (ig * (NQ // 2) + half) * 16 + 1)
                        dve.wait_ge(weighted, (ig * NQ + q) * TT + TT + 1)
                        settle(dve)
                        v_.tensor_copy(hT_out[s][:], out_bank).then_inc(out_kept, 1)

                    def invert(q, part):
                        n = ig * NQ + q
                        cols = slice(part * QN // DEN_PARTS, (part + 1) * QN // DEN_PARTS)
                        dve.wait_ge(den_done, n + 1 + 1)
                        dve.wait_ge(h_done, n + 1)
                        v_.reciprocal(rden[:, cols], den_bank[:, cols]).then_inc(rden_done, 1)

                    def attend(q, s, half, first=False):
                        n = ig * NQ + q
                        if not first:
                            dve.wait_ge(den_done, n)
                        for kt in range(TT):
                            sums(kt, n, s)
                            if kt and kt % 2 == 0 and kt // 2 <= DEN_PARTS and not first:
                                invert(q - 1, kt // 2 - 1)
                        keep_out(q, s, half)

                    dve.wait_ge(o1_stored, (ig + 1) * (16 * NLC) + 1)
                    attend(0, 0, 0, first=True)
                    with dve.Fori(0, NQ // 2 - 1) as i:
                        attend(i * 2 + 1, 1, i)
                        attend(i * 2 + 2, 0, i + 1)
                    attend(NQ - 1, 1, NQ // 2 - 1)
                    for part in range(DEN_PARTS):
                        invert(NQ - 1, part)

                for a in range(2):
                    dve.wait_ge(wop_hi_done, b * 2 + a + 1 + 1)
                    v_.tensor_tensor(wop_lo[:, a], wop_raw[:, a], f32(wop_hi[:, a]), ALU.subtract).then_inc(wop_done, 1)
                with dve.Fori(0, NF // 2) as i:
                    for s in range(2):
                        f = i * 2 + s
                        n = b * NF + f
                        link = linker(f_dve, n * F_STEPS)

                        def split_o(j):
                            dve.wait_ge(oT_hi_done, n * FT + (j + 1) + 1)
                            v_.tensor_tensor(oT_lo[:, :, j * P:(j + 1) * P], flat[j % 2].rearrange("p (k n) -> p k n", k=KC),
                                             f32(oT_hi[:, :, j * P:(j + 1) * P]), ALU.subtract).then_inc(oT_done, 1)

                        def add_y(j):
                            dve.wait_ge(yz_done, n * FT + (j + 1) + FT + 1)
                            steps = link(v_.tensor_tensor(y[s][:, j, :], flat[4 + j % 2], y[s][:, j, :], ALU.add))
                            v_.scalar_tensor_tensor(y[s][:, j, :], flat[6 + j % 2], gain[:, j:j + 1], y[s][:, j, :],
                                                    ALU.mult, ALU.add).then_inc(y_done, 1)
                            return steps

                        split_o(0)
                        split_o(1)
                        normalise(b + 1, f, s, i)
                        split_o(2)
                        dve.wait_ge(gate_done, n + 1 + 1)
                        link(v_.tensor_tensor(lg[:], flat[2][:, 0:FT * NGATE].rearrange("p (t n) -> p t n", t=FT)[:, :, 0:NR + NS],
                                              bg[:].unsqueeze(1).broadcast_to([P, FT, NR + NS]), ALU.add))
                        settle(dve)
                        for j in range(FT):
                            ins = v_.max(top8[:, j, :], lg[:, j, 0:NR])
                        link(ins)
                        link(v_.tensor_reduce(smax[:], lg[:, :, NR:NR + NS], AX.X, ALU.max))
                        v_.tensor_tensor(z[:, :, 0:NR], lg[:, :, 0:NR], top8[:, :, 0:1].broadcast_to([P, FT, NR]), ALU.subtract)
                        v_.tensor_tensor(z[:, :, NR:NR + NS], lg[:, :, NR:NR + NS], smax[:].broadcast_to([P, FT, NS]), ALU.subtract)
                        v_.tensor_tensor(z[:, :, NR + NS:NZ], top8[:, :, 0:TOP], top8[:, :, 0:1].broadcast_to([P, FT, TOP]),
                                         ALU.subtract).then_inc(gate_z, 1)
                        dve.wait_ge(gate_exp, n + 1 + 1)
                        v_.tensor_reduce(zsum[:, :, 0], z[:, :, 0:NR], AX.X, ALU.add)
                        v_.tensor_reduce(zsum[:, :, 1], z[:, :, NR:NR + NS], AX.X, ALU.add)
                        link(v_.tensor_reduce(zsum[:, :, 2], z[:, :, NR + NS:NZ], AX.X, ALU.add))
                        link(v_.reciprocal(zrec[:], zsum[:, :, 0:2]))
                        link(v_.tensor_tensor(share[:, :, 0:NS], z[:, :, NR:NR + NS], zrec[:, :, 1:2].broadcast_to([P, FT, NS]),
                                              ALU.mult))
                        v_.tensor_tensor(share[:, :, 2], share[:, :, 0], share[:, :, 1], ALU.add)
                        link(v_.tensor_tensor(share[:, :, 3], zsum[:, :, 2], zrec[:, :, 0], ALU.mult))
                        link(v_.tensor_tensor(share[:, :, 2], share[:, :, 2], share[:, :, 0], ALU.mult))
                        link(v_.scalar_tensor_tensor(share[:, :, 3], share[:, :, 3], 2.0 * TOP, share[:, :, 1], ALU.mult, ALU.mult))
                        v_.scalar_tensor_tensor(gain[:], share[:, :, 2], 2.0, share[:, :, 3], ALU.mult, ALU.add
                                                ).then_inc(gain_ready, 1)
                        dve.wait_ge(gain_ready, n + 1 + 1)
                        dve.wait_ge(y_biased, n + 1 + 1)
                        add_y(0)
                        split_o(3)
                        for j in range(1, FT):
                            steps = add_y(j)
                        assert steps == F_STEPS
                        sum_x(b + 1, f)


def kernel(**inputs):
    import numpy as np
    import concourse.bacc as bacc
    from concourse import mybir as mb
    from concourse.bass_utils import run_bass_kernel_spmd

    a = {k: np.asarray(v) for k, v in inputs.items()}
    six = [a["L0_ffn_Wq"].T, a["L0_ffn_Wk"].T, a["L0_ffn_Wv"].T, a["L0_attn_wq"], a["L0_attn_wk"], a["L0_attn_wv"]]

    def rows(w):
        return w.reshape(KC, P, -1).transpose(1, 0, 2)

    arrays = {
        "x": a["L0_attn_x"],
        "w6": np.stack([rows(np.concatenate([w[:, g * P:(g + 1) * P] for w in six], axis=1)) for g in range(NG)]),
        "wop": np.stack([rows(a["L0_attn_wo"]), rows(a["L0_ffn_Wp"].T)], axis=1),
        "wg": rows(np.concatenate([a["L0_ffn_Wr"], a["L0_ffn_Ws"]], axis=0).T),
        "bqkv": np.stack([np.concatenate([a[n][g * P:(g + 1) * P] for n in ("L0_ffn_bq", "L0_ffn_bk", "L0_ffn_bv")])
                          for g in range(NG)]),
        "bp": a["L0_ffn_bp"],
        "bg": np.concatenate([a["L0_ffn_br"], a["L0_ffn_bs"]]),
        "temp": a["L0_ffn_temperature"].reshape(-1),
        "qe": a["L0_ffn_query_embedding"].reshape(-1),
    }
    arrays = {f"in_{k}": np.ascontiguousarray(v) for k, v in arrays.items()}
    nc = bacc.Bacc("TRN2", target_bir_lowering=False, num_devices=1)
    args = [nc.dram_tensor(k, v.shape, mb.dt.from_np(v.dtype), kind="ExternalInput").ap() for k, v in arrays.items()]
    args.append(nc.dram_tensor("out", (B, S, D), mb.dt.float32, kind="ExternalOutput").ap())
    build(nc, *args)
    r = run_bass_kernel_spmd(nc, [arrays], core_ids=[0])
    return r.results[0]["out"]
```

```python
from contextlib import ExitStack

import concourse.bass as bass
from concourse import mybir

F32 = mybir.dt.float32
F32R = mybir.dt.float32r
I32 = mybir.dt.int32
ALU = mybir.AluOpType
ACT = mybir.ActivationFunctionType
AX = mybir.AxisListType

P = 128
B, S, D, H, HD = 4, 2048, 512, 16, 32
HG = P // HD
NG = H // HG
KC = D // P
TT = S // P
CH = 2
NCH = TT // CH
CT = CH * P
LC = 4
NLC = TT // LC
QN = 512
NQ = S // QN
FT = 4
NF = TT // FT
W6 = 6 * P
NR, NS = 15, 2
NGATE = NR + NS + 1
TOP = 3
DVE_SUMS = TT + TT // 2 + 1
POOL_SUMS = TT // 2 - 1
ROUNDED = (0, 0, 0, 1, 1, 1, 1, 4)
SPLIT = (2, 1, 1, 1, 1, 1, 1, 0)
assert sum(ROUNDED) == sum(SPLIT) == 2 * KC and len(ROUNDED) == len(SPLIT) == POOL_SUMS + 1
TOTAL_AT = 1
DEN_PARTS = 4
VW = HD + 1
LN_EPS, ATT_EPS = 1e-5, 1e-6
SHIFT = 65.0
BOUND2 = (2 * SHIFT) ** 2


def f32(ap):
    return ap.bitcast(F32)


def build(nc, x_d, w6_d, wop_d, wg_d, bqkv_d, bp_d, bg_d, temp_d, qe_d, out_d):
    o1_d = nc.dram_tensor("o1_scratch", [B, S, D], F32, kind="Internal").ap()
    hT_d = nc.dram_tensor("hT_scratch", [B, D, S], F32, kind="Internal").ap()

    with ExitStack() as ctx:
        def sem(name):
            return ctx.enter_context(nc.semaphore(name))

        counted = []

        def counter(name, ahead=0):
            counted.append((sem(name), 1 + ahead))
            return counted[-1][0]

        KB = 1024
        cursor = [17 * KB]

        def at(name, shape, dt, off):
            return nc.alloc_sbuf_tensor_at(name, shape, dt, offset=off)

        def sb(name, shape, dt):
            n = 4
            for d in shape[1:]:
                n *= d
            off = cursor[0]
            cursor[0] += (n + 31) // 32 * 32
            return at(name, shape, dt, off)

        xT = sb("xT", [P, KC, S], F32)
        kaug = sb("kaug", [P, HG, S], F32R)
        qaug = sb("qaug", [P, HG, S], F32R)
        w_hi = sb("w_hi", [P, KC, W6], F32R)
        w_lo = sb("w_lo", [P, KC, W6], F32R)
        v = sb("v", [P, TT, P], F32)
        sq = sb("sq", [P, CH, P], F32)
        state = sb("state", [P, 2 * CH, HG, VW], F32)
        ident = sb("ident", [P, P], F32)
        ident_r = sb("ident_r", [P, P], F32R)
        causal = sb("causal", [P, P], F32)
        headmask = sb("headmask", [P, HG], F32)
        ones32 = sb("ones32", [P, HD], F32)
        minus_half = sb("minus_half", [P, CH, HG], F32)
        neg_shift = sb("neg_shift", [P, 1], F32)
        bias_g = sb("bias_g", [P, 3 * P], F32)
        kmean_b = sb("kmean_b", [P, P], F32)
        bp = sb("bp", [P, D], F32)
        bg = sb("bg", [P, NR + NS], F32)
        et = sb("et", [P, H, HD], F32)
        et_g = sb("et_g", [P, P], F32)
        temp = sb("temp", [P, H], F32)
        tnt = sb("tnt", [P, H], F32)
        tsc = sb("tsc", [P, H], F32)
        tsc_g = sb("tsc_g", [P, HG], F32)
        tb = sb("tb", [P, H], F32)
        tb_g = sb("tb_g", [P, HG], F32)
        xpart = sb("xpart", [P, KC, TT // LC], F32)
        xmean = sb("xmean", [P, KC], F32)
        xbar = sb("xbar", [P, KC, P], F32R)
        stats = sb("stats", [P, LC, 6], F32)
        mv = sb("mv", [P, LC, 2], F32)
        rstd = sb("rstd", [P, LC], F32)
        ss = sb("ss", [P, CH, HG], F32)
        rn = sb("rn", [P, CH, HG], F32)
        rnt = sb("rnt", [P, CH, HG], F32)
        kss = sb("kss", [P, CH, HG], F32)
        kmax = sb("kmax", [P, CH, HG], F32)
        kmax2 = sb("kmax2", [P, HG], F32)
        bound = sb("bound", [P, 1], F32)
        bound1 = sb("bound1", [1, 1], F32)
        flag = sb("flag", [1, 1], I32)
        rowmax = sb("rowmax", [P, 1], F32)
        dn = sb("dn", [P, 2, HG], F32)
        rdn = sb("rdn", [P, 2, HG], F32)
        wg_raw = sb("wg_raw", [P, KC, NGATE], F32)
        wg_hi = sb("wg_hi", [P, KC, NGATE], F32R)
        wg_lo = sb("wg_lo", [P, KC, NGATE], F32R)
        NZ = NR + NS + TOP
        rden = sb("rden", [P, QN], F32)
        lgT = rden[0:NGATE, :]
        lg = sb("lg", [P, FT, NR + NS], F32)
        top8 = sb("top8", [P, FT, 8], F32)
        smax = sb("smax", [P, FT, 1], F32)
        z = sb("z", [P, FT, NZ], F32)
        zsum = sb("zsum", [P, FT, 3], F32)
        zrec = sb("zrec", [P, FT, 2], F32)
        share = sb("share", [P, FT, 4], F32)
        gain = sb("gain", [P, FT], F32)
        r1 = cursor[0]
        xs_hi = [at(f"xs_hi{s}", [P, KC, CT], F32R, r1 + s * 4 * KB) for s in range(2)]
        xs_lo = [at(f"xs_lo{s}", [P, KC, CT], F32R, r1 + (8 + s * 4) * KB) for s in range(2)]
        q_cat = at("q_cat", [P, CH, HG, P], F32R, r1 + 16 * KB)
        k_cat = at("k_cat", [P, CH, HG, P], F32R, r1 + 20 * KB)
        xs0_hi = at("xs0_hi", [P, KC, P], F32R, r1 + 24 * KB)
        xs0_lo = at("xs0_lo", [P, KC, P], F32R, r1 + 26 * KB)
        qh = at("qh", [P, CH, P], F32, r1 + 28 * KB)
        ksq = at("ksq", [P, CH, P], F32, r1 + 31 * KB)
        o1 = at("o1", [P, LC, P], F32, r1 + 29 * KB)
        hT_out = [at(f"hT_out{s}", [P, QN], F32, r1 + (32 + 2 * s) * KB) for s in range(2)]
        r1_end = r1 + 36 * KB
        w_raw = at("w_raw", [P, KC, W6], F32, r1)
        hT_in = at("hT_in", [P, KC, FT * P], F32, r1)
        o1_in = at("o1_in", [P, FT, D], F32, r1 + 12 * KB)
        x_in = [at(f"x_in{s}", [P, LC, D], F32, r1 + (28 - s * 8) * KB) for s in range(2)]
        scan_q = at("scan_q", [P, P], F32R, r1)
        scan_m = at("scan_m", [P, P], F32, r1 + KB)
        r2 = (r1_end + 31) // 32 * 32
        lin = [at(f"lin{s}", [P, CH, 3 * P], F32, r2 + s * 3 * KB) for s in range(2)]
        ex = at("ex", [P, CH, 2 * P], F32, r2 + 6 * KB)
        phi = [at(f"phi{s}", [P, CH, 2 * P], F32, r2 + (8 + s * 2) * KB) for s in range(2)]
        qkT = at("qkT", [P, CH, 2, P], F32, r2 + 12 * KB)
        qbd = at("qbd", [P, CH, HG, P], F32, r2 + 14 * KB)
        am = at("am", [P, CH, HG, P], F32, r1 + 32 * KB)
        VB = CH * HG * VW * 4
        v1 = [at(f"v1{s}", [P, CH, HG, VW], F32, r2 + 18 * KB + s * VB) for s in range(2)]
        kvm = at("kvm", [P, CH, HG, VW], F32, r2 + 18 * KB + 2 * VB)
        qk = at("qk", [P, 2, CH, P], F32, r2 + 22 * KB)
        assert 18 * KB + 3 * VB <= 22 * KB
        prob = [[at(f"prob{t}{p}", [P, 2, QN], F32, r2 + (t * 2 + p) * 4 * KB) for p in range(2)] for t in range(2)]
        acc = [[at(f"acc{s}{p}", [P, 2, QN], F32, (r2 + 16 * KB, r1 + 12 * KB)[s] + p * 4 * KB) for p in range(2)]
               for s in range(2)]
        acc_pool = [at(f"acc_pool{s}", [P, 2, QN], F32, r1 + (28 - 8 * s) * KB) for s in range(2)]
        hT_hi1 = at("hT_hi1", [P, KC, FT * P], F32R, r2)
        hT_lo1 = at("hT_lo1", [P, KC, FT * P], F32R, r2 + 8 * KB)
        y = [at("y0", [P, FT, D], F32, r2 + 16 * KB), v[:].rearrange("p t (a n) -> p t a n", a=1).rearrange(
            "p (j r) a n -> p j (r a n)", j=FT)]
        assert r2 + 24 * KB <= nc.sbuf_usable_end, (r2 + 24 * KB, nc.sbuf_usable_end)
        wop_raw = xT[:, 0:2, :].rearrange("p a (k n) -> p a k n", k=KC)
        wop_hi = kaug[:, 0:2, :].rearrange("p a (k n) -> p a k n", k=KC)
        wop_lo = kaug[:, 2:4, :].rearrange("p a (k n) -> p a k n", k=KC)
        hT_hi = [qaug[:, 0, :].rearrange("p (k n) -> p k n", k=KC), hT_hi1[:]]
        hT_lo = [qaug[:, 1, :].rearrange("p (k n) -> p k n", k=KC), hT_lo1[:]]
        oT_hi = qaug[:, 2, :].rearrange("p (k n) -> p k n", k=KC)
        oT_lo = qaug[:, 3, :].rearrange("p (k n) -> p k n", k=KC)

        low = ctx.enter_context(nc.psum_tensor("low", [P, 4, 512], F32))
        high = ctx.enter_context(nc.psum_tensor("high", [P, 4, 512], F32))
        flat = [t[:, i, :] for t in (low, high) for i in range(4)]
        places = [low[:, 0:2, :], low[:, 2:4, :], high[:, 0:2, :]]
        out_bank, den_bank = flat[6], flat[7]

        const_in = sem("const_in")
        settled = sem("settled")
        pool_const = sem("pool_const")
        dve_const = counter("dve_const")
        act_const = sem("act_const")
        x_loaded = [counter(f"x_loaded{s}") for s in range(2)]
        ln_stats, ln_rstd, ln_dve, ln_done = counter("ln_stats"), counter("ln_rstd"), counter("ln_dve"), counter("ln_done")
        xT_turned, xT_kept = counter("xT_turned", LC), counter("xT_kept")
        xpart_done, xbar_ready = counter("xpart_done"), counter("xbar_ready")
        w_loaded, w_split, w_hi_done = counter("w_loaded"), counter("w_split"), counter("w_hi_done")
        xs_hi_done, xs_done = counter("xs_hi_done"), counter("xs_done")
        xs0_hi_done, xs0_done = counter("xs0_hi_done"), counter("xs0_done")
        proj_done, projA_kept, projB_kept = counter("proj_done"), counter("projA_kept"), counter("projB_kept")
        qk_kept = counter("qk_kept")
        ss_ready, rn_ready, qh_ready = counter("ss_ready"), counter("rn_ready"), counter("qh_ready")
        cat_hi, k_cat_done, q_cat_done = counter("cat_hi"), counter("k_cat_done"), counter("q_cat_done")
        k_turned, q_turned, k_kept, q_kept = counter("k_turned"), counter("q_turned"), counter("k_kept"), counter("q_kept")
        g_dve, g_set = counter("g_dve"), counter("g_set")
        kmean_done, bias_ready = counter("kmean_done"), counter("bias_ready")
        bound_ready, bound_turned, flag_ready = counter("bound_ready"), counter("bound_turned"), counter("flag_ready")
        scan_staged, scan_scored, scan_max, scan_turned, scan_row = (
            counter("scan_staged"), counter("scan_scored"), counter("scan_max"), counter("scan_turned"), counter("scan_row"))
        bound_dve, scan_reduced = counter("bound_dve"), counter("scan_reduced")
        neg_part, exp_part, phi_ready, v1_ready = counter("neg_part"), counter("exp_part"), counter("phi_ready"), counter("v1_ready")
        phi_turned, qkT_kept, kv_done, qbd_ready = counter("phi_turned"), counter("qkT_kept"), counter("kv_done"), counter("qbd_ready")
        at_done, am_ready, state_ready, num_done = counter("at_done"), counter("am_ready"), counter("state_ready"), counter("num_done")
        states_dve, outputs_dve, o1_ready, o1_stored = counter("states_dve"), counter("outputs_dve"), counter("o1_ready"), counter("o1_stored")
        scored, exped, weighted = counter("scored"), counter("exped"), counter("weighted")
        summed, pool_summed = counter("summed"), counter("pool_summed")
        out_kept, den_done, rden_done, h_done = counter("out_kept"), counter("den_done"), counter("rden_done"), counter("h_done")
        hT_stored = [counter(f"hT_stored{s}") for s in range(2)]
        wop_loaded, wop_hi_done, wop_done = counter("wop_loaded"), counter("wop_hi_done"), counter("wop_done")
        hT_loaded, o1_loaded = counter("hT_loaded"), counter("o1_loaded")
        xr_loaded = [counter(f"xr_loaded{s}") for s in range(2)]
        hT_hi_done, hT_done = counter("hT_hi_done"), counter("hT_done")
        o1_turned, oT_hi_done, oT_done = counter("o1_turned"), counter("oT_hi_done"), counter("oT_done")
        gateT_done, gateT_kept = counter("gateT_done"), counter("gateT_kept")
        gate_done, gate_z, gate_exp, gain_ready = counter("gate_done"), counter("gate_z"), counter("gate_exp"), counter("gain_ready")
        f_dve, yz_done, y_done = counter("f_dve"), counter("yz_done", FT), counter("y_done")
        y_biased = counter("y_biased")
        y_stored = [counter(f"y_stored{s}") for s in range(2)]

        NCONST = 5
        POOL_CONST = 8
        DVE_CONST = 16
        L_STEPS, SET_STEPS, G_STEPS, BOUND_STEPS, C_STEPS, F_STEPS = 2, 5, 6, 3, 2, 13

        dve_order = [(kt, p) for kt in range(TT) for p in range(2) if p == 0 or kt % 2 or kt == 0]
        DVE_AT = {kp: i + 1 for i, kp in enumerate(dve_order)}
        assert len(dve_order) == DVE_SUMS

        UNITS = 2 * TT

        def place(q, u):
            return (q * UNITS + u) % 3

        def settle(eng):
            eng.sem_inc(settled, 1)

        block = ctx.enter_context(nc.Block())

        @block.sync
        def _(sp):
            for dst, src in (
                (bp[:], bp_d.partition_broadcast(P)),
                (bg[:], bg_d.partition_broadcast(P)),
                (temp[:], temp_d.partition_broadcast(P)),
                (et[:].rearrange("p h e -> p (h e)"), qe_d.partition_broadcast(P)),
                (wg_raw[:, :, 0:NR + NS], wg_d),
            ):
                sp.dma_start(dst, src).then_inc(const_in, 16)

            for started, n in counted:
                sp.sem_inc(started, n)

            def load_x(lb, batch, t, s):
                sp.wait_ge(xT_turned, (lb * NF + t - 1) * LC + LC + 1)
                sp.dma_start(x_in[s][:], x_d[batch, bass.ds(t * (LC * P), LC * P), :].rearrange(
                    "o (t p) d -> p (o t) d", p=P)).then_inc(x_loaded[s], 16)

            for s in range(2):
                load_x(0, slice(0, 1), s, s)
            sp.dma_start(w_raw[:], w6_d[0]).then_inc(w_loaded, 16)
            sp.dma_start(bias_g[:], bqkv_d[0].partition_broadcast(P)).then_inc(w_loaded, 16)
            with sp.Fori(1, NF // 2) as i:
                for s in range(2):
                    load_x(0, slice(0, 1), i * 2 + s, s)

            with sp.Fori(0, B) as b:
                def load_o(f):
                    sp.dma_start(o1_in[:], o1_d[bass.ds(b, 1), bass.ds(f * (FT * P), FT * P), :].rearrange(
                        "o (t p) d -> p (o t) d", p=P)).then_inc(o1_loaded, 16)

                def load_h(f):
                    sp.dma_start(hT_in[:], hT_d[bass.ds(b, 1), :, bass.ds(f * (FT * P), FT * P)].rearrange(
                        "o (k p) n -> p (o k) n", p=P)).then_inc(hT_loaded, 16)

                with sp.Fori(0, NG) as g:
                    ig = b * NG + g
                    with sp.Fori(0, NLC) as c:
                        m = ig * NLC + c
                        sp.wait_ge(o1_ready, (m + 1) * (LC // CH) + 1)
                        sp.dma_start(
                            o1_d[bass.ds(b, 1), bass.ds(c * (LC * P), LC * P), bass.ds(g * P, P)].rearrange(
                                "o (t p) d -> p (o t) d", p=P), o1[:]).then_inc(o1_stored, 16)
                    sp.wait_ge(num_done, ig * TT + TT + 1)
                    sp.wait_ge(o1_stored, (ig + 1) * (16 * NLC) + 1)
                    sp.wait_ge(scored, ig * (NQ * UNITS) + 1 + 1)
                    sp.dma_start(w_raw[:], w6_d[bass.ds((g + 1) % NG, 1)].rearrange("o p k n -> p (o k) n")).then_inc(
                        w_loaded, 16)
                    sp.dma_start(bias_g[:], bqkv_d[bass.ds((g + 1) % NG, 1), :].rearrange(
                        "o n -> (o n)").partition_broadcast(P)).then_inc(w_loaded, 16)
                    def store_h(q):
                        s = q % 2
                        sp.wait_ge(h_done, ig * NQ + q + 1 + 1)
                        sp.dma_start(hT_d[bass.ds(b, 1), bass.ds(g * P, P), q * QN:(q + 1) * QN].rearrange(
                            "o p n -> (o p) n"), hT_out[s][:]).then_inc(hT_stored[s], 16)

                    with sp.If((g + 1) % NG):
                        settle(sp)
                    with sp.Else():
                        sp.dma_start(wop_raw, wop_d).then_inc(wop_loaded, 16)
                    for q in range(NQ - 1):
                        store_h(q)
                    with sp.If((g + 1) % NG):
                        settle(sp)
                    with sp.Else():
                        sp.wait_ge(w_split, (b + 1) * NG + 1 + 1)
                        sp.wait_ge(hT_stored[0], (b + 1) * (16 * NG * NQ // 2) + 1)
                        settle(sp)
                        load_h(0)
                        sp.wait_ge(den_done, (b + 1) * (NG * NQ) + 1)
                        load_o(0)
                    store_h(NQ - 1)

                def load(f, s, half, first=False):
                    n = b * NF + f
                    if not first:
                        sp.wait_ge(hT_done, n + 1)
                        settle(sp)
                        load_h(f)
                        sp.wait_ge(o1_turned, n * FT + 1)
                        load_o(f)
                    sp.wait_ge(hT_stored[1], (b + 1) * (16 * NG * NQ // 2) + 1)
                    load_x(b + 1, bass.ds((b + 1) % B, 1), f, s)
                    sp.wait_ge(y_stored[s], (b * (NF // 2) + half) * 16 + 1)
                    sp.dma_start(y[s][:], x_d[bass.ds(b, 1), bass.ds(f * (FT * P), FT * P), :].rearrange(
                        "o (t p) d -> p (o t) d", p=P)).then_inc(xr_loaded[s], 16)

                def store(f, s):
                    sp.wait_ge(y_done, (b * NF + f) * FT + FT + 1)
                    sp.dma_start(out_d[bass.ds(b, 1), bass.ds(f * (FT * P), FT * P), :].rearrange(
                        "o (t p) d -> p (o t) d", p=P), y[s][:]).then_inc(y_stored[s], 16)

                load(0, 0, 0, first=True)
                with sp.Fori(0, NF // 2 - 1) as i:
                    load(i * 2 + 1, 1, i)
                    store(i * 2, 0)
                    load(i * 2 + 2, 0, i + 1)
                    store(i * 2 + 1, 1)
                load(NF - 1, 1, NF // 2 - 1)
                store(NF - 2, 0)
                store(NF - 1, 1)
            for s in range(2):
                sp.wait_ge(y_stored[s], 16 * B * NF // 2 + 1)
                sp.wait_ge(x_loaded[s], 16 * (B + 1) * NF // 2 + 1)
                sp.wait_ge(hT_stored[s], 16 * B * NG * NQ // 2 + 1)
            sp.wait_ge(o1_stored, 16 * B * NG * NLC + 1)
            sp.wait_ge(w_loaded, 32 * (B * NG + 1) + 1)

        @block.gpsimd
        def _(pool):
            g = nc.gpsimd
            g.memset(ident[:], 0.0).then_inc(pool_const, 1)
            g.memset(causal[:], 1.0).then_inc(pool_const, 1)
            g.memset(headmask[:], 1.0).then_inc(pool_const, 1)
            g.memset(minus_half[:], -0.5).then_inc(pool_const, 1)
            pool.wait_ge(pool_const, 4)
            g.affine_select(out=ident[:], in_=ident[:], compare_op=ALU.not_equal, fill=1.0, base=0,
                            pattern=[[-1, P]], channel_multiplier=1).then_inc(pool_const, 1)
            g.affine_select(out=causal[:], in_=causal[:], compare_op=ALU.is_ge, fill=0.0, base=0,
                            pattern=[[1, P]], channel_multiplier=-1).then_inc(pool_const, 1)
            g.affine_select(out=headmask[:], in_=headmask[:], compare_op=ALU.is_ge, fill=0.0, base=0,
                            pattern=[[-HD, HG]], channel_multiplier=1).then_inc(pool_const, 1)
            pool.wait_ge(pool_const, 7)
            g.affine_select(out=headmask[:], in_=headmask[:], compare_op=ALU.is_ge, fill=0.0, base=HD - 1,
                            pattern=[[HD, HG]], channel_multiplier=-1).then_inc(pool_const, 1)

            HW6 = W6 // 2

            def round_weights(n, i):
                if i == 0:
                    pool.wait_ge(w_loaded, n * 32 + 32 + 1)
                    settle(pool)
                r = slice(i % 2 * HW6, (i % 2 + 1) * HW6)
                g.tensor_copy(w_hi[:, i // 2, r], w_raw[:, i // 2, r]).then_inc(w_hi_done, 1)

            def rest_of_weights(n, i):
                r = slice(i % 2 * HW6, (i % 2 + 1) * HW6)
                pool.wait_ge(w_hi_done, (n + 1) * (2 * KC) + 1)
                ins = g.tensor_tensor(w_lo[:, i // 2, r], w_raw[:, i // 2, r], f32(w_hi[:, i // 2, r]), ALU.subtract)
                if i == 2 * KC - 1:
                    ins.then_inc(w_split, 1)

            def rstd_of(lb, t):
                pool.wait_ge(ln_stats, lb * NF + t + 1 + 1)
                g.tensor_tensor(rstd[:], rstd[:], minus_half[:].rearrange("p a b -> p (a b)")[:, 0:LC],
                                ALU.pow).then_inc(ln_rstd, 1)

            for t in range(NF):
                rstd_of(0, t)
                if t == 1:
                    for i in range(2 * KC):
                        rest_of_weights(0, i)
            with pool.Fori(0, B) as b:
                with pool.Fori(0, NG) as gr:
                    ig = b * NG + gr
                    with pool.Fori(0, NCH) as c:
                        n = ig * NCH + c
                        pool.wait_ge(ss_ready, n + 1 + 1)
                        g.tensor_tensor(rn[:], ss[:], minus_half[:], ALU.pow).then_inc(rn_ready, 1)

                    def scale(q):
                        pool.wait_ge(rden_done, (ig * NQ + q) * DEN_PARTS + DEN_PARTS + 1)
                        g.tensor_tensor(hT_out[q % 2][:], hT_out[q % 2][:], rden[:], ALU.mult).then_inc(h_done, 1)

                    def sums(q, split=None, pieces=(0,) * (POOL_SUMS + 1)):
                        def split_after(m):
                            for piece in range(sum(pieces[:m]), sum(pieces[:m + 1])):
                                split(ig + 1, piece)

                        n, s = ig * NQ + q, q % 2
                        split_after(0)
                        pool.wait_ge(summed, n * DVE_SUMS + DVE_AT[0, 1] + 1)
                        for m in range(1, POOL_SUMS + 1):
                            pool.wait_ge(exped, n * UNITS + (4 * m + 2) + 1)
                            if m > 1:
                                pool.wait_ge(pool_summed, n * POOL_SUMS + (m - 1) + 1)
                            g.tensor_tensor(acc_pool[s][:], acc_pool[s][:], prob[0][1][:], ALU.add
                                            ).then_inc(pool_summed, 1)
                            split_after(m)
                            if m == 4 and q:
                                scale(q - 1)

                    sums(0, split=round_weights, pieces=ROUNDED)
                    for q in range(1, NQ - 1):
                        sums(q)
                    sums(NQ - 1, split=rest_of_weights, pieces=SPLIT)
                    scale(NQ - 1)

                with pool.Fori(0, NF // 2) as i:
                    for s in range(2):
                        f = i * 2 + s
                        n = b * NF + f
                        pool.wait_ge(hT_hi_done, n + 1 + 1)
                        g.tensor_tensor(hT_lo[s], hT_in[:], f32(hT_hi[s]), ALU.subtract).then_inc(hT_done, 1)
                        rstd_of(b + 1, f)
                        pool.wait_ge(xr_loaded[s], (b * (NF // 2) + i) * 16 + 16 + 1)
                        g.tensor_tensor(y[s][:], y[s][:], bp[:].unsqueeze(1).broadcast_to([P, FT, D]), ALU.add
                                        ).then_inc(y_biased, 1)

        @block.scalar
        def _(act):
            s_ = nc.scalar
            act.wait_ge(dve_const, 2 + 1)
            s_.activation(tnt[:], tnt[:], ACT.Exp).then_inc(act_const, 1)
            act.wait_ge(dve_const, 3 + 1)
            s_.activation(tnt[:], tnt[:], ACT.Ln).then_inc(act_const, 1)
            act.wait_ge(dve_const, DVE_CONST + 1)

            def keep_x(lb, t, j, bank=3):
                n = (lb * NF + t) * LC + j
                act.wait_ge(xT_turned, n + 1 + LC + 1)
                settle(act)
                s_.activation(xT[:, :, bass.ds(t * (LC * P) + j * P, P)], flat[bank].rearrange("p (k n) -> p k n", k=KC),
                              ACT.Copy).then_inc(xT_kept, 1)

            act.wait_ge(w_loaded, 32 + 1)
            s_.activation(w_hi[:], w_raw[:], ACT.Copy).then_inc(w_hi_done, 2 * KC)
            with act.Fori(0, NF) as t:
                for j in range(LC):
                    keep_x(0, t, j, 3 - j % 2)

            with act.Fori(0, B) as b:
                act.wait_ge(xT_kept, (b + 1) * TT + 1)
                settle(act)
                s_.activation(xs0_hi[:], xT[:, :, 0:P], ACT.Copy).then_inc(xs0_hi_done, 1)
                with act.Fori(0, NG) as g:
                    ig = b * NG + g

                    def part_x(c, s, tile0=0):
                        s_.activation(xs_hi[s][:, :, tile0 * P:CT], xT[:, :, bass.ds(c * CT + tile0 * P, CT - tile0 * P)],
                                      ACT.Copy).then_inc(xs_hi_done, 1)

                    def keep_lin(c, s, j):
                        act.wait_ge(proj_done, (ig * NCH + c) * CH + (j + 1) + 1)
                        s_.activation(lin[s][:, j, :], flat[2 * j + 1][:, 0:3 * P], ACT.Copy).then_inc(projB_kept, 1)

                    def stack_k(c):
                        n = ig * NCH + c
                        act.wait_ge(qk_kept, n + 1 + 1)
                        act.wait_ge(k_turned, n * CH + 1)
                        s_.activation(k_cat[:, :, :, 0:2 * HD].rearrange("p c h (r e) -> p (c h) r e", r=2),
                                      qk[:, 1].rearrange("p c (h e) -> p (c h) e", h=HG).unsqueeze(2)
                                      .broadcast_to([P, CH * HG, 2, HD]), ACT.Copy).then_inc(cat_hi, 1)

                    def stack_q(c):
                        n = ig * NCH + c
                        act.wait_ge(qh_ready, n + 1 + 1)
                        act.wait_ge(q_turned, n * CH + 1)
                        s_.activation(q_cat[:, :, :, 0:4 * HD].rearrange("p c h (r e) -> p (c h) r e", r=4)[:, :, 0:3:2],
                                      qh[:].rearrange("p c (h e) -> p (c h) e", h=HG).unsqueeze(2)
                                      .broadcast_to([P, CH * HG, 2, HD]), ACT.Copy).then_inc(cat_hi, 1)

                    def keep_q(c, j, bank=5):
                        act.wait_ge(q_turned, (ig * NCH + c) * CH + (j + 1) + 1)
                        settle(act)
                        s_.activation(qaug[:, :, bass.ds(c * CT + j * P, P)], flat[bank].rearrange("p (h n) -> p h n", h=HG),
                                      ACT.Copy).then_inc(q_kept, 1)

                    def keep_last_k(c, j, bank):
                        act.wait_ge(k_turned, (ig * NCH + c) * CH + (j + 1) + 1)
                        settle(act)
                        s_.activation(kaug[:, :, bass.ds(c * CT + j * P, P)], flat[bank].rearrange("p (h n) -> p h n", h=HG),
                                      ACT.Copy).then_inc(k_kept, 1)

                    def exp_part_of(c):
                        act.wait_ge(neg_part, ig * NCH + c + 1 + 1)
                        s_.activation(ex[:], ex[:], ACT.Exp).then_inc(exp_part, 1)

                    def keep_v(c, s):
                        s_.activation(v1[s][:, :, :, 0:HD], lin[s][:, :, 2 * P:3 * P].rearrange("p t (h e) -> p t h e", h=HG),
                                      ACT.Copy).then_inc(v1_ready, 1)

                    def keep_qkT(c):
                        act.wait_ge(phi_turned, ig * NCH + c + 1 + 1)
                        s_.activation(qkT[:].rearrange("p t a n -> p (t a n)"), flat[6], ACT.Copy).then_inc(qkT_kept, 1)

                    def step(c, s, last=True, ahead=True):
                        if last:
                            stack_k(c - 1)
                            stack_q(c - 1)
                        if ahead:
                            act.wait_ge(proj_done, (ig * NCH + c) * CH + 1)
                            settle(act)
                            part_x(c + 1, 1 - s)
                        keep_lin(c, s, 0)
                        if last:
                            keep_qkT(c - 1)
                            keep_q(c - 1, 0)
                        keep_lin(c, s, 1)
                        exp_part_of(c)
                        keep_v(c, s)
                        if last:
                            keep_q(c - 1, 1)

                    act.wait_ge(den_done, ig * NQ + 1)
                    act.wait_ge(w_split, ig + 1 + 1)
                    act.wait_ge(xbar_ready, b + 1 + 1)
                    act.wait_ge(y_stored[0], b * (16 * NF // 2) + 1)
                    part_x(0, 0, tile0=1)
                    step(0, 0, last=False)
                    with act.Fori(0, NCH // 2 - 1) as i:
                        step(i * 2 + 1, 1)
                        step(i * 2 + 2, 0)
                    step(NCH - 1, 1, ahead=False)
                    c = NCH - 1
                    stack_k(c)
                    stack_q(c)
                    keep_qkT(c)
                    keep_last_k(c, 0, bank=4)
                    keep_last_k(c, 1, bank=0)
                    keep_q(c, 0)
                    keep_q(c, 1, bank=1)

                    act.wait_ge(flag_ready, ig + 1 + 1)
                    settle(act)
                    wide = act.value_load(flag[0:1, 0:1], min_val=0, max_val=1)
                    with act.If(wide):
                        with act.Fori(0, HG * TT) as r:
                            act.wait_ge(scan_scored, ig * (HG * TT) + r + 1)
                            settle(act)
                            s_.activation(scan_q[:], f32(qaug[:].rearrange("p h n -> p (h n)")[:, bass.ds(r * P, P)]),
                                          ACT.Copy).then_inc(scan_staged, 1)
                    with act.Else():
                        act.sem_inc(scan_staged, HG * TT)

                    def exps(q):
                        n = ig * NQ + q
                        for kt in range(TT):
                            for p in range(2):
                                act.wait_ge(scored, n * UNITS + (2 * kt + p + 1) + 1)
                                back, n0 = (kt - 2, n) if kt >= 2 else (kt - 2 + TT, n - 1)
                                if kt >= 2 or q:
                                    if p == 0:
                                        act.wait_ge(weighted, n0 * TT + (back + 1) + 1)
                                    if p == 1 and back % 2 == 0 and back > 0:
                                        act.wait_ge(pool_summed, n0 * POOL_SUMS + back // 2 + 1)
                                    else:
                                        act.wait_ge(summed, n0 * DVE_SUMS + DVE_AT[back, p] + 1)
                                s_.activation(prob[kt % 2][p][:], places[place(q, 2 * kt + p)], ACT.Exp,
                                              bias=neg_shift[:, 0:1]).then_inc(exped, 1)

                    for q in range(NQ):
                        exps(q)

                act.wait_ge(wop_loaded, b * 16 + 16 + 1)
                for a in range(2):
                    s_.activation(wop_hi[:, a], wop_raw[:, a], ACT.Copy).then_inc(wop_hi_done, 1)
                with act.Fori(0, NF // 2) as i:
                    for s in range(2):
                        f = i * 2 + s
                        n = b * NF + f

                        def keep_o(j):
                            act.wait_ge(o1_turned, n * FT + (j + 1) + 1)
                            act.wait_ge(yz_done, (n - 1) * FT + (j + 1) + FT + 1)
                            s_.activation(oT_hi[:, :, j * P:(j + 1) * P], flat[j % 2].rearrange("p (k n) -> p k n", k=KC),
                                          ACT.Copy).then_inc(oT_hi_done, 1)

                        act.wait_ge(hT_loaded, n * 16 + 16 + 1)
                        act.wait_ge(yz_done, (n - 1) * FT + FT + 1)
                        s_.activation(hT_hi[s], hT_in[:], ACT.Copy).then_inc(hT_hi_done, 1)
                        keep_o(0)
                        keep_o(1)
                        act.wait_ge(gateT_done, n + 1 + 1)
                        s_.activation(lgT, flat[2][0:NGATE, :], ACT.Copy).then_inc(gateT_kept, 1)
                        keep_x(b + 1, f, 0)
                        keep_o(2)
                        act.wait_ge(gate_z, n + 1 + 1)
                        s_.activation(z[:], z[:], ACT.Exp).then_inc(gate_exp, 1)
                        keep_x(b + 1, f, 1)
                        keep_o(3)
                        keep_x(b + 1, f, 2)
                        keep_x(b + 1, f, 3)

        @block.tensor
        def _(pe):
            t_ = nc.tensor
            pe.wait_ge(pool_const, POOL_CONST)
            pe.wait_ge(dve_const, DVE_CONST + 1)

            def parts(out, hi, lo, whi, wlo, open_group=True):
                for k in range(KC):
                    t_.matmul(out, hi(k), whi(k), start=(k == 0 and open_group), stop=False)
                    t_.matmul(out, hi(k), wlo(k), start=False, stop=False)
                    last = t_.matmul(out, lo(k), whi(k), start=False, stop=(k == KC - 1))
                return last

            def turn_x(lb, t, s, j, bank=3):
                n = (lb * NF + t) * LC + j
                if j == 0:
                    pe.wait_ge(ln_done, lb * NF + t + 1 + 1)
                pe.wait_ge(xT_kept, n + 1 if j == 0 or bank == 3 else n)
                for k in range(KC):
                    last = t_.transpose(flat[bank][:, k * P:(k + 1) * P], x_in[s][:, j, k * P:(k + 1) * P], ident[:])
                last.then_inc(xT_turned, 1)

            with pe.Fori(0, NF // 2) as i:
                for s in range(2):
                    for j in range(LC):
                        turn_x(0, i * 2 + s, s, j, 3 - j % 2)

            with pe.Fori(0, B) as b:
                with pe.Fori(0, NG) as g:
                    ig = b * NG + g

                    pe.wait_ge(w_split, ig + 1 + 1)
                    pe.wait_ge(out_kept, ig * NQ + 1)
                    pe.wait_ge(xT_kept, (b + 1) * TT + 1)
                    pe.wait_ge(oT_done, b * TT + 1)

                    def project(c, s, j, pieces=range(KC), first=False):
                        n = ig * NCH + c
                        if first:
                            pe.wait_ge(xs0_done, b + 1 + 1)
                        else:
                            pe.wait_ge(xs_done, n + 1 + 1)
                        pe.wait_ge(projA_kept, n * CH + 1)
                        pe.wait_ge(projB_kept, n * CH + 1)
                        for k in pieces:
                            hi, lo = (x[:, k, :] for x in (xs0_hi, xs0_lo)) if first else (
                                x[:, k, j * P:(j + 1) * P] for x in (xs_hi[s], xs_lo[s]))
                            for x, w in ((hi, w_hi), (hi, w_lo), (lo, w_hi)):
                                for a in range(2):
                                    last = t_.matmul(flat[2 * j + a][:, 0:3 * P], x, w[:, k, a * 3 * P:(a + 1) * 3 * P],
                                                     start=(k == 0 and x is hi and w is w_hi),
                                                     stop=(k == KC - 1 and x is lo))
                        if k == KC - 1:
                            last.then_inc(proj_done, 1)

                    def turn_cat(c, j, cat, done, kept, turned, bank, free):
                        n = ig * NCH + c
                        pe.wait_ge(done, n + 1 + 1)
                        if not free:
                            pe.wait_ge(kept, n * CH + j + 1)
                        for h in range(HG):
                            last = t_.transpose(bank[:, h * P:(h + 1) * P].bitcast(F32R), cat[:, j, h, :], ident_r[:])
                        last.then_inc(turned, 1)

                    def turn_k(c, j, bank=4):
                        turn_cat(c, j, k_cat, k_cat_done, k_kept, k_turned, flat[bank], bank != 4)

                    def turn_q(c, j, bank=5):
                        turn_cat(c, j, q_cat, q_cat_done, q_kept, q_turned, flat[bank], bank != 5)

                    def turn_phi(c, s):
                        n = ig * NCH + c
                        pe.wait_ge(phi_ready, n + 1 + 1)
                        pe.wait_ge(bias_ready, ig + 1 + 1)
                        pe.wait_ge(o1_ready, n + 1)
                        for t in range(CH):
                            for a in range(2):
                                last = t_.transpose(flat[6][:, (2 * t + a) * P:(2 * t + a + 1) * P],
                                                    phi[s][:, t, a * P:(a + 1) * P], ident[:])
                        last.then_inc(phi_turned, 1)

                    def key_values(c, s):
                        n = ig * NCH + c
                        pe.wait_ge(v1_ready, n + 1 + 1)
                        pe.wait_ge(rden_done, ig * (NQ * DEN_PARTS) + 1)
                        pe.wait_ge(am_ready, n * CH + 1)
                        for t in range(CH):
                            last = t_.matmul(flat[7][:, t * HG * VW:(t + 1) * HG * VW], phi[s][:, t, P:2 * P],
                                             v1[s][:, t].rearrange("p h e -> p (h e)"), start=True, stop=True)
                        last.then_inc(kv_done, 1)

                    def key_query(c, t):
                        n = ig * NCH + c
                        pe.wait_ge(qkT_kept, n + 1 + 1)
                        if t:
                            pe.wait_ge(state_ready, n + 1 + 1)
                        pe.wait_ge(qbd_ready, n * CH + (t + 1) + 1)
                        t_.matmul(flat[6 + t], qkT[:, t, 1, :], qbd[:, t].rearrange("p h n -> p (h n)"),
                                  start=True, stop=True).then_inc(at_done, 1)

                    def outputs(c, s, t):
                        n = ig * NCH + c
                        pe.wait_ge(state_ready, n + 1 + 1)
                        pe.wait_ge(am_ready, n * CH + (t + 1) + 1)
                        o = t * HG * VW
                        t_.matmul(flat[6][:, o:o + HG * VW], qkT[:, t, 0, :],
                                  state[:, 2 * s + t].rearrange("p h e -> p (h e)"), start=True, stop=True)
                        for h in range(HG):
                            last = t_.matmul(flat[6][:, o + h * VW:o + (h + 1) * VW], am[:, t, h, :], v1[s][:, t, h, :],
                                             start=False, stop=True, skip_group_check=True)
                        last.then_inc(num_done, 1)

                    def step(c, s):
                        project(c, s, 0)
                        turn_phi(c - 1, 1 - s)
                        key_values(c - 1, 1 - s)
                        turn_k(c - 1, 0)
                        turn_q(c - 1, 0)
                        project(c, s, 1, range(KC // 2))
                        key_query(c - 1, 0)
                        project(c, s, 1, range(KC // 2, KC))
                        key_query(c - 1, 1)
                        outputs(c - 1, 1 - s, 0)
                        turn_k(c - 1, 1)
                        turn_q(c - 1, 1)
                        outputs(c - 1, 1 - s, 1)

                    project(0, 0, 0, first=True)
                    pe.wait_ge(xbar_ready, b + 1 + 1)
                    pe.wait_ge(y_done, b * TT + 1)
                    for k in range(KC):
                        last = t_.matmul(flat[6][:, 0:P], xbar[:, k, :], w_hi[:, k, P:2 * P],
                                         start=(k == 0), stop=(k == KC - 1))
                    last.then_inc(kmean_done, 1)
                    project(0, 0, 1)
                    with pe.Fori(0, NCH // 2 - 1) as i:
                        step(i * 2 + 1, 1)
                        step(i * 2 + 2, 0)
                    step(NCH - 1, 1)
                    c = NCH - 1
                    turn_phi(c, 1)
                    key_values(c, 1)
                    pe.wait_ge(bound_ready, ig + 1 + 1)
                    pe.wait_ge(projA_kept, (ig + 1) * TT + 1)
                    pe.wait_ge(projB_kept, (ig + 1) * TT + 1)
                    t_.transpose(flat[2][0:1, 0:P], bound[:], ident[:]).then_inc(bound_turned, 1)
                    turn_k(c, 0)
                    turn_k(c, 1, bank=0)
                    pe.wait_ge(flag_ready, ig + 1 + 1)
                    settle(pe)
                    wide = pe.value_load(flag[0:1, 0:1], min_val=0, max_val=1)
                    turn_q(c, 0)
                    turn_q(c, 1, bank=1)
                    for t in range(CH):
                        key_query(c, t)
                    outputs(c, 1, 0)
                    pe.wait_ge(q_kept, (ig + 1) * TT + 1)
                    pe.wait_ge(k_kept, (ig + 1) * TT + 1)
                    settle(pe)

                    with pe.If(wide):
                        with pe.Fori(0, HG) as h:
                            with pe.Fori(0, TT) as r:
                                n = ig * (HG * TT) + h * TT + r
                                pe.wait_ge(scan_staged, n + 1 + 1)
                                pe.wait_ge(scan_row, n + 1)
                                for k in range(4):
                                    last = t_.matmul(flat[k], scan_q[:], kaug[:].rearrange("p h n -> p (h n)")[
                                        :, bass.ds(h * S + k * 512, 512)], start=True, stop=True)
                                last.then_inc(scan_scored, 1)
                                pe.wait_ge(scan_max, n + 1 + 1)
                                t_.transpose(flat[4][:, 0:P], scan_m[:], ident[:]).then_inc(scan_turned, 1)
                    with pe.Else():
                        pe.sem_inc(scan_scored, HG * TT)
                        pe.sem_inc(scan_turned, HG * TT)

                    pe.wait_ge(scan_row, (ig + 1) * (HG * TT) + 1)
                    settle(pe)
                    def score(q, u):
                        kt, p = u // 2, u % 2
                        if u >= 3 or q:
                            pe.wait_ge(exped, (ig * NQ + q) * UNITS + u - 2 + 1)
                        for a in range(2):
                            h = 2 * p + a
                            last = t_.matmul(places[place(q, u)][:, a, :], kaug[:, h, kt * P:(kt + 1) * P],
                                             qaug[:, h, bass.ds(q * QN, QN)], start=True, stop=True)
                        last.then_inc(scored, 1)

                    def weigh(q, kt):
                        pe.wait_ge(exped, (ig * NQ + q) * UNITS + (2 * kt + 2) + 1)
                        for h in range(HG):
                            last = t_.matmul(out_bank[h * HD:(h + 1) * HD, :], v[:, kt, h * HD:(h + 1) * HD],
                                             prob[kt % 2][h // 2][:, h % 2, :], start=(kt == 0), stop=(kt == TT - 1))
                        last.then_inc(weighted, 1)

                    def total(q):
                        n = ig * NQ + q
                        pe.wait_ge(summed, (n + 1) * DVE_SUMS + 1)
                        pe.wait_ge(pool_summed, (n + 1) * POOL_SUMS + 1)
                        pe.wait_ge(rden_done, n * DEN_PARTS + 1)
                        for i in range(2):
                            for h in range(i * 2, HG):
                                last = t_.matmul(den_bank[h * HD:(h + 1) * HD, :], ones32[:],
                                                 (acc_pool[q % 2] if i else acc[q % 2][h // 2])[:, h % 2, :],
                                                 start=(i == 0), stop=(i == 1 or h < 2))
                        last.then_inc(den_done, 1)

                    def attend(q):
                        for kt in range(TT):
                            for u in (2 * kt + 3, 2 * kt + 4):
                                if u < UNITS:
                                    score(q, u)
                                elif q < NQ - 1:
                                    score(q + 1, u - UNITS)
                            if kt == 0 and q == 0:
                                pe.wait_ge(o1_ready, (ig + 1) * NCH + 1)
                            elif kt == 0:
                                pe.wait_ge(out_kept, ig * NQ + q + 1)
                            weigh(q, kt)
                            if kt == TOTAL_AT and q:
                                total(q - 1)

                    for u in range(3):
                        score(0, u)
                    outputs(NCH - 1, 1, 1)
                    for q in range(NQ):
                        attend(q)
                    total(NQ - 1)

                with pe.Fori(0, NF // 2) as i:
                    for s in range(2):
                        f = i * 2 + s
                        n = b * NF + f

                        def turn_o(j):
                            if j == 0:
                                pe.wait_ge(o1_loaded, n * 16 + 16 + 1)
                            pe.wait_ge(oT_done, n * FT + max(j - 1, 0) + 1)
                            for k in range(KC):
                                last = t_.transpose(flat[j % 2][:, k * P:(k + 1) * P], o1_in[:, j, k * P:(k + 1) * P], ident[:])
                            last.then_inc(o1_turned, 1)

                        def out_o(j):
                            r = slice(j * P, (j + 1) * P)
                            pe.wait_ge(oT_done, n * FT + (j + 1) + 1)
                            pe.wait_ge(y_done, n * FT + max(j - 1, 0) + 1)
                            parts(flat[4 + j % 2], lambda k: oT_hi[:, k, r], lambda k: oT_lo[:, k, r],
                                  lambda k: wop_hi[:, 0, k, :], lambda k: wop_lo[:, 0, k, :])

                        def out_h(j):
                            r = slice(j * P, (j + 1) * P)
                            parts(flat[6 + j % 2], lambda k: hT_hi[s][:, k, r], lambda k: hT_lo[s][:, k, r],
                                  lambda k: wop_hi[:, 1, k, :], lambda k: wop_lo[:, 1, k, :]).then_inc(yz_done, 1)

                        turn_o(0)
                        turn_o(1)
                        pe.wait_ge(hT_done, n + 1 + 1)
                        pe.wait_ge(gain_ready, n + 1)
                        parts(flat[2][0:NGATE, :], lambda k: wg_hi[:, k, :], lambda k: wg_lo[:, k, :],
                              lambda k: hT_hi[s][:, k, :], lambda k: hT_lo[s][:, k, :]).then_inc(gateT_done, 1)
                        pe.wait_ge(wop_done, (b + 1) * 2 + 1)
                        pe.wait_ge(out_kept, (b + 1) * (NG * NQ) + 1)
                        pe.wait_ge(rden_done, (b + 1) * (NG * NQ * DEN_PARTS) + 1)
                        out_o(0)
                        out_h(0)
                        pe.wait_ge(gateT_kept, n + 1 + 1)
                        settle(pe)
                        for j in range(FT):
                            last = t_.transpose(flat[2][:, j * NGATE:(j + 1) * NGATE], lgT[:, j * P:(j + 1) * P],
                                                ident[0:NGATE, 0:NGATE])
                        last.then_inc(gate_done, 1)
                        turn_x(b + 1, f, s, 0)
                        turn_o(2)
                        out_o(1)
                        out_h(1)
                        turn_x(b + 1, f, s, 1)
                        turn_o(3)
                        out_o(2)
                        turn_x(b + 1, f, s, 2)
                        out_h(2)
                        turn_x(b + 1, f, s, 3)
                        out_o(3)
                        out_h(3)

        @block.vector
        def _(dve):
            v_ = nc.vector

            def linker(sem_, base):
                count = [0]

                def link(ins):
                    count[0] += 1
                    ins.then_inc(sem_, 1)
                    dve.wait_ge(sem_, base + count[0] + 1)
                    return count[0]
                return link

            dve.wait_ge(const_in, 16 * NCONST)
            link = linker(dve_const, 0)
            link(v_.tensor_scalar(tnt[:], temp[:], -1.0, None, ALU.mult))
            link(v_.tensor_tensor(tnt[:], tnt[:], temp[:], ALU.min))
            dve.wait_ge(act_const, 1)
            link(v_.tensor_scalar(tnt[:], tnt[:], 1.0, None, ALU.add))
            dve.wait_ge(act_const, 2)
            link(v_.scalar_tensor_tensor(tsc[:], temp[:], 0.0, tnt[:], ALU.max, ALU.add))
            link(v_.tensor_scalar(tsc[:], tsc[:], HD ** -0.5, None, ALU.mult))
            link(v_.tensor_tensor(et[:], et[:], tsc[:].unsqueeze(2).broadcast_to([P, H, HD]), ALU.mult))
            link(v_.tensor_tensor(xT[:, 0, 0:D], et[:].rearrange("p h e -> p (h e)"), et[:].rearrange("p h e -> p (h e)"),
                                  ALU.mult))
            link(v_.tensor_reduce(tb[:], xT[:, 0, 0:D].rearrange("p (h e) -> p h e", h=H), AX.X, ALU.add))
            link(v_.tensor_tensor(tnt[:], tsc[:], tsc[:], ALU.mult))
            link(v_.tensor_tensor(tb[:], tb[:], tnt[:], ALU.add))
            link(v_.tensor_scalar(tb[:], tb[:], 2.0, None, ALU.mult))
            link(v_.memset(wg_raw[:, :, NR + NS:NGATE], 0.0))
            link(v_.tensor_copy(wg_hi[:], wg_raw[:]))
            link(v_.tensor_tensor(wg_lo[:], wg_raw[:], f32(wg_hi[:]), ALU.subtract))
            link(v_.memset(ones32[:], 1.0))
            dve.wait_ge(pool_const, POOL_CONST)
            v_.tensor_copy(ident_r[:], ident[:])
            link(v_.memset(neg_shift[:], -SHIFT))

            def normalise(lb, t, s, half):
                n = lb * NF + t
                xt = x_in[s]
                link = linker(ln_dve, n * L_STEPS)
                dve.wait_ge(x_loaded[s], (lb * (NF // 2) + half) * 16 + 16 + 1)
                settle(dve)
                for j in range(LC):
                    ins = v_.bn_stats(stats[:, j, :], xt[:, j, :])
                link(ins)
                settle(dve)
                for j in range(LC):
                    ins = v_.bn_aggr(mv[:, j, :], stats[:, j, :])
                assert link(ins) == L_STEPS
                v_.tensor_scalar(rstd[:], mv[:, :, 1], LN_EPS, None, ALU.add).then_inc(ln_stats, 1)
                dve.wait_ge(ln_rstd, n + 1 + 1)
                for j in range(LC):
                    ins = v_.tensor_scalar(xt[:, j, :], xt[:, j, :], mv[:, j, 0:1], rstd[:, j:j + 1],
                                           ALU.subtract, ALU.mult)
                ins.then_inc(ln_done, 1)

            def sum_x(lb, t):
                dve.wait_ge(xT_kept, (lb * NF + t) * LC + LC + 1)
                settle(dve)
                v_.tensor_reduce(xpart[:, :, bass.ds(t, 1)].rearrange("p k o -> p (k o)"),
                                 xT[:, :, bass.ds(t * (LC * P), LC * P)], AX.X, ALU.add).then_inc(xpart_done, 1)

            with dve.Fori(0, NF // 2) as i:
                for s in range(2):
                    normalise(0, i * 2 + s, s, i)
                for s in range(2):
                    sum_x(0, i * 2 + s)

            with dve.Fori(0, B) as b:
                dve.wait_ge(xs0_hi_done, b + 1 + 1)
                v_.tensor_tensor(xs0_lo[:], xT[:, :, 0:P], f32(xs0_hi[:]), ALU.subtract).then_inc(xs0_done, 1)
                dve.wait_ge(xpart_done, (b + 1) * NF + 1)
                settle(dve)
                link = linker(g_set, b * (2 + SET_STEPS * NG))
                link(v_.tensor_reduce(xmean[:], xpart[:], AX.X, ALU.add))
                link(v_.tensor_scalar(xmean[:], xmean[:], 1.0 / S, None, ALU.mult))
                v_.tensor_copy(xbar[:], xmean[:].unsqueeze(2).broadcast_to([P, KC, P])).then_inc(xbar_ready, 1)

                with dve.Fori(0, NG) as g:
                    ig = b * NG + g

                    def part_x(c, s, tile0=0):
                        r = slice(tile0 * P, CT)
                        dve.wait_ge(xs_hi_done, ig * NCH + c + 1 + 1)
                        v_.tensor_tensor(xs_lo[s][:, :, r], xT[:, :, bass.ds(c * CT + tile0 * P, CT - tile0 * P)],
                                         f32(xs_hi[s][:, :, r]), ALU.subtract).then_inc(xs_done, 1)

                    part_x(0, 0, tile0=1)
                    link = linker(g_set, b * (2 + SET_STEPS * NG) + g * SET_STEPS + 2)
                    dve.wait_ge(w_split, ig + 1 + 1)
                    dve.wait_ge(y_stored[1], b * (16 * NF // 2) + 1)
                    link(v_.tensor_copy(et_g[:], et[:, bass.ds(g * HG, HG), :].rearrange("p h e -> p (h e)")))
                    link(v_.tensor_copy(tsc_g[:], tsc[:, bass.ds(g * HG, HG)]))
                    link(v_.tensor_copy(tb_g[:], tb[:, bass.ds(g * HG, HG)]))
                    v_.memset(kmax[:], 0.0)
                    v_.memset(f32(q_cat[:, :, :, 3 * HD:P]), 0.0)
                    v_.memset(f32(k_cat[:, :, :, 3 * HD + 1:P]), 0.0)
                    link(v_.memset(f32(k_cat[:, :, :, 3 * HD:3 * HD + 1]), 1.0))
                    for s in range(2):
                        v_.memset(v1[s][:, :, :, HD:VW], 1.0)
                    v_.memset(state[:, 0], 0.0)
                    dve.wait_ge(kmean_done, ig + 1 + 1)
                    v_.tensor_tensor(kmean_b[:], flat[6][:, 0:P], bias_g[:, P:2 * P], ALU.add).then_inc(bias_ready, 1)
                    dve.wait_ge(bias_ready, ig + 1 + 1)
                    assert link(v_.tensor_tensor(bias_g[:, P:2 * P], bias_g[:, P:2 * P], kmean_b[:], ALU.subtract)
                                ) == SET_STEPS

                    def keep_qk(c, j):
                        n = ig * NCH + c
                        if j == 0:
                            dve.wait_ge(cat_hi, n * 2 + 1)
                            dve.wait_ge(k_cat_done, n + 1)
                        dve.wait_ge(proj_done, n * CH + (j + 1) + 1)
                        ins = v_.tensor_tensor(qk[:, :, j, :], flat[2 * j][:, 0:2 * P].rearrange("p (a n) -> p a n", a=2),
                                               bias_g[:, 0:2 * P].rearrange("p (a n) -> p a n", a=2), ALU.add)
                        if j == CH - 1:
                            ins.then_inc(qk_kept, 1)
                        v_.tensor_tensor(v[:, bass.ds(c * CH + j, 1), :].rearrange("p o n -> p (o n)"),
                                         flat[2 * j][:, 2 * P:3 * P], bias_g[:, 2 * P:3 * P], ALU.add).then_inc(projA_kept, 1)

                    def squares(c):
                        n = ig * NCH + c
                        link = linker(g_dve, n * G_STEPS)
                        dve.wait_ge(qk_kept, n + 1 + 1)
                        link(v_.tensor_tensor(sq[:], qk[:, 0], qk[:, 0], ALU.mult))
                        v_.tensor_reduce(ss[:], sq[:].rearrange("p c (h e) -> p c h e", h=HG), AX.X, ALU.add
                                         ).then_inc(ss_ready, 1)
                        link(v_.tensor_tensor(ksq[:], qk[:, 1], qk[:, 1], ALU.mult))
                        link(v_.tensor_reduce(kss[:], ksq[:].rearrange("p c (h e) -> p c h e", h=HG), AX.X, ALU.add))
                        link(v_.tensor_tensor(kmax[:], kmax[:], kss[:], ALU.max))

                    def scale_q_stack_low_k(c):
                        n = ig * NCH + c
                        link = linker(g_dve, n * G_STEPS + 4)
                        dve.wait_ge(rn_ready, n + 1 + 1)
                        link(v_.tensor_tensor(rnt[:], rn[:], tsc_g[:].unsqueeze(1).broadcast_to([P, CH, HG]), ALU.mult))
                        steps = link(v_.tensor_tensor(qh[:].rearrange("p c (h e) -> p c h e", h=HG),
                                                      qk[:, 0].rearrange("p c (h e) -> p c h e", h=HG),
                                                      rnt[:].unsqueeze(3).broadcast_to([P, CH, HG, HD]), ALU.mult))
                        assert 4 + steps == G_STEPS
                        v_.tensor_tensor(qh[:], qh[:], et_g[:].unsqueeze(1).broadcast_to([P, CH, P]),
                                         ALU.add).then_inc(qh_ready, 1)
                        dve.wait_ge(cat_hi, n * 2 + 1 + 1)
                        v_.tensor_tensor(k_cat[:, :, :, 2 * HD:3 * HD], qk[:, 1].rearrange("p c (h e) -> p c h e", h=HG),
                                         f32(k_cat[:, :, :, 0:HD]), ALU.subtract).then_inc(k_cat_done, 1)

                    def stack_low_q(c):
                        n = ig * NCH + c
                        dve.wait_ge(cat_hi, n * 2 + 2 + 1)
                        v_.tensor_tensor(q_cat[:, :, :, HD:2 * HD], qh[:].rearrange("p c (h e) -> p c h e", h=HG),
                                         f32(q_cat[:, :, :, 0:HD]), ALU.subtract).then_inc(q_cat_done, 1)

                    def keep_k(c, j):
                        dve.wait_ge(k_turned, (ig * NCH + c) * CH + (j + 1) + 1)
                        settle(dve)
                        v_.tensor_copy(kaug[:, :, bass.ds(c * CT + j * P, P)], flat[4].rearrange("p (h n) -> p h n", h=HG)
                                       ).then_inc(k_kept, 1)

                    def negatives(c, s):
                        dve.wait_ge(projB_kept, (ig * NCH + c) * CH + CH + 1)
                        v_.tensor_scalar(ex[:], lin[s][:, :, 0:2 * P], 0.0, None, ALU.min).then_inc(neg_part, 1)

                    def features(c, s):
                        dve.wait_ge(exp_part, ig * NCH + c + 1 + 1)
                        v_.scalar_tensor_tensor(phi[s][:], lin[s][:, :, 0:2 * P], 0.0, ex[:], ALU.max, ALU.add
                                                ).then_inc(phi_ready, 1)

                    def spread_q(c):
                        dve.wait_ge(qkT_kept, ig * NCH + c + 1 + 1)
                        for t in range(CH):
                            v_.tensor_tensor(qbd[:, t], qkT[:, t, 0, :].unsqueeze(1).broadcast_to([P, HG, P]),
                                             headmask[:].unsqueeze(2).broadcast_to([P, HG, P]), ALU.mult).then_inc(qbd_ready, 1)

                    def states(c, s):
                        n = ig * NCH + c
                        link = linker(states_dve, n * C_STEPS)
                        dve.wait_ge(state_ready, n + 1)
                        dve.wait_ge(kv_done, n + 1 + 1)
                        link(v_.tensor_tensor(kvm[:], flat[7][:, 0:CH * HG * VW].rearrange("p (t h e) -> p t h e", t=CH, h=HG),
                                              headmask[:].unsqueeze(1).unsqueeze(3).broadcast_to([P, CH, HG, VW]), ALU.mult))
                        assert link(v_.tensor_tensor(state[:, 2 * s + 1], state[:, 2 * s], kvm[:, 0], ALU.add)) == C_STEPS
                        v_.tensor_tensor(state[:, 2 * (1 - s)], state[:, 2 * s + 1], kvm[:, 1], ALU.add).then_inc(state_ready, 1)

                    def mask(c, t):
                        n = ig * NCH + c
                        for s in range(2):
                            dve.wait_ge(hT_stored[s], ig * (16 * NQ // 2) + 1)
                        dve.wait_ge(at_done, n * CH + (t + 1) + 1)
                        v_.tensor_tensor(am[:, t], flat[6 + t].rearrange("p (h n) -> p h n", h=HG),
                                         causal[:].unsqueeze(1).broadcast_to([P, HG, P]), ALU.mult).then_inc(am_ready, 1)

                    def outputs(c, s, store):
                        n = ig * NCH + c
                        link = linker(outputs_dve, n * C_STEPS)
                        dve.wait_ge(o1_ready, n + 1)
                        if s == 0:
                            dve.wait_ge(o1_stored, (ig * NLC + store) * 16 + 1)
                        dve.wait_ge(num_done, n * CH + CH + 1)
                        num = flat[6][:, 0:CH * HG * VW].rearrange("p (t h e) -> p t h e", t=CH, h=HG)
                        link(v_.tensor_scalar(dn[:], num[:, :, :, HD], ATT_EPS, None, ALU.add))
                        assert link(v_.reciprocal(rdn[:], dn[:])) == C_STEPS
                        v_.tensor_tensor(o1[:, s * CH:(s + 1) * CH].rearrange("p t (h e) -> p t h e", h=HG),
                                         num[:, :, :, 0:HD], rdn[:].unsqueeze(3).broadcast_to([P, CH, HG, HD]),
                                         ALU.mult).then_inc(o1_ready, 1)

                    def step(c, s, store, last=True, ahead=True):
                        if last:
                            scale_q_stack_low_k(c - 1)
                            stack_low_q(c - 1)
                        keep_qk(c, 0)
                        if last:
                            spread_q(c - 1)
                            states(c - 1, 1 - s)
                            keep_k(c - 1, 0)
                        if ahead:
                            part_x(c + 1, 1 - s)
                        if last:
                            mask(c - 1, 0)
                        keep_qk(c, 1)
                        if last:
                            mask(c - 1, 1)
                        negatives(c, s)
                        squares(c)
                        features(c, s)
                        if last:
                            keep_k(c - 1, 1)
                            outputs(c - 1, 1 - s, store)

                    step(0, 0, 0, last=False)
                    with dve.Fori(0, NCH // 2 - 1) as i:
                        step(i * 2 + 1, 1, i)
                        step(i * 2 + 2, 0, i)
                    step(NCH - 1, 1, NCH // 2 - 1, ahead=False)
                    link = linker(bound_dve, ig * BOUND_STEPS)
                    link(v_.tensor_tensor(kmax2[:], kmax[:, 0, :], kmax[:, 1, :], ALU.max))
                    link(v_.tensor_tensor(kmax2[:], kmax2[:], tb_g[:], ALU.mult))
                    v_.tensor_reduce(bound[:], kmax2[:], AX.X, ALU.max).then_inc(bound_ready, 1)
                    c = NCH - 1
                    scale_q_stack_low_k(c)
                    dve.wait_ge(bound_turned, ig + 1 + 1)
                    assert link(v_.tensor_reduce(bound1[:], flat[2][0:1, 0:P], AX.X, ALU.max)) == BOUND_STEPS
                    v_.tensor_scalar(flag[:], bound1[:], BOUND2, None, ALU.is_gt).then_inc(flag_ready, 1)
                    stack_low_q(c)
                    spread_q(c)
                    states(c, 1)
                    for t in range(CH):
                        mask(c, t)

                    dve.wait_ge(flag_ready, ig + 1 + 1)
                    settle(dve)
                    wide = dve.value_load(flag[0:1, 0:1], min_val=0, max_val=1)
                    with dve.If(wide):
                        v_.memset(scan_m[:], 0.0)
                        with dve.Fori(0, HG * TT) as r:
                            n = ig * (HG * TT) + r
                            dve.wait_ge(scan_scored, n + 1 + 1)
                            v_.tensor_reduce(rowmax[:], low[:], AX.XY, ALU.max).then_inc(scan_reduced, 1)
                            dve.wait_ge(scan_reduced, n + 1 + 1)
                            v_.tensor_scalar(scan_m[:, 3 * HD:3 * HD + 1], rowmax[:], -1.0, SHIFT, ALU.mult, ALU.add
                                             ).then_inc(scan_max, 1)
                            dve.wait_ge(scan_turned, n + 1 + 1)
                            settle(dve)
                            v_.tensor_copy(qaug[3 * HD:3 * HD + 1, :, :].rearrange("p h n -> p (h n)")[:, bass.ds(r * P, P)],
                                           flat[4][3 * HD:3 * HD + 1, 0:P]).then_inc(scan_row, 1)
                    with dve.Else():
                        dve.sem_inc(scan_reduced, HG * TT)
                        dve.sem_inc(scan_max, HG * TT)
                        dve.sem_inc(scan_row, HG * TT)

                    def sums(kt, q):
                        n, s = ig * NQ + q, q % 2
                        for p in range(2):
                            if (kt, p) in dve_order:
                                dve.wait_ge(exped, n * UNITS + (2 * kt + p + 1) + 1)
                                if kt > p:
                                    dve.wait_ge(summed, n * DVE_SUMS + DVE_AT[kt - 1 - p, p] + 1)
                                if q == 0 and kt < p:
                                    dve.wait_ge(o1_stored, (ig + 1) * (16 * NLC) + 1)
                                if kt <= p:
                                    settle(dve)
                                    v_.tensor_copy((acc_pool[s] if kt < p else acc[s][p])[:], prob[kt][p][:]).then_inc(summed, 1)
                                else:
                                    v_.tensor_tensor(acc[s][p][:], acc[s][p][:], prob[kt % 2][p][:], ALU.add).then_inc(summed, 1)

                    def keep_out(q):
                        s = q % 2
                        dve.wait_ge(hT_stored[s], (ig * (NQ // 2) + q // 2) * 16 + 1)
                        dve.wait_ge(weighted, (ig * NQ + q) * TT + TT + 1)
                        settle(dve)
                        v_.tensor_copy(hT_out[s][:], out_bank).then_inc(out_kept, 1)

                    def invert(q, part):
                        n = ig * NQ + q
                        cols = slice(part * QN // DEN_PARTS, (part + 1) * QN // DEN_PARTS)
                        dve.wait_ge(den_done, n + 1 + 1)
                        dve.wait_ge(h_done, n + 1)
                        v_.reciprocal(rden[:, cols], den_bank[:, cols]).then_inc(rden_done, 1)

                    def attend(q):
                        n = ig * NQ + q
                        if q:
                            dve.wait_ge(den_done, n)
                        for kt in range(TT):
                            sums(kt, q)
                            if kt and kt % 2 == 0 and kt // 2 <= DEN_PARTS and q:
                                invert(q - 1, kt // 2 - 1)
                        keep_out(q)

                    outputs(NCH - 1, 1, NLC - 1)
                    for q in range(NQ):
                        attend(q)
                    for part in range(DEN_PARTS):
                        invert(NQ - 1, part)

                for a in range(2):
                    dve.wait_ge(wop_hi_done, b * 2 + a + 1 + 1)
                    v_.tensor_tensor(wop_lo[:, a], wop_raw[:, a], f32(wop_hi[:, a]), ALU.subtract).then_inc(wop_done, 1)
                with dve.Fori(0, NF // 2) as i:
                    for s in range(2):
                        f = i * 2 + s
                        n = b * NF + f
                        link = linker(f_dve, n * F_STEPS)

                        def split_o(j):
                            dve.wait_ge(oT_hi_done, n * FT + (j + 1) + 1)
                            v_.tensor_tensor(oT_lo[:, :, j * P:(j + 1) * P], flat[j % 2].rearrange("p (k n) -> p k n", k=KC),
                                             f32(oT_hi[:, :, j * P:(j + 1) * P]), ALU.subtract).then_inc(oT_done, 1)

                        def add_y(j):
                            dve.wait_ge(yz_done, n * FT + (j + 1) + FT + 1)
                            steps = link(v_.tensor_tensor(y[s][:, j, :], flat[4 + j % 2], y[s][:, j, :], ALU.add))
                            v_.scalar_tensor_tensor(y[s][:, j, :], flat[6 + j % 2], gain[:, j:j + 1], y[s][:, j, :],
                                                    ALU.mult, ALU.add).then_inc(y_done, 1)
                            return steps

                        split_o(0)
                        split_o(1)
                        normalise(b + 1, f, s, i)
                        split_o(2)
                        dve.wait_ge(gate_done, n + 1 + 1)
                        link(v_.tensor_tensor(lg[:], flat[2][:, 0:FT * NGATE].rearrange("p (t n) -> p t n", t=FT)[:, :, 0:NR + NS],
                                              bg[:].unsqueeze(1).broadcast_to([P, FT, NR + NS]), ALU.add))
                        settle(dve)
                        for j in range(FT):
                            ins = v_.max(top8[:, j, :], lg[:, j, 0:NR])
                        link(ins)
                        link(v_.tensor_reduce(smax[:], lg[:, :, NR:NR + NS], AX.X, ALU.max))
                        v_.tensor_tensor(z[:, :, 0:NR], lg[:, :, 0:NR], top8[:, :, 0:1].broadcast_to([P, FT, NR]), ALU.subtract)
                        v_.tensor_tensor(z[:, :, NR:NR + NS], lg[:, :, NR:NR + NS], smax[:].broadcast_to([P, FT, NS]), ALU.subtract)
                        v_.tensor_tensor(z[:, :, NR + NS:NZ], top8[:, :, 0:TOP], top8[:, :, 0:1].broadcast_to([P, FT, TOP]),
                                         ALU.subtract).then_inc(gate_z, 1)
                        dve.wait_ge(gate_exp, n + 1 + 1)
                        v_.tensor_reduce(zsum[:, :, 0], z[:, :, 0:NR], AX.X, ALU.add)
                        v_.tensor_reduce(zsum[:, :, 1], z[:, :, NR:NR + NS], AX.X, ALU.add)
                        link(v_.tensor_reduce(zsum[:, :, 2], z[:, :, NR + NS:NZ], AX.X, ALU.add))
                        link(v_.reciprocal(zrec[:], zsum[:, :, 0:2]))
                        link(v_.tensor_tensor(share[:, :, 0:NS], z[:, :, NR:NR + NS], zrec[:, :, 1:2].broadcast_to([P, FT, NS]),
                                              ALU.mult))
                        v_.tensor_tensor(share[:, :, 2], share[:, :, 0], share[:, :, 1], ALU.add)
                        link(v_.tensor_tensor(share[:, :, 3], zsum[:, :, 2], zrec[:, :, 0], ALU.mult))
                        link(v_.tensor_tensor(share[:, :, 2], share[:, :, 2], share[:, :, 0], ALU.mult))
                        link(v_.scalar_tensor_tensor(share[:, :, 3], share[:, :, 3], 2.0 * TOP, share[:, :, 1], ALU.mult, ALU.mult))
                        v_.scalar_tensor_tensor(gain[:], share[:, :, 2], 2.0, share[:, :, 3], ALU.mult, ALU.add
                                                ).then_inc(gain_ready, 1)
                        dve.wait_ge(gain_ready, n + 1 + 1)
                        dve.wait_ge(y_biased, n + 1 + 1)
                        add_y(0)
                        split_o(3)
                        for j in range(1, FT - 1):
                            add_y(j)
                        sum_x(b + 1, f)
                        assert add_y(FT - 1) == F_STEPS


def kernel(**inputs):
    import numpy as np
    import concourse.bacc as bacc
    from concourse import mybir as mb
    from concourse.bass_utils import run_bass_kernel_spmd

    a = {k: np.asarray(v) for k, v in inputs.items()}
    six = [a["L0_ffn_Wq"].T, a["L0_ffn_Wk"].T, a["L0_ffn_Wv"].T, a["L0_attn_wq"], a["L0_attn_wk"], a["L0_attn_wv"]]

    def rows(w):
        return w.reshape(KC, P, -1).transpose(1, 0, 2)

    arrays = {
        "x": a["L0_attn_x"],
        "w6": np.stack([rows(np.concatenate([w[:, g * P:(g + 1) * P] for w in six], axis=1)) for g in range(NG)]),
        "wop": np.stack([rows(a["L0_attn_wo"]), rows(a["L0_ffn_Wp"].T)], axis=1),
        "wg": rows(np.concatenate([a["L0_ffn_Wr"], a["L0_ffn_Ws"]], axis=0).T),
        "bqkv": np.stack([np.concatenate([a[n][g * P:(g + 1) * P] for n in ("L0_ffn_bq", "L0_ffn_bk", "L0_ffn_bv")])
                          for g in range(NG)]),
        "bp": a["L0_ffn_bp"],
        "bg": np.concatenate([a["L0_ffn_br"], a["L0_ffn_bs"]]),
        "temp": a["L0_ffn_temperature"].reshape(-1),
        "qe": a["L0_ffn_query_embedding"].reshape(-1),
    }
    arrays = {f"in_{k}": np.ascontiguousarray(v) for k, v in arrays.items()}
    nc = bacc.Bacc("TRN2", target_bir_lowering=False, num_devices=1)
    args = [nc.dram_tensor(k, v.shape, mb.dt.from_np(v.dtype), kind="ExternalInput").ap() for k, v in arrays.items()]
    args.append(nc.dram_tensor("out", (B, S, D), mb.dt.float32, kind="ExternalOutput").ap())
    build(nc, *args)
    r = run_bass_kernel_spmd(nc, [arrays], core_ids=[0])
    return r.results[0]["out"]
```
